# Optimizing a Trainium2 kernel written in Bass

```python
import numpy as np
import jax
import jax.numpy as jnp

def _softmax(x, axis=-1):
    return jax.nn.softmax(x, axis=axis)

def _gelu(x):
    return jax.nn.gelu(x, approximate=True)

def _silu(x):
    return jax.nn.silu(x)

def _sigmoid(x):
    return jax.nn.sigmoid(x)

def _layernorm(x, axis=-1, eps=1e-05):
    m = jnp.mean(x, axis=axis, keepdims=True)
    v = jnp.var(x, axis=axis, keepdims=True)
    return (x - m) / jnp.sqrt(v + eps)

def _scatter_add(tgt, idx, src, axis=0):
    return tgt.at[idx].add(src)

def _segment_sum(src, seg, n):
    return jax.ops.segment_sum(src, seg, n)
kernel_name = 'mk_flamingo_gated_d4_seqx_r8_5169d8'

def setup_inputs(seed: int=0):
    np.random.seed(seed)
    _w = jnp.asarray

    def _rec_inputs():
        import jax
        import jax.numpy as jnp
        _rk = jax.random.key(seed)
        x = -0.0005207 + 1.001 * jax.random.normal(jax.random.fold_in(_rk, 1), (8, 128, 128), jnp.float32)
        _lenS = 128 - jax.random.randint(jax.random.fold_in(_rk, 7), (8,), 0, max(1, 128 // 4) + 1, jnp.int32)
        _lenS2 = 128 - jax.random.randint(jax.random.fold_in(_rk, 8), (8,), 0, max(1, 128 // 4) + 1, jnp.int32)
        _ctx_1024P = jax.random.normal(jax.random.fold_in(_rk, 11), (8, 16, 128), jnp.float32)
        _ctx_1024c = jax.random.dirichlet(jax.random.fold_in(_rk, 511), 0.3 * jnp.ones((16,), jnp.float32), (8, 128))
        _ctx_1024t = jnp.einsum('bsk,bkd->bsd', _ctx_1024c, _ctx_1024P)
        _ctx_1024t = _ctx_1024t * jax.lax.rsqrt(jnp.mean(jnp.square(_ctx_1024t)) + 1e-12) * 0.953939
        ctx_1024 = -0.000514642 + 1.00011 * (_ctx_1024t + 0.3 * jax.random.normal(jax.random.fold_in(_rk, 611), (8, 128, 128), jnp.float32))
        _g = jax.random.normal(jax.random.fold_in(_rk, 9001), (2, 4), jnp.float32)
        _g = jnp.sign(_g) * jnp.maximum(jnp.abs(_g), 1.0) + (_g == 0) * 1.0
        g_xattn = _g[0]
        g_ffn = _g[1]
        return (x, ctx_1024, g_xattn, g_ffn)
    x, ctx_1024, g_xattn, g_ffn = _rec_inputs()

    def _L0_xattn_setup():
        import jax, jax.numpy as jnp
        import numpy as np
        DIM = 128
        HEADS = 8
        HEAD_DIM = DIM // HEADS
        TAU = HEAD_DIM ** 0.5
        BS, SEQ = (1, 256)
        key = jax.random.key(seed)
        kq, kk, kv, kb = jax.random.split(key, 4)
        q = jax.random.normal(kq, (BS, SEQ, DIM), jnp.float32)
        k = jax.random.normal(kk, (BS, SEQ, DIM), jnp.float32)
        v = jax.random.normal(kv, (BS, SEQ, DIM), jnp.float32)
        Wi_w = jnp.zeros((HEADS, 3 * DIM), jnp.float32)
        Wi_b = 0.1 * jax.random.normal(kb, (HEADS,), jnp.float32)
        Wf_w = jnp.zeros((HEADS, 3 * DIM), jnp.float32)
        Wf_b = jnp.linspace(3.0, 6.0, HEADS, dtype=jnp.float32)
        gn_w = jnp.ones((DIM,), jnp.float32)
        gn_b = jnp.zeros((DIM,), jnp.float32)
        return {'q': q, 'k': k, 'v': v, 'Wi_w': Wi_w, 'Wi_b': Wi_b, 'Wf_w': Wf_w, 'Wf_b': Wf_b, 'gn_w': gn_w, 'gn_b': gn_b}
    _L0_xattn_all = _L0_xattn_setup()
    _L0_xattn_in = {k: v for k, v in _L0_xattn_all.items() if k in ('Wi_w', 'Wi_b', 'Wf_w', 'Wf_b', 'gn_w', 'gn_b')}
    del _L0_xattn_all

    def _L0_ffn_setup():
        import math
        import jax, jax.numpy as jnp
        import numpy as np
        B, T, H = (4, 256, 128)
        E, K, F = (8, 2, 256)
        CAP_FACTOR = 1.25

        def _moe_forward(x, Wg, W_in, W_out):
            b, t, h = x.shape
            xf = x.reshape(-1, h)
            S = xf.shape[0]
            C = int(math.ceil(K * S / E * CAP_FACTOR))
            logits = xf @ Wg
            probs = jax.nn.softmax(logits, axis=-1)
            top_vals, top_idx = jax.lax.top_k(probs, K)
            flat_idx = top_idx.T.reshape(-1)
            onehot = jax.nn.one_hot(flat_idx, E, dtype=jnp.int32)
            cum = jnp.cumsum(onehot, axis=0) - 1
            loc = jnp.take_along_axis(cum, flat_idx[:, None], axis=1)[:, 0]
            loc = loc.reshape(K, S).T
            keep = loc < C
            gates = top_vals * keep.astype(top_vals.dtype)
            denom = jnp.maximum(gates.sum(-1, keepdims=True), 1e-09)
            gates = gates / denom
            loc_c = jnp.where(keep, loc, C)
            e_flat = top_idx.reshape(-1)
            l_flat = loc_c.reshape(-1)
            xk = jnp.broadcast_to(xf[:, None, :], (S, K, h)).reshape(-1, h)
            xk = jnp.where(keep.reshape(-1, 1), xk, 0.0)
            buf = jnp.zeros((E, C + 1, h), x.dtype).at[e_flat, l_flat].set(xk)
            inp = buf[:, :C]
            hid = jnp.einsum('ech,ehf->ecf', inp, W_in)
            a, g = jnp.split(hid, 2, axis=-1)
            hid = jax.nn.gelu(a, approximate=False) * g
            out_e = jnp.einsum('ecf,efh->ech', hid, W_out)
            out_pad = jnp.concatenate([out_e, jnp.zeros((E, 1, h), out_e.dtype)], axis=1)
            gathered = out_pad[e_flat, l_flat].reshape(S, K, h)
            y = (gathered * gates[..., None]).sum(axis=1)
            return y.reshape(b, t, h)
        key = jax.random.key(seed)
        k1, k2, k3, k4 = jax.random.split(key, 4)
        x = jax.random.normal(k1, (B, T, H), dtype=jnp.float32)
        Wg = jax.random.normal(k2, (H, E), dtype=jnp.float32) * 0.02
        W_in = jax.random.normal(k3, (E, H, 2 * F), dtype=jnp.float32) * (1.0 / math.sqrt(H))
        W_out = jax.random.normal(k4, (E, F, H), dtype=jnp.float32) * (1.0 / math.sqrt(F))
        return {'x': x, 'Wg': Wg, 'W_in': W_in, 'W_out': W_out}
    _L0_ffn_all = _L0_ffn_setup()
    _L0_ffn_in = {k: v for k, v in _L0_ffn_all.items() if k in ('Wg', 'W_in', 'W_out')}
    del _L0_ffn_all

    def _L1_xattn_setup():
        import jax, jax.numpy as jnp
        import numpy as np
        D1, D2, D3 = (128, 128, 128)
        key = jax.random.key(seed)
        k1, k2, kw, kb = jax.random.split(key, 4)
        x1 = jax.random.normal(k1, (8, 256, D1), dtype=jnp.float32)
        x2 = jax.random.normal(k2, (8, 256, D2), dtype=jnp.float32)
        bound = 1.0 / np.sqrt(D1 + D2)
        W = jax.random.uniform(kw, (D3, D1 + D2), minval=-bound, maxval=bound, dtype=jnp.float32)
        b = jax.random.uniform(kb, (D3,), minval=-bound, maxval=bound, dtype=jnp.float32)
        return {'x1': x1, 'x2': x2, 'W': W, 'b': b}
    _L1_xattn_all = _L1_xattn_setup()
    _L1_xattn_in = {k: v for k, v in _L1_xattn_all.items() if k in ('W', 'b')}
    del _L1_xattn_all

    def _L1_ffn_setup():
        import jax, jax.numpy as jnp
        import numpy as np
        BLOCK = 32
        W_BITS = 4
        ACT_BITS = 16

        def act_qdq(x):
            qmax = 2.0 ** (ACT_BITS - 1) - 1.0
            scale = jnp.maximum(jnp.max(jnp.abs(x)) / qmax, 1e-12)
            return jnp.clip(jnp.round(x / scale), -qmax - 1.0, qmax) * scale

        def fixed_qdq_u16(x):
            scale = 1.0 / 65536.0
            return jnp.clip(jnp.round(x / scale), 0.0, 65535.0) * scale

        def lpbq_dequant(w):
            O, I = w.shape
            qmax = 2.0 ** (W_BITS - 1) - 1.0
            wb = w.reshape(O, I // BLOCK, BLOCK)
            s = jnp.maximum(jnp.max(jnp.abs(wb), axis=-1, keepdims=True) / qmax, 1e-12)
            wq = jnp.clip(jnp.round(wb / s), -qmax - 1.0, qmax) * s
            return wq.reshape(O, I)
        key = jax.random.key(seed)
        k1, k2, k3, k4 = jax.random.split(key, 4)
        B, S, H, I = (2, 512, 128, 384)
        x = jax.random.normal(k1, (B, S, H), jnp.float32)
        w_gate = jax.random.normal(k2, (I, H), jnp.float32) * 0.02
        w_up = jax.random.normal(k3, (I, H), jnp.float32) * 0.02
        w_down = jax.random.normal(k4, (H, I), jnp.float32) * 0.02
        return {'x': x, 'w_gate': w_gate, 'w_up': w_up, 'w_down': w_down}
    _L1_ffn_all = _L1_ffn_setup()
    _L1_ffn_in = {k: v for k, v in _L1_ffn_all.items() if k in ('w_gate', 'w_up', 'w_down')}
    del _L1_ffn_all

    def _L2_xattn_setup():
        import jax, jax.numpy as jnp
        import numpy as np
        B, S, SC, E, H = (2, 256, 256, 128, 16)
        D = E // H
        EPS = 1e-06

        def _layernorm(x, g, b):
            m = jnp.mean(x, axis=-1, keepdims=True)
            v = jnp.mean((x - m) ** 2, axis=-1, keepdims=True)
            return (x - m) / jnp.sqrt(v + EPS) * g + b

        def _mha(xk, xv, xq, Wk, Wv, Wq, Wo, bo, masked):
            K = jnp.einsum('bse,hed->bhsd', xk, Wk)
            V = jnp.einsum('bse,hed->bhsd', xv, Wv)
            Q = jnp.einsum('bqe,hed->bhqd', xq, Wq)
            scores = jnp.einsum('bhqd,bhkd->bhqk', Q, K)
            sk = xk.shape[1]
            if masked:
                causal = jnp.triu(jnp.ones((xq.shape[1], sk), dtype=bool), k=1)
                scores = jnp.where(causal, -jnp.inf, scores)
            att = jax.nn.softmax(scores / jnp.sqrt(jnp.asarray(sk, scores.dtype)), axis=-1)
            out = jnp.einsum('bhqk,bhkd->bhqd', att, V)
            out = out.transpose(0, 2, 1, 3).reshape(out.shape[0], out.shape[2], -1)
            return jax.nn.relu(out @ Wo + bo)
        key = jax.random.key(seed)
        ks = jax.random.split(key, 16)
        w = lambda k, shape: jax.random.normal(k, shape, jnp.float32) * 0.02
        return {'inputs': jax.random.normal(ks[0], (B, S, E), jnp.float32), 'context_seq': jax.random.normal(ks[1], (B, SC, E), jnp.float32), 'Wk1': w(ks[2], (H, E, D)), 'Wv1': w(ks[3], (H, E, D)), 'Wq1': w(ks[4], (H, E, D)), 'Wo1': w(ks[5], (E, E)), 'bo1': jnp.zeros((E,), jnp.float32), 'Wk2': w(ks[6], (H, E, D)), 'Wv2': w(ks[7], (H, E, D)), 'Wq2': w(ks[8], (H, E, D)), 'Wo2': w(ks[9], (E, E)), 'bo2': jnp.zeros((E,), jnp.float32), 'Wf': w(ks[10], (E, E)), 'bf': jnp.zeros((E,), jnp.float32), 'g1': jnp.ones((E,), jnp.float32), 'b1': jnp.zeros((E,), jnp.float32), 'g2': jnp.ones((E,), jnp.float32), 'b2': jnp.zeros((E,), jnp.float32), 'g3': jnp.ones((E,), jnp.float32), 'b3': jnp.zeros((E,), jnp.float32)}
    _L2_xattn_all = _L2_xattn_setup()
    _L2_xattn_in = {k: v for k, v in _L2_xattn_all.items() if k in ('Wk1', 'Wv1', 'Wq1', 'Wo1', 'bo1', 'Wk2', 'Wv2', 'Wq2', 'Wo2', 'bo2', 'Wf', 'bf', 'g1', 'b1', 'g2', 'b2', 'g3', 'b3')}
    del _L2_xattn_all

    def _L2_ffn_setup():
        import jax, jax.numpy as jnp
        import numpy as np
        E, H, I, K = (8, 128, 256, 2)
        B, S = (4, 256)
        key = jax.random.key(seed)
        k1, k2, k3, k4 = jax.random.split(key, 4)
        x = jax.random.normal(k1, (B, S, H), dtype=jnp.float32)
        router_w = jax.random.uniform(k2, (E, H), dtype=jnp.float32, minval=-1.0, maxval=1.0) / np.sqrt(H).astype(np.float32)
        w13 = jax.random.normal(k3, (E, H, 2 * I), dtype=jnp.float32) * 0.02
        w2 = jax.random.normal(k4, (E, I, H), dtype=jnp.float32) * 0.02
        return {'x': x, 'router_w': router_w, 'w13': w13, 'w2': w2}
    _L2_ffn_all = _L2_ffn_setup()
    _L2_ffn_in = {k: v for k, v in _L2_ffn_all.items() if k in ('router_w', 'w13', 'w2')}
    del _L2_ffn_all

    def _L3_xattn_setup():
        import jax, jax.numpy as jnp
        import numpy as np
        EMBED_DIM = 128
        NUM_HEADS = 16
        HEAD_DIM = EMBED_DIM // NUM_HEADS

        def _split_heads(x, B, S):
            return x.reshape(B, S, NUM_HEADS, HEAD_DIM).transpose(0, 2, 1, 3)
        key = jax.random.key(seed)
        ks = jax.random.split(key, 11)
        B, S, D = (2, 256, EMBED_DIM)
        scale = 1.0 / np.sqrt(D)
        inp = {'query': jax.random.normal(ks[0], (B, S, D), jnp.float32), 'key': jax.random.normal(ks[1], (B, S, D), jnp.float32), 'value': jax.random.normal(ks[2], (B, S, D), jnp.float32), 'Wq': jax.random.normal(ks[3], (D, D), jnp.float32) * scale, 'bq': jnp.zeros((D,), jnp.float32), 'Wk': jax.random.normal(ks[4], (D, D), jnp.float32) * scale, 'bk': jnp.zeros((D,), jnp.float32), 'Wv': jax.random.normal(ks[5], (D, D), jnp.float32) * scale, 'bv': jnp.zeros((D,), jnp.float32), 'Wo': jax.random.normal(ks[6], (D, D), jnp.float32) * scale, 'bo': jnp.zeros((D,), jnp.float32)}
        return inp
    _L3_xattn_all = _L3_xattn_setup()
    _L3_xattn_in = {k: v for k, v in _L3_xattn_all.items() if k in ('Wq', 'bq', 'Wk', 'bk', 'Wv', 'bv', 'Wo', 'bo')}
    del _L3_xattn_all

    def _L3_ffn_setup():
        import jax, jax.numpy as jnp
        import numpy as np
        B, S, D, E, H, K = (4, 256, 128, 8, 64, 2)
        key = jax.random.key(seed)
        ks = jax.random.split(key, 11)
        sc = 0.02
        return {'x': jax.random.normal(ks[0], (B, S, D), dtype=jnp.float32), 'gate_W': jax.random.normal(ks[1], (D, E), dtype=jnp.float32) * sc, 'W1': jax.random.normal(ks[2], (E, D, H), dtype=jnp.float32) * sc, 'b1': jnp.zeros((E, H), dtype=jnp.float32), 'W2': jax.random.normal(ks[3], (E, H, D), dtype=jnp.float32) * sc, 'b2': jnp.zeros((E, D), dtype=jnp.float32), 'Ws1': jax.random.normal(ks[4], (D, H), dtype=jnp.float32) * sc, 'bs1': jnp.zeros((H,), dtype=jnp.float32), 'Ws2': jax.random.normal(ks[5], (H, D), dtype=jnp.float32) * sc, 'bs2': jnp.zeros((D,), dtype=jnp.float32), 'route_scale': jnp.ones((), dtype=jnp.float32)}
    _L3_ffn_all = _L3_ffn_setup()
    _L3_ffn_in = {k: v for k, v in _L3_ffn_all.items() if k in ('gate_W', 'W1', 'b1', 'W2', 'b2', 'Ws1', 'bs1', 'Ws2', 'bs2', 'route_scale')}
    del _L3_ffn_all
    return {'x': x, 'ctx_1024': ctx_1024, 'g_xattn': g_xattn, 'g_ffn': g_ffn, 'L0_xattn_Wi_w': _L0_xattn_in['Wi_w'], 'L0_xattn_Wi_b': _L0_xattn_in['Wi_b'], 'L0_xattn_Wf_w': _L0_xattn_in['Wf_w'], 'L0_xattn_Wf_b': _L0_xattn_in['Wf_b'], 'L0_xattn_gn_w': _L0_xattn_in['gn_w'], 'L0_xattn_gn_b': _L0_xattn_in['gn_b'], 'L0_ffn_Wg': _L0_ffn_in['Wg'], 'L0_ffn_W_in': _L0_ffn_in['W_in'], 'L0_ffn_W_out': _L0_ffn_in['W_out'], 'L1_xattn_W': _L1_xattn_in['W'], 'L1_xattn_b': _L1_xattn_in['b'], 'L1_ffn_w_gate': _L1_ffn_in['w_gate'], 'L1_ffn_w_up': _L1_ffn_in['w_up'], 'L1_ffn_w_down': _L1_ffn_in['w_down'], 'L2_xattn_Wk1': _L2_xattn_in['Wk1'], 'L2_xattn_Wv1': _L2_xattn_in['Wv1'], 'L2_xattn_Wq1': _L2_xattn_in['Wq1'], 'L2_xattn_Wo1': _L2_xattn_in['Wo1'], 'L2_xattn_bo1': _L2_xattn_in['bo1'], 'L2_xattn_Wk2': _L2_xattn_in['Wk2'], 'L2_xattn_Wv2': _L2_xattn_in['Wv2'], 'L2_xattn_Wq2': _L2_xattn_in['Wq2'], 'L2_xattn_Wo2': _L2_xattn_in['Wo2'], 'L2_xattn_bo2': _L2_xattn_in['bo2'], 'L2_xattn_Wf': _L2_xattn_in['Wf'], 'L2_xattn_bf': _L2_xattn_in['bf'], 'L2_xattn_g1': _L2_xattn_in['g1'], 'L2_xattn_b1': _L2_xattn_in['b1'], 'L2_xattn_g2': _L2_xattn_in['g2'], 'L2_xattn_b2': _L2_xattn_in['b2'], 'L2_xattn_g3': _L2_xattn_in['g3'], 'L2_xattn_b3': _L2_xattn_in['b3'], 'L2_ffn_router_w': _L2_ffn_in['router_w'], 'L2_ffn_w13': _L2_ffn_in['w13'], 'L2_ffn_w2': _L2_ffn_in['w2'], 'L3_xattn_Wq': _L3_xattn_in['Wq'], 'L3_xattn_bq': _L3_xattn_in['bq'], 'L3_xattn_Wk': _L3_xattn_in['Wk'], 'L3_xattn_bk': _L3_xattn_in['bk'], 'L3_xattn_Wv': _L3_xattn_in['Wv'], 'L3_xattn_bv': _L3_xattn_in['bv'], 'L3_xattn_Wo': _L3_xattn_in['Wo'], 'L3_xattn_bo': _L3_xattn_in['bo'], 'L3_ffn_gate_W': _L3_ffn_in['gate_W'], 'L3_ffn_W1': _L3_ffn_in['W1'], 'L3_ffn_b1': _L3_ffn_in['b1'], 'L3_ffn_W2': _L3_ffn_in['W2'], 'L3_ffn_b2': _L3_ffn_in['b2'], 'L3_ffn_Ws1': _L3_ffn_in['Ws1'], 'L3_ffn_bs1': _L3_ffn_in['bs1'], 'L3_ffn_Ws2': _L3_ffn_in['Ws2'], 'L3_ffn_bs2': _L3_ffn_in['bs2'], 'L3_ffn_route_scale': _L3_ffn_in['route_scale']}

def reference(x, ctx_1024, g_xattn, g_ffn, L0_xattn_Wi_w, L0_xattn_Wi_b, L0_xattn_Wf_w, L0_xattn_Wf_b, L0_xattn_gn_w, L0_xattn_gn_b, L0_ffn_Wg, L0_ffn_W_in, L0_ffn_W_out, L1_xattn_W, L1_xattn_b, L1_ffn_w_gate, L1_ffn_w_up, L1_ffn_w_down, L2_xattn_Wk1, L2_xattn_Wv1, L2_xattn_Wq1, L2_xattn_Wo1, L2_xattn_bo1, L2_xattn_Wk2, L2_xattn_Wv2, L2_xattn_Wq2, L2_xattn_Wo2, L2_xattn_bo2, L2_xattn_Wf, L2_xattn_bf, L2_xattn_g1, L2_xattn_b1, L2_xattn_g2, L2_xattn_b2, L2_xattn_g3, L2_xattn_b3, L2_ffn_router_w, L2_ffn_w13, L2_ffn_w2, L3_xattn_Wq, L3_xattn_bq, L3_xattn_Wk, L3_xattn_bk, L3_xattn_Wv, L3_xattn_bv, L3_xattn_Wo, L3_xattn_bo, L3_ffn_gate_W, L3_ffn_W1, L3_ffn_b1, L3_ffn_W2, L3_ffn_b2, L3_ffn_Ws1, L3_ffn_bs1, L3_ffn_Ws2, L3_ffn_bs2, L3_ffn_route_scale):
    import jax
    import jax.numpy as jnp

    def _L0_xattn_ref(q, k, v, Wi_w, Wi_b, Wf_w, Wf_b, gn_w, gn_b):
        import jax, jax.numpy as jnp
        import numpy as np
        DIM = 128
        HEADS = 8
        HEAD_DIM = DIM // HEADS
        TAU = HEAD_DIM ** 0.5
        BS, SEQ = (1, 256)
        bs, seq, dim = q.shape
        gate_in = jnp.concatenate([q, k, v], axis=-1)
        itilde = jnp.einsum('bsd,hd->bhs', gate_in, Wi_w) + Wi_b[None, :, None]
        ftilde = jnp.einsum('bsd,hd->bhs', gate_in, Wf_w) + Wf_b[None, :, None]
        csum = jnp.cumsum(jax.nn.log_sigmoid(ftilde), axis=-1)
        Fmat = csum[..., :, None] - csum[..., None, :]
        mask = jnp.tril(jnp.ones((seq, seq), dtype=bool))
        F_act = jnp.where(mask, Fmat, -jnp.inf)
        Dtilde = F_act + itilde[..., None, :]
        max_d = jnp.max(Dtilde, axis=-1, keepdims=True)
        D = jnp.exp(Dtilde - max_d)
        qh = q.reshape(bs, seq, HEADS, HEAD_DIM).transpose(0, 2, 1, 3)
        kh = k.reshape(bs, seq, HEADS, HEAD_DIM).transpose(0, 2, 1, 3)
        vh = v.reshape(bs, seq, HEADS, HEAD_DIM).transpose(0, 2, 1, 3)
        Ctilde = jnp.einsum('bhid,bhjd->bhij', qh, kh) * D / TAU
        maxit = jnp.maximum(jnp.abs(jnp.sum(Ctilde, axis=-1, keepdims=True)), jnp.exp(-max_d))
        Htilde = jnp.einsum('bhij,bhjd->bhid', Ctilde, vh) / (maxit + 1e-06)
        x = Htilde.transpose(0, 2, 1, 3).reshape(bs * seq, HEADS, HEAD_DIM)
        mean = jnp.mean(x, axis=-1, keepdims=True)
        var = jnp.var(x, axis=-1, keepdims=True)
        xn = (x - mean) / jnp.sqrt(var + 1e-05)
        out = xn.reshape(bs * seq, DIM) * gn_w + gn_b
        return out.reshape(bs, seq, DIM)

    def _L0_ffn_ref(x, Wg, W_in, W_out):
        import math
        import jax, jax.numpy as jnp
        import numpy as np
        B, T, H = (4, 256, 128)
        E, K, F = (8, 2, 256)
        CAP_FACTOR = 1.25

        def _moe_forward(x, Wg, W_in, W_out):
            b, t, h = x.shape
            xf = x.reshape(-1, h)
            S = xf.shape[0]
            C = int(math.ceil(K * S / E * CAP_FACTOR))
            logits = xf @ Wg
            probs = jax.nn.softmax(logits, axis=-1)
            top_vals, top_idx = jax.lax.top_k(probs, K)
            flat_idx = top_idx.T.reshape(-1)
            onehot = jax.nn.one_hot(flat_idx, E, dtype=jnp.int32)
            cum = jnp.cumsum(onehot, axis=0) - 1
            loc = jnp.take_along_axis(cum, flat_idx[:, None], axis=1)[:, 0]
            loc = loc.reshape(K, S).T
            keep = loc < C
            gates = top_vals * keep.astype(top_vals.dtype)
            denom = jnp.maximum(gates.sum(-1, keepdims=True), 1e-09)
            gates = gates / denom
            loc_c = jnp.where(keep, loc, C)
            e_flat = top_idx.reshape(-1)
            l_flat = loc_c.reshape(-1)
            xk = jnp.broadcast_to(xf[:, None, :], (S, K, h)).reshape(-1, h)
            xk = jnp.where(keep.reshape(-1, 1), xk, 0.0)
            buf = jnp.zeros((E, C + 1, h), x.dtype).at[e_flat, l_flat].set(xk)
            inp = buf[:, :C]
            hid = jnp.einsum('ech,ehf->ecf', inp, W_in)
            a, g = jnp.split(hid, 2, axis=-1)
            hid = jax.nn.gelu(a, approximate=False) * g
            out_e = jnp.einsum('ecf,efh->ech', hid, W_out)
            out_pad = jnp.concatenate([out_e, jnp.zeros((E, 1, h), out_e.dtype)], axis=1)
            gathered = out_pad[e_flat, l_flat].reshape(S, K, h)
            y = (gathered * gates[..., None]).sum(axis=1)
            return y.reshape(b, t, h)
        return _moe_forward(x, Wg, W_in, W_out)

    def _L1_xattn_ref(x1, x2, W, b):
        import jax, jax.numpy as jnp
        import numpy as np
        D1, D2, D3 = (128, 128, 128)
        d1 = x1.shape[-1]
        W1 = W[:, :d1]
        W2 = W[:, d1:]
        part1 = jnp.einsum('bld,ed->ble', x1, W1)
        part2 = jnp.einsum('bld,ed->be', x2, W2) / x2.shape[1]
        return part1 + part2[:, None, :] + b

    def _L1_ffn_ref(x, w_gate, w_up, w_down):
        import jax, jax.numpy as jnp
        import numpy as np
        BLOCK = 32
        W_BITS = 4
        ACT_BITS = 16

        def act_qdq(x):
            qmax = 2.0 ** (ACT_BITS - 1) - 1.0
            scale = jnp.maximum(jnp.max(jnp.abs(x)) / qmax, 1e-12)
            return jnp.clip(jnp.round(x / scale), -qmax - 1.0, qmax) * scale

        def fixed_qdq_u16(x):
            scale = 1.0 / 65536.0
            return jnp.clip(jnp.round(x / scale), 0.0, 65535.0) * scale

        def lpbq_dequant(w):
            O, I = w.shape
            qmax = 2.0 ** (W_BITS - 1) - 1.0
            wb = w.reshape(O, I // BLOCK, BLOCK)
            s = jnp.maximum(jnp.max(jnp.abs(wb), axis=-1, keepdims=True) / qmax, 1e-12)
            wq = jnp.clip(jnp.round(wb / s), -qmax - 1.0, qmax) * s
            return wq.reshape(O, I)
        x = act_qdq(x)
        up = act_qdq(x @ lpbq_dequant(w_up).T)
        gate = act_qdq(x @ lpbq_dequant(w_gate).T)
        sig = fixed_qdq_u16(jax.nn.sigmoid(gate))
        gate = act_qdq(gate * sig)
        o = act_qdq(gate * up)
        return o @ lpbq_dequant(w_down).T

    def _L2_xattn_ref(inputs, context_seq, Wk1, Wv1, Wq1, Wo1, bo1, Wk2, Wv2, Wq2, Wo2, bo2, Wf, bf, g1, b1, g2, b2, g3, b3):
        import jax, jax.numpy as jnp
        import numpy as np
        B, S, SC, E, H = (2, 256, 256, 128, 16)
        D = E // H
        EPS = 1e-06

        def _layernorm(x, g, b):
            m = jnp.mean(x, axis=-1, keepdims=True)
            v = jnp.mean((x - m) ** 2, axis=-1, keepdims=True)
            return (x - m) / jnp.sqrt(v + EPS) * g + b

        def _mha(xk, xv, xq, Wk, Wv, Wq, Wo, bo, masked):
            K = jnp.einsum('bse,hed->bhsd', xk, Wk)
            V = jnp.einsum('bse,hed->bhsd', xv, Wv)
            Q = jnp.einsum('bqe,hed->bhqd', xq, Wq)
            scores = jnp.einsum('bhqd,bhkd->bhqk', Q, K)
            sk = xk.shape[1]
            if masked:
                causal = jnp.triu(jnp.ones((xq.shape[1], sk), dtype=bool), k=1)
                scores = jnp.where(causal, -jnp.inf, scores)
            att = jax.nn.softmax(scores / jnp.sqrt(jnp.asarray(sk, scores.dtype)), axis=-1)
            out = jnp.einsum('bhqk,bhkd->bhqd', att, V)
            out = out.transpose(0, 2, 1, 3).reshape(out.shape[0], out.shape[2], -1)
            return jax.nn.relu(out @ Wo + bo)
        a = _mha(inputs, inputs, inputs, Wk1, Wv1, Wq1, Wo1, bo1, masked=True)
        a = _layernorm(inputs + a, g1, b1)
        c = _mha(context_seq, context_seq, a, Wk2, Wv2, Wq2, Wo2, bo2, masked=False)
        c = _layernorm(c + c, g2, b2)
        f = jax.nn.relu(c @ Wf + bf)
        return _layernorm(c + f, g3, b3)

    def _L2_ffn_ref(x, router_w, w13, w2):
        import jax, jax.numpy as jnp
        import numpy as np
        E, H, I, K = (8, 128, 256, 2)
        B, S = (4, 256)
        logits = jnp.einsum('bsh,eh->bse', x, router_w)
        probs = jax.nn.softmax(logits, axis=-1)
        weights, indices = jax.lax.top_k(probs, K)
        weights = weights / (weights.sum(axis=-1, keepdims=True) + 1e-06)
        h13 = jnp.einsum('bsh,ehi->bsei', x, w13)
        gate, up = jnp.split(h13, 2, axis=-1)
        h = jax.nn.silu(gate) * up
        y = jnp.einsum('bsei,eih->bseh', h, w2)
        y_sel = jnp.take_along_axis(y, indices[..., None], axis=2)
        return (y_sel * weights[..., None]).sum(axis=2)

    def _L3_xattn_ref(query, key, value, Wq, bq, Wk, bk, Wv, bv, Wo, bo):
        import jax, jax.numpy as jnp
        import numpy as np
        EMBED_DIM = 128
        NUM_HEADS = 16
        HEAD_DIM = EMBED_DIM // NUM_HEADS

        def _split_heads(x, B, S):
            return x.reshape(B, S, NUM_HEADS, HEAD_DIM).transpose(0, 2, 1, 3)
        B, S, D = query.shape
        q = _split_heads(query @ Wq + bq, B, S)
        k = _split_heads(key @ Wk + bk, B, S)
        v = _split_heads(value @ Wv + bv, B, S)
        score = jnp.einsum('bhqd,bhkd->bhqk', q, k) / np.sqrt(HEAD_DIM)
        weights = jax.nn.softmax(score, axis=-1)
        attn = jnp.einsum('bhqk,bhkd->bhqd', weights, v)
        out = attn.transpose(0, 2, 1, 3).reshape(B, S, D)
        return out @ Wo + bo

    def _L3_ffn_ref(x, gate_W, W1, b1, W2, b2, Ws1, bs1, Ws2, bs2, route_scale):
        import jax, jax.numpy as jnp
        import numpy as np
        B, S, D, E, H, K = (4, 256, 128, 8, 64, 2)
        scores = jax.nn.sigmoid(x @ gate_W) * route_scale
        topk_scores, topk_idx = jax.lax.top_k(scores, K)
        topk_w = topk_scores / topk_scores.sum(-1, keepdims=True)
        onehot = jax.nn.one_hot(topk_idx, E, dtype=x.dtype)
        gate_full = jnp.einsum('bsk,bske->bse', topk_w, onehot)
        h = jax.nn.gelu(jnp.einsum('bsd,edh->bseh', x, W1) + b1, approximate=False)
        y = jnp.einsum('bseh,ehd->bsed', h, W2) + b2
        expert_out = jnp.einsum('bse,bsed->bsd', gate_full, y)
        shared = jax.nn.gelu(x @ Ws1 + bs1, approximate=False) @ Ws2 + bs2
        return expert_out + shared
    x = x + jnp.tanh(g_xattn[0]) * _L0_xattn_ref(_layernorm(x, axis=-1), ctx_1024, ctx_1024, L0_xattn_Wi_w, L0_xattn_Wi_b, L0_xattn_Wf_w, L0_xattn_Wf_b, L0_xattn_gn_w, L0_xattn_gn_b)
    x = x + jnp.tanh(g_ffn[0]) * _L0_ffn_ref(_layernorm(x, axis=-1), L0_ffn_Wg, L0_ffn_W_in, L0_ffn_W_out)
    x = x + jnp.tanh(g_xattn[1]) * _L1_xattn_ref(_layernorm(x, axis=-1), ctx_1024, L1_xattn_W, L1_xattn_b)
    x = x + jnp.tanh(g_ffn[1]) * _L1_ffn_ref(_layernorm(x, axis=-1), L1_ffn_w_gate, L1_ffn_w_up, L1_ffn_w_down)
    x = x + jnp.tanh(g_xattn[2]) * _L2_xattn_ref(_layernorm(x, axis=-1), ctx_1024, L2_xattn_Wk1, L2_xattn_Wv1, L2_xattn_Wq1, L2_xattn_Wo1, L2_xattn_bo1, L2_xattn_Wk2, L2_xattn_Wv2, L2_xattn_Wq2, L2_xattn_Wo2, L2_xattn_bo2, L2_xattn_Wf, L2_xattn_bf, L2_xattn_g1, L2_xattn_b1, L2_xattn_g2, L2_xattn_b2, L2_xattn_g3, L2_xattn_b3)
    x = x + jnp.tanh(g_ffn[2]) * _L2_ffn_ref(_layernorm(x, axis=-1), L2_ffn_router_w, L2_ffn_w13, L2_ffn_w2)
    x = x + jnp.tanh(g_xattn[3]) * _L3_xattn_ref(_layernorm(x, axis=-1), ctx_1024, ctx_1024, L3_xattn_Wq, L3_xattn_bq, L3_xattn_Wk, L3_xattn_bk, L3_xattn_Wv, L3_xattn_bv, L3_xattn_Wo, L3_xattn_bo)
    x = x + jnp.tanh(g_ffn[3]) * _L3_ffn_ref(_layernorm(x, axis=-1), L3_ffn_gate_W, L3_ffn_W1, L3_ffn_b1, L3_ffn_W2, L3_ffn_b2, L3_ffn_Ws1, L3_ffn_bs1, L3_ffn_Ws2, L3_ffn_bs2, L3_ffn_route_scale)
    return x

_drawn_inputs = setup_inputs


def setup_inputs(seed=0):
    import zlib

    import numpy as np

    out = dict(_drawn_inputs(seed))
    spreads = {'L0_xattn_Wi_w': (0.0, 0.1),
     'L0_xattn_Wf_w': (0.0, 0.1),
     'L0_xattn_gn_w': (1.0, 0.2),
     'L0_xattn_gn_b': (0.0, 0.1),
     'L2_xattn_bo1': (0.0, 2.0),
     'L2_xattn_bo2': (0.0, 0.1),
     'L2_xattn_bf': (0.0, 0.272),
     'L2_xattn_g1': (1.0, 0.6),
     'L2_xattn_b1': (0.0, 2.0),
     'L2_xattn_g2': (1.0, 0.2),
     'L2_xattn_b2': (0.0, 0.1),
     'L2_xattn_g3': (1.0, 0.2),
     'L2_xattn_b3': (0.0, 0.273),
     'L3_xattn_bq': (0.0, 2.0),
     'L3_xattn_bk': (0.0, 2.0),
     'L3_xattn_bv': (0.0, 0.61),
     'L3_xattn_bo': (0.0, 0.577),
     'L3_ffn_b1': (0.0, 0.8),
     'L3_ffn_b2': (0.0, 0.8),
     'L3_ffn_bs1': (0.0, 0.8),
     'L3_ffn_bs2': (0.0, 0.708)}
    factors = {'g_ffn': 8.0,
     'L0_xattn_Wi_b': 28.506,
     'L1_xattn_b': 3.04,
     'L1_ffn_w_gate': 8.0,
     'L1_ffn_w_up': 8.0,
     'L1_ffn_w_down': 8.0,
     'L2_xattn_Wk1': 24.455,
     'L2_xattn_Wv1': 8.0,
     'L2_xattn_Wq1': 23.101,
     'L2_xattn_Wo1': 8.0,
     'L2_xattn_Wk2': 8.0,
     'L2_xattn_Wq2': 8.0,
     'L2_ffn_router_w': 8.0,
     'L2_ffn_w13': 8.0,
     'L2_ffn_w2': 8.0,
     'L3_ffn_W1': 8.0,
     'L3_ffn_W2': 8.0,
     'L3_ffn_Ws1': 6.217,
     'L3_ffn_Ws2': 5.842}
    for name, (base, spread) in spreads.items():
        noise = np.random.default_rng([zlib.crc32(name.encode()), seed]).standard_normal(out[name].shape)
        drawn = base * np.exp(spread * noise) if base else spread * noise
        out[name] = jnp.asarray(drawn.astype(out[name].dtype))
    for name, factor in factors.items():
        out[name] = (out[name] * factor).astype(out[name].dtype)
    return out
```

```python
from contextlib import ExitStack

import concourse.bass as bass
from concourse import mybir

F32 = mybir.dt.float32
F16 = mybir.dt.float16
BF16 = mybir.dt.bfloat16
ALU = mybir.AluOpType
ACT = mybir.ActivationFunctionType
AX = mybir.AxisListType

NB = 8
P = 128
D = 128
NE = 8
F = 256
CAP = 320
I1 = 384
H0, D0 = 8, 16
HA, DA = 16, 8
SLOT0, SLOTA = 64, 32
PSUM_BANKS, BANK = 8, 512
MASKED = -1.0e30
MAGIC = 12582912.0
QMAX = 32767.0
QMAX4 = 7.0
FPS = 2
HALF = 4


def schedule():
    out = [("setup", 0)]

    def skew(names, items):
        for t in range(len(items) + len(names) - 1):
            for s in reversed(range(len(names))):
                if 0 <= t - s < len(items):
                    out.append((names[s], items[t - s]))

    batches = list(range(NB))
    skew(["x0_norm", "x0_z", "x0_gate"], batches)
    out.append(("x0_forget", 0))
    skew(["x0_stack", "x0_score", "x0_value", "x0_group", "f0_norm", "f0_z"], batches)
    out.append(("f0_route", 0))
    experts = [(e, g) for e in range(NE) for g in range(FPS)]
    skew(["f0_up", "f0_down"], experts)
    skew(["x1_norm", "x1_z", "x1_out", "f1_norm", "f1_z"], batches)
    out.append(("f1_scale", 0))
    skew(["f1_up"], [(c, g) for c in range(3) for g in range(FPS)])
    out.append(("f1_mid", 0))
    skew(["f1_down"], batches)
    att = ["kv", "stack", "max", "again", "exp", "av", "wo"]
    skew(["x2_norm", "x2_z"] + ["a_" + s for s in att] + ["a_norm", "b_q"] + ["b_" + s for s in att]
         + ["b_norm", "b_f", "b_last", "f2_norm", "f2_z"], batches)
    out.append(("f2_route", 0))
    skew(["f2_up", "f2_down"], experts)
    skew(["x3_norm", "x3_z", "c_kv"] + ["c_" + s for s in att[1:]] + ["f3_norm", "f3_z"], batches)
    out.append(("f3_route", 0))
    skew(["f3_up", "f3_down"], [0, 1])
    return out


def psum_units(stage, item):
    one = {
        "x0_z": 1, "x0_forget": 3, "x0_value": 1, "f0_z": 1, "f0_route": 1 + 1, "f0_down": 1,
        "x1_z": 1, "x1_out": 1, "f1_z": 1, "f1_scale": 2, "f1_up": 2, "f1_down": 1,
        "x2_z": 1, "b_q": 1, "b_f": 1, "f2_z": 1, "f2_route": 1, "f2_down": 1,
        "x3_z": 1, "f3_z": 1, "f3_route": 1, "f3_down": 4, "b_last": 1,
    }
    if stage == "setup":
        names = ["ctx0", "ctx1", "gate_w", "w1"] + [f"l1_{i}" for i in range(3)] + ["router"]
    elif stage == "x0_gate":
        names = ["gates"] if item == 0 else []
    elif stage == "x0_stack":
        names = ["qk", "am"]
    elif stage == "x0_score":
        names = ["e0", "e1", "s0", "s1"]
    elif stage in ("f0_up", "f2_up"):
        names = ["a0", "g0", "a1", "g1"]
    elif stage == "f1_mid":
        names = ["ug_t", "ug_b", "gs_t", "gs_b", "o_t", "o_b"]
    elif stage == "f3_up":
        names = [f"h{c}" for c in range(5)] + [f"gate{c}" for c in range(4)]
        names = ["h0", "gate0", "h1", "gate1", "h2", "gate2", "h3", "gate3", "h4"]
    elif stage in ("a_kv", "b_kv", "c_kv"):
        names = ["qkv"]
    elif stage in ("a_stack", "b_stack", "c_stack"):
        names = ["qk"]
    elif stage in ("a_max", "b_max", "c_max"):
        names = [f"s{i}" for i in range(4)]
    elif stage in ("a_again", "b_again", "c_again"):
        names = ["q"]
    elif stage in ("a_exp", "b_exp", "c_exp"):
        names = [f"t{i}" for i in range(4)]
    elif stage in ("a_av", "b_av", "c_av"):
        names = ["av"]
    elif stage in ("a_wo", "b_wo", "c_wo"):
        names = ["t", "wo"]
    elif stage == "b_q":
        names = ["t", "q"]
    elif stage == "b_f":
        names = ["t", "f"]
    elif stage == "b_last":
        names = []
    elif stage == "f1_up":
        names = ["up", "gate"]
    elif stage == "x0_forget":
        names = ["csum", "at", "m"]
    elif stage == "f0_route":
        names = ["logit", "cum", "total"]
    elif stage == "f1_scale":
        names = ["x_t", "x_b"]
    elif stage == "f3_route":
        names = ["logit", "gt0", "gt1"]
    elif stage == "f3_down":
        names = ["o"]
    else:
        names = ["u"] * one.get(stage, 0)
    return names


class Banks:

    def __init__(self, order, psum, full, free):
        self.psum, self.full, self.free = psum, full, free
        self.place = {}
        n = 0
        for stage, item in order:
            for name in psum_units(stage, item):
                self.place[stage, item, name] = (n % PSUM_BANKS, n // PSUM_BANKS)
                n += 1

    def tile(self, *key):
        k, _ = self.place[key]
        return self.psum[:, k * BANK:(k + 1) * BANK]

    def take(self, pe, *key):
        k, turn = self.place[key]
        if turn:
            pe.wait_ge(self.free[k], turn)
        return self.psum[:, k * BANK:(k + 1) * BANK]

    def freed(self, *key):
        k, turn = self.place[key]
        return self.free[k], turn + 1

    def fill(self, ins, *key):
        ins.then_inc(self.full[self.place[key][0]], 1)

    def get(self, eng, *key):
        k, turn = self.place[key]
        eng.wait_ge(self.full[k], turn + 1)
        return self.psum[:, k * BANK:(k + 1) * BANK]


class Chain:

    def __init__(self, eng, own):
        self.eng, self.own, self.count, self.last = eng, own, {}, None

    def do(self, ins, sem=None):
        sem = self.own if sem is None else sem
        if isinstance(sem, tuple):
            ins.then_inc(sem[0], 1)
            self.last = sem
            return
        ins.then_inc(sem, 1)
        n = self.count[sem.name] = self.count.get(sem.name, 0) + 1
        self.last = (sem, n)

    def sync(self):
        self.eng.wait_ge(*self.last)


def bc(ap, shape):
    return ap.to_broadcast(list(shape))


def gated_stack(nc, t):
    order = schedule()
    with ExitStack() as ctx:
        def sb(name, shape, dt=F32):
            return ctx.enter_context(nc.sbuf_tensor(name, shape, dt))

        sems = {}

        def sem(name):
            if name not in sems:
                sems[name] = ctx.enter_context(nc.semaphore(name))
            return sems[name]

        x = sb("x", [P, NB, D])
        z = sb("z", [P, NB, D])
        zT = sb("zT", [P, NB, P])
        zTh = sb("zTh", [P, NB, P], F16)
        zTl = sb("zTl", [P, NB, P], F16)
        c = sb("c", [P, NB, D])
        cT = sb("cT", [P, NB, P])
        ident = sb("ident", [P, P])
        ident16 = sb("ident16", [P, P], F16)
        identb = sb("identb", [P, P], BF16)
        ones = sb("ones", [P, P])
        tri = sb("tri", [P, P])
        maskT = sb("maskT", [P, 4, P], BF16)
        maskQ = sb("maskQ", [P, 4, P], BF16)
        mhalf = sb("mhalf", [P, 8])
        reset = sb("reset", [P, 2 * NE, NB])
        rank = sb("rank", [P, NB, NE])
        tg = sb("tg", [P, 8])
        wifT = sb("wifT", [P, 3, 2 * H0])
        ifb = sb("ifb", [P, 2 * H0])
        wg0 = sb("wg0", [P, NE])
        stage_f32 = sb("stage_f32", [P, NE * 2 * F])
        split = {"f0": sb("split0", [P, 2 * NE * 2 * F // 2]), "f2": sb("split2", [P, 2 * NE * 2 * F // 2])}
        phase = sb("phase", [P, 8192])
        work = sb("work", [P, 4096])
        win = stage_f32[:, :].rearrange("p (e f) -> p e f", e=NE)
        winh = {k: t_[:, 0:NE * F].bitcast(F16).rearrange("p (e f) -> p e f", e=NE) for k, t_ in split.items()}
        winl = {k: t_[:, NE * F:2 * NE * F].bitcast(F16).rearrange("p (e f) -> p e f", e=NE) for k, t_ in split.items()}

        def carve(region, *tiles):
            at_, out = 0, []
            for shape, dt in tiles:
                n = 1
                for k in shape:
                    n *= k
                words = n if dt == F32 else n // 2
                v_ = region[:, at_:at_ + words]
                if dt != F32:
                    v_ = v_.bitcast(dt)
                names = " ".join("abcd"[:len(shape)])
                if len(shape) > 1:
                    v_ = v_.rearrange(f"p ({names}) -> p {names}", **{"abcd"[i]: shape[i] for i in range(1, len(shape))})
                out.append(v_)
                at_ += words
            assert at_ <= region.shape[1]
            return out
        wout = {"f0": sb("wout0", [P, NE, 2, D]), "f2": sb("wout2", [P, NE, 2, D])}
        t1 = sb("t1", [P, NB, D])
        t1f = t1[:, :, :].rearrange("p b d -> p (b d)")
        wif, w1 = t1f[0:2 * H0, 0:3 * D], t1f[:, 3 * D:5 * D]
        w1T = sb("w1T", [P, 2, D])
        cmean = sb("cmean", [P, NB])
        cmeanB = sb("cmeanB", [P, NB, P])
        at = sb("at", [P, NB + 1, D])
        wq8 = at[:, :, :].rearrange("p (i c) d -> p i c d", i=3)
        w8T = sb("w8T", [P, 3, I1])
        w8s = sb("w8s", [P, 3, 12])
        w8r = sb("w8r", [P, 3, 12])
        wA = sb("wA", [P, 3, D])
        woA = sb("woA", [P, D])
        wB = sb("wB", [P, 3, D])
        woB = sb("woB", [P, D])
        wf = sb("wf", [P, D])
        router = sb("router", [NE, D])
        routerT = sb("routerT", [P, NE])
        wC = sb("wC", [P, 3, D])
        woC = sb("woC", [P, D])
        wg3 = sb("wg3", [P, NE])
        w31 = sb("w31", [P, NE, 64])
        w32 = sb("w32", [P, 4, D])
        b31 = sb("b31", [P, 4])
        b32 = sb("b32", [NE, D])
        ws1 = sb("ws1", [P, 64])
        ws2 = sb("ws2", [64, D])
        bs1 = sb("bs1", [64, 1])
        rscale = sb("rscale", [P, 1])
        sel = sb("sel", [NE, 4, P])
        vecs = ["L0_xattn_gn_w", "L0_xattn_gn_b", "L1_xattn_b", "L2_xattn_bo1", "L2_xattn_g1",
                "L2_xattn_b1", "L2_xattn_bo2", "L2_xattn_g2", "L2_xattn_b2", "L2_xattn_bf",
                "L2_xattn_g3", "L2_xattn_b3", "L3_xattn_bo", "L3_ffn_bs2"]
        rows = sb("rows", [P, len(vecs), D])
        bqkv = sb("bqkv", [P, 3, D])

        def vec(name):
            return rows[:, vecs.index(name), :]

        stats = sb("stats", [P, NB, 6])
        mv = sb("mv", [P, NB, 2])
        vr = sb("vr", [P, NB])
        rstd = sb("rstd", [P, NB])
        gi = sb("gi", [P, NB, H0])
        gf = sb("gf", [P, NB, H0])
        ga = sb("ga", [P, NB, H0])
        gb = sb("gb", [P, NB, H0])
        cs = sb("cs", [P, NB, H0])
        aT = sb("aT", [NB * H0, P])
        mT = sb("mT", [NB * H0, P])
        mm = sb("mm", [P, NB, H0])
        floor = sb("floor", [P, NB, H0])
        nrm = sb("nrm", [P, H0])
        hm = sb("hm", [P, H0])
        sq = sb("sq", [P, D])
        hv = sb("hv", [P, NB, H0])
        hr = sb("hr", [P, NB, H0])
        lg = sb("lg", [P, NB, NE])
        pr = sb("pr", [P, NB, NE])
        p2 = sb("p2", [P, NB, NE])
        eq = sb("eq", [P, NB, NE])
        top = sb("top", [P, NB, 1])
        oh = sb("oh", [P, 2, NB, NE])
        cum = sb("cum", [P, 2, NB, NE])
        tot = sb("tot", [P, 2 * NE, NB])
        inc = sb("inc", [P, 2 * NE, NB])
        gate = sb("gate", [P, NB, NE])
        gsum = sb("gsum", [P, NB, 1])
        mx = sb("mx", [P, 2])
        m1 = sb("m1", [2, 2])
        m1b = sb("m1b", [2, 2])
        sc = sb("sc", [P, 8])
        qs = sb("qs", [P, NB, HA, SLOTA], F16)
        ks = sb("ks", [P, NB, HA, SLOTA], F16)
        nmax = sb("nmax", [P, NB, HA])
        rden = sb("rden", [P, HA])
        atT = sb("atT", [P, 2, P])
        t2 = c
        hh = t1
        acc = at
        mst, am, q0, k0, qk0, dec, cc = carve(
            phase, ((NB * H0, SLOT0), F16), ((2, 8, P), F16), ((2, H0, SLOT0), F16),
            ((2, H0, SLOT0), F16), ((2, 8, P), F16), ((2, 4, P), F32), ((2, H0, P), F32))
        xq, up, gt = carve(phase, ((NB * P,), F32), ((3, NB * P), F32), ((3, NB * P), F32))
        pt, qkT = carve(phase, ((2, HA, P), F32), ((NB, 8, P), F16))
        act, hid = carve(work, ((2, 2, BANK), F32), ((2, 2, BANK), F32))
        v0, ast = carve(work, ((NB, H0, D0 + 1), F32), ((NB * H0, SLOT0), F16))
        (h3,) = carve(work, ((5, BANK), F32))
        (sg,) = carve(split["f0"], ((3, NB * P), F32))
        q2T, q32, v9 = carve(stage_f32, ((NB, 4, P), F16), ((2, 3, D), F32), ((NB, HA, DA + 1), F32))
        gT = cmeanB[0:NE, :, :]
        psum = ctx.enter_context(nc.psum_tensor("psum", [P, PSUM_BANKS * BANK], F32))
        full = [sem(f"bank{k}_full") for k in range(PSUM_BANKS)]
        free = [sem(f"bank{k}_free") for k in range(PSUM_BANKS)]
        banks = Banks(order, psum, full, free)

        norms_ = [o for o in order if o[0].endswith("_norm") or o[0] == "b_last"]
        norm_turn = {o: n + 1 for n, o in enumerate(norms_)}
        pt_turn = {(s[0], b): n for n, (s, b) in enumerate(o for o in order if o[0] in ("a_exp", "b_exp", "c_exp"))}
        assert list(pt_turn) == [(s[0], b) for s, b in order if s in ("a_av", "b_av", "c_av")]

        def as16(tile):
            return tile.bitcast(F16)

        done = sem("stored")
        n_loads = {}

        block = ctx.enter_context(nc.Block())

        loads = [
            ("x", x[:, :, :], t["x"].rearrange("b p d -> p b d")),
            ("x", c[:, :, :], t["ctx_1024"].rearrange("b p d -> p b d")),
            ("x0", wif[0:H0, :], t["L0_xattn_Wi_w"]),
            ("x0", wif[H0:2 * H0, :], t["L0_xattn_Wf_w"]),
            ("x0", ifb[:, 0:H0], t["L0_xattn_Wi_b"].partition_broadcast(P)),
            ("x0", ifb[:, H0:2 * H0], t["L0_xattn_Wf_b"].partition_broadcast(P)),
            ("x0", tg[:, 0:4], t["g_xattn"].partition_broadcast(P)),
            ("x0", tg[:, 4:8], t["g_ffn"].partition_broadcast(P)),
            ("x0", wg0[:, :], t["L0_ffn_Wg"]),
            ("win", win, t["L0_ffn_W_in"].rearrange("e h f -> h e f")),
        ] + [("rows", rows[:, i, :], t[n].partition_broadcast(P)) for i, n in enumerate(vecs)] + [
            ("wout", wout["f0"][:, :, :, :], t["L0_ffn_W_out"].rearrange("e (c p) h -> p e c h", p=P)),
            ("l1", w1[:, :], t["L1_xattn_W"]),
            ("l1", wq8[:, 0, :, :], t["L1_ffn_w_up"].rearrange("(c p) d -> p c d", p=P)),
            ("l1", wq8[:, 1, :, :], t["L1_ffn_w_gate"].rearrange("(c p) d -> p c d", p=P)),
            ("l1", wq8[:, 2, :, :], t["L1_ffn_w_down"].rearrange("p (c d) -> p c d", c=3)),
            ("l1", router[:, :], t["L2_ffn_router_w"]),
        ] + [("l2", w[:, i, :].rearrange("e (h d) -> e h d", h=HA), t[f"L2_xattn_W{n}{m}"].rearrange("h e d -> e h d"))
             for w, m in ((wA, 1), (wB, 2)) for i, n in enumerate("qkv")] + [
            ("l2", woA[:, :], t["L2_xattn_Wo1"]),
            ("l2", woB[:, :], t["L2_xattn_Wo2"]),
            ("l2", wf[:, :], t["L2_xattn_Wf"]),
            ("win2", win, t["L2_ffn_w13"].rearrange("e h f -> h e f")),
            ("win2", wout["f2"][:, :, :, :], t["L2_ffn_w2"].rearrange("e (c p) h -> p e c h", p=P)),
        ] + [("l3", wC[:, i, :], t[f"L3_xattn_W{n}"]) for i, n in enumerate("qkv")] \
          + [("l3", bqkv[:, i, :], t[f"L3_xattn_b{n}"].partition_broadcast(P)) for i, n in enumerate("qkv")] + [
            ("l3", woC[:, :], t["L3_xattn_Wo"]),
            ("l3", wg3[:, :], t["L3_ffn_gate_W"]),
            ("l3", w31[:, :, :], t["L3_ffn_W1"].rearrange("e d h -> d e h")),
            ("l3", w32[:, :, :], t["L3_ffn_W2"].rearrange("(c two) h d -> (two h) c d", two=2)),
            ("l3", b31[:, :], t["L3_ffn_b1"].rearrange("(c two) h -> (two h) c", two=2)),
            ("l3", b32[:, :], t["L3_ffn_b2"]),
            ("l3", ws1[:, :], t["L3_ffn_Ws1"]),
            ("l3", ws2[:, :], t["L3_ffn_Ws2"]),
            ("l3", bs1[:, :], t["L3_ffn_bs1"].rearrange("(h o) -> h o", o=1)),
            ("l3", rscale[:, :], t["L3_ffn_route_scale"].partition_broadcast(P)),
        ]
        for g, _, _ in loads:
            n_loads[g] = n_loads.get(g, 0) + 16

        def loaded(eng, *groups):
            for g in groups:
                eng.wait_ge(sem("loaded_" + g), n_loads[g])

        @block.sync
        def _(sp):
            with nc.allow_non_contiguous_dma(reason="weights laid out once"):
                for g, dst, src in loads:
                    if g == "win2" and dst is win:
                        sp.wait_ge(sem("win_split"), NE)
                    sp.dma_start(dst, src).then_inc(sem("loaded_" + g), 16)
            for b in range(NB):
                sp.wait_ge(sem("x_final"), (b // HALF + 1) * HALF)
                sp.dma_start(t["out"][b], x[:, b, :]).then_inc(done, 16)
            sp.wait_ge(done, 16 * NB)

        @block.gpsimd
        def _(pool):
            ch = Chain(pool, sem("pool_step"))

            def rsqrt(col, eps, ready):
                pool.wait_ge(*ready)
                ch.do(pool.tensor_scalar(vr[:, col:col + 1], mv[:, col, 1:2], eps, None, ALU.add))
                ch.sync()
                ch.do(pool.tensor_tensor(rstd[:, col:col + 1], vr[:, col:col + 1], mhalf[:, 0:1], ALU.pow),
                      sem("rstd_ready"))

            def split_weights(which, group):
                loaded(pool, group)
                for e in range(NE):
                    ch.do(pool.tensor_copy(winh[which][:, e, :], win[:, e, :]))
                    ch.sync()
                    ch.do(pool.tensor_tensor(winl[which][:, e, :], win[:, e, :], winh[which][:, e, :], ALU.subtract),
                          sem("win_split"))

            for stage, b in order:
                if stage == "setup":
                    ch.do(pool.memset(ident[:, :], 0.0))
                    ch.do(pool.memset(ones[:, :], 1.0))
                    ch.do(pool.memset(tri[:, :], 1.0))
                    ch.do(pool.memset(maskT[:, :, :], 0.0))
                    ch.do(pool.memset(maskQ[:, :, :], 0.0))
                    ch.do(pool.memset(mhalf[:, :], -0.5))
                    ch.sync()
                    ch.do(pool.affine_select(out=ident[:, :], in_=ident[:, :], compare_op=ALU.not_equal, fill=1.0,
                                             base=0, pattern=[[-1, P]], channel_multiplier=1))
                    ch.sync()
                    ch.do(pool.tensor_copy(ident16[:, :], ident[:, :]))
                    ch.do(pool.tensor_copy(identb[:, :], ident[:, :]), sem("ident_ready"))
                    ch.do(pool.affine_select(out=tri[:, :], in_=tri[:, :], compare_op=ALU.is_ge, fill=0.0,
                                             base=0, pattern=[[1, P]], channel_multiplier=-1))
                    ch.do(pool.affine_select(out=maskT[:, :, :], in_=maskT[:, :, :], compare_op=ALU.is_ge,
                                             fill=MASKED, base=0, pattern=[[0, 4], [1, P]], channel_multiplier=-1))
                    ch.do(pool.affine_select(out=maskQ[:, :, :], in_=maskQ[:, :, :], compare_op=ALU.is_ge,
                                             fill=MASKED, base=0, pattern=[[0, 4], [-1, P]], channel_multiplier=1))
                    ch.do(pool.memset(reset[:, :, :], 1.0))
                    ch.sync()
                    ch.do(pool.memset(reset[:, :, 0:1], 0.0))
                    for e in range(NE):
                        ch.do(pool.memset(rank[:, :, e:e + 1], float(NE - e)))
                    ch.do(pool.memset(ast[:, :, :], 0.0))
                    ch.do(pool.memset(mst[:, :, :], 0.0))
                    ch.do(pool.memset(q0[:, :, :, :], 0.0))
                    ch.do(pool.memset(k0[:, :, :, :], 0.0))
                    ch.do(pool.memset(v0[:, :, :, D0:D0 + 1], 1.0))
                    ch.do(pool.memset(qs[:, :, :, :], 0.0))
                    ch.do(pool.memset(ks[:, :, :, :], 0.0))
                    ch.sync()
                    ch.do(pool.memset(ast[:, :, 3:6], 1.0))
                    ch.do(pool.memset(mst[:, :, 0:3], 1.0))
                    ch.do(pool.memset(ks[:, :, :, 3 * DA:3 * DA + 2], 1.0), sem("const_ready"))
                    ch.do(pool.memset(sel[:, :, :], 1.0))
                    ch.sync()
                    ch.do(pool.affine_select(out=sel[:, :, :], in_=sel[:, :, :], compare_op=ALU.is_ge, fill=0.0,
                                             base=0, pattern=[[P, 4], [1, P]], channel_multiplier=-64))
                    ch.sync()
                    ch.do(pool.affine_select(out=sel[:, :, :], in_=sel[:, :, :], compare_op=ALU.is_ge, fill=0.0,
                                             base=63, pattern=[[-P, 4], [-1, P]], channel_multiplier=64), sem("sel_ready"))
                    loaded(pool, "x")
                    for b_ in range(NB):
                        ch.do(pool.tensor_copy(v0[:, b_, :, 0:D0], c[:, b_, :].rearrange("p (h d) -> p h d", h=H0)),
                              sem("v0_ready"))
                elif stage in ("x0_norm", "f0_norm", "x1_norm", "f1_norm", "x2_norm", "f2_norm", "x3_norm", "f3_norm"):
                    rsqrt(b, 1e-5, (sem("stats_ready"), norm_turn[stage, b]))
                elif stage in ("a_norm", "b_norm", "b_last"):
                    rsqrt(b, 1e-6, (sem("stats_ready"), norm_turn[stage, b]))
                elif stage == "x0_stack":
                    if b >= 2:
                        pool.wait_ge(sem("x0_stacked"), b - 1)
                    kk = k0[:, b % 2, :, :]
                    cb = c[:, b, :].rearrange("p (h d) -> p h d", h=H0)
                    ch.do(pool.tensor_copy(kk[:, :, 0:D0], cb))
                    ch.sync()
                    ch.do(pool.tensor_copy(kk[:, :, 2 * D0:3 * D0], kk[:, :, 0:D0]))
                    ch.do(pool.tensor_tensor(kk[:, :, D0:2 * D0], cb, kk[:, :, 0:D0], ALU.subtract), sem("k0_ready"))
                elif stage == "x0_group":
                    pool.wait_ge(sem("hv_ready"), b + 1)
                    for h in range(1):
                        ch.do(pool.tensor_tensor(hr[:, b, :], hv[:, b, :], mhalf[:, :], ALU.pow), sem("hr_ready"))
                elif stage == "x0_forget":
                    split_weights("f0", "win")
                elif stage in ("f0_z", "f2_z"):
                    l = {"f0_z": 0, "f2_z": 1}[stage]
                    pool.wait_ge(sem("zTh_ready"), l * NB + b + 1)
                    ch.do(pool.tensor_tensor(zTl[:, b, :], zT[:, b, :], zTh[:, b, :], ALU.subtract), sem("zTl_ready"))
                elif stage == "f1_scale":
                    split_weights("f2", "win2")
                    ch.sync()
                    ch.do(pool.memset(v9[:, :, :, DA:DA + 1], 1.0), sem("v9_ones"))

        @block.tensor
        def _(pe):
            mm_ = nc.tensor.matmul
            tr = nc.tensor.transpose

            def one(out, a, b_):
                return mm_(out, a, b_, start=True, stop=True)

            def to_T(key, b, ready):
                pe.wait_ge(*ready)
                u = banks.take(pe, key, b, "u")
                banks.fill(tr(u[:, 0:P], z[:, b, :], ident[:, :]), key, b, "u")

            zs = [0]
            for stage, b in order:
                if stage == "setup":
                    pe.wait_ge(sem("ident_ready"), 1)
                    loaded(pe, "x")
                    for i in range(2):
                        u = banks.take(pe, "setup", 0, f"ctx{i}")
                        for j in range(4):
                            last = tr(u[:, j * P:(j + 1) * P], c[:, 4 * i + j, :], ident[:, :])
                        banks.fill(last, "setup", 0, f"ctx{i}")
                    loaded(pe, "x0")
                    u = banks.take(pe, "setup", 0, "gate_w")
                    for j in range(3):
                        last = tr(u[:, j * 2 * H0:(j + 1) * 2 * H0], wif[:, j * D:(j + 1) * D], ident[0:2 * H0, 0:2 * H0])
                    banks.fill(last, "setup", 0, "gate_w")
                    loaded(pe, "l1")
                    u = banks.take(pe, "setup", 0, "w1")
                    for j in range(2):
                        last = tr(u[:, j * D:(j + 1) * D], w1[:, j * D:(j + 1) * D], ident[:, :])
                    banks.fill(last, "setup", 0, "w1")
                    for i in range(3):
                        pe.wait_ge(sem("w8_ready"), i + 1)
                        u = banks.take(pe, "setup", 0, f"l1_{i}")
                        for j in range(3):
                            last = tr(u[:, j * P:(j + 1) * P], wq8[:, i, j, :], ident[:, :])
                        banks.fill(last, "setup", 0, f"l1_{i}")
                    u = banks.take(pe, "setup", 0, "router")
                    banks.fill(tr(u[:, 0:NE], router[:, :], ident[0:NE, 0:NE]), "setup", 0, "router")
                elif stage in ("x0_z", "f0_z", "x1_z", "f1_z", "x2_z", "f2_z", "x3_z", "f3_z"):
                    zs[0] += 1
                    to_T(stage, b, (sem("z_ready"), zs[0]))
                elif stage == "x0_gate":
                    pe.wait_ge(sem("x0_zT"), b + 1)
                    if b == 0:
                        u0 = banks.take(pe, "x0_gate", 0, "gates")
                        pe.wait_ge(sem("wT_ready"), 3)
                    o = u0[:, b * 2 * H0:(b + 1) * 2 * H0]
                    mm_(o, zT[:, b, :], wifT[:, 0, :], start=True, stop=False)
                    mm_(o, cT[:, b, :], wifT[:, 1, :], start=False, stop=False)
                    last = mm_(o, cT[:, b, :], wifT[:, 2, :], start=False, stop=True)
                    if b == NB - 1:
                        banks.fill(last, "x0_gate", 0, "gates")
                elif stage == "x0_forget":
                    pe.wait_ge(sem("log_forget"), 1)
                    pe.wait_ge(sem("const_ready"), 1)
                    u = banks.take(pe, stage, 0, "csum")
                    banks.fill(one(u[:, 0:NB * H0], tri[:, :], gf[:, :, :]), stage, 0, "csum")
                    pe.wait_ge(sem("a_ready"), 1)
                    u = banks.take(pe, stage, 0, "at")
                    banks.fill(tr(u[0:NB * H0, 0:P], ga[:, :, :].rearrange("p b h -> p (b h)"), ident[:, :]), stage, 0, "at")
                    pe.wait_ge(sem("mT_ready"), 1)
                    u = banks.take(pe, stage, 0, "m")
                    banks.fill(tr(u[:, 0:NB * H0], mT[:, :], ident[0:NB * H0, 0:NB * H0]), stage, 0, "m")
                elif stage == "x0_stack":
                    pe.wait_ge(sem("q0_ready"), b + 1)
                    pe.wait_ge(sem("k0_ready"), b + 1)
                    u = as16(banks.take(pe, stage, b, "qk"))
                    for i, st in enumerate((q0, k0)):
                        for j in range(4):
                            o = (4 * i + j) * P
                            last = tr(u[:, o:o + P], st[:, b % 2, 2 * j:2 * j + 2, :].rearrange("p h s -> p (h s)"), ident16[:, :])
                    banks.fill(last, stage, b, "qk")
                    u = as16(banks.take(pe, stage, b, "am"))
                    pe.wait_ge(sem("am_ready"), 1)
                    for i, st in enumerate((ast, mst)):
                        for j in range(4):
                            h = b * H0 + 2 * j
                            o = (4 * i + j) * P
                            last = tr(u[:, o:o + P], st[:, h:h + 2, :].rearrange("p h s -> p (h s)"), ident16[:, :])
                    banks.fill(last, stage, b, "am")
                elif stage == "x0_score":
                    pe.wait_ge(sem("qk0_T"), b + 1)
                    pe.wait_ge(sem("am_T"), b + 1)
                    us = [banks.take(pe, stage, b, f"e{g}") for g in range(2)]
                    for g in range(2):
                        mm_(us[g], identb[:, :], maskT[:, :, :].rearrange("p h q -> p (h q)"), start=True, stop=False)
                    for j in range(4):
                        for g in range(2):
                            r = 64 * g
                            last = mm_(us[g][:, j * P:(j + 1) * P], am[r:r + 6, b % 2, j, :], am[r:r + 6, b % 2, 4 + j, :],
                                       start=False, stop=(j == 3))
                            if j == 3:
                                banks.fill(last, stage, b, f"e{g}")
                    us = [banks.take(pe, stage, b, f"s{g}") for g in range(2)]
                    for j in range(4):
                        for g in range(2):
                            r = 64 * g
                            last = one(us[g][:, j * P:(j + 1) * P], qk0[r:r + 48, b % 2, 4 + j, :], qk0[r:r + 48, b % 2, j, :])
                            if j == 3:
                                banks.fill(last, stage, b, f"s{g}")
                elif stage == "x0_value":
                    pe.wait_ge(sem("cc_ready"), 2 * (b + 1))
                    pe.wait_ge(sem("v0_ready"), b + 1)
                    u = banks.take(pe, stage, b, "u")
                    for h in range(H0):
                        last = one(u[:, h * (D0 + 1):(h + 1) * (D0 + 1)], cc[:, b % 2, h, :], v0[:, b, h, :])
                    banks.fill(last, stage, b, "u")
                elif stage in ("f0_route", "f2_route", "f3_route"):
                    w = {"f0_route": wg0, "f2_route": routerT, "f3_route": wg3}[stage]
                    l = {"f0_route": 1, "f2_route": 2, "f3_route": 3}[stage]
                    if stage == "f3_route":
                        loaded(pe, "l3")
                    pe.wait_ge(sem(stage[:2] + "_zT"), NB)
                    name = "u" if stage == "f2_route" else "logit"
                    u = banks.take(pe, stage, 0, name)
                    for b_ in range(NB):
                        last = one(u[:, b_ * NE:(b_ + 1) * NE], zT[:, b_, :], w[:, :])
                    banks.fill(last, stage, 0, name)
                    if stage == "f0_route":
                        pe.wait_ge(sem("oh_ready"), 1)
                        u = banks.take(pe, stage, 0, "cum")
                        banks.fill(one(u[:, 0:2 * NB * NE], tri[:, :], oh[:, :, :, :].rearrange("p k b e -> p (k b e)")), stage, 0, "cum")
                        u = banks.take(pe, stage, 0, "total")
                        banks.fill(one(u[:, 0:2 * NB * NE], ones[:, :], oh[:, :, :, :].rearrange("p k b e -> p (k b e)")), stage, 0, "total")
                    if stage == "f3_route":
                        pe.wait_ge(sem("gate_ready"), 3)
                        for g in range(2):
                            u = banks.take(pe, stage, 0, f"gt{g}")
                            for j in range(4):
                                last = tr(u[0:NE, j * P:(j + 1) * P], gate[:, 4 * g + j, :], ident[:, :])
                            banks.fill(last, stage, 0, f"gt{g}")
                elif stage in ("f0_up", "f2_up"):
                    e, g = b
                    l = {"f0": 0, "f2": 1}[stage[:2]]
                    pe.wait_ge(sem("zTl_ready"), l * NB + 4 * (g + 1) if e == 0 else (l + 1) * NB)
                    pe.wait_ge(sem("win_split"), l * NE + e + 1)
                    cols = slice(4 * g, 4 * g + 4)
                    xh = zTh[:, cols, :].rearrange("p b q -> p (b q)")
                    xl = zTl[:, cols, :].rearrange("p b q -> p (b q)")
                    for i, name in enumerate(("a0", "g0", "a1", "g1")):
                        u = banks.take(pe, stage, b, name)
                        f = (i // 2) * P + (i % 2) * F
                        mm_(u, winh[stage[:2]][:, e, f:f + P], xh, start=True, stop=False)
                        mm_(u, winh[stage[:2]][:, e, f:f + P], xl, start=False, stop=False)
                        last = mm_(u, winl[stage[:2]][:, e, f:f + P], xh, start=False, stop=True)
                        banks.fill(last, stage, b, name)
                elif stage in ("f0_down", "f2_down"):
                    e, g = b
                    f = stage[:2]
                    l = {"f0": 0, "f2": 1}[f]
                    n = l * NE * FPS + e * FPS + g
                    if e == 0 and g == 0:
                        loaded(pe, "wout" if f == "f0" else "win2")
                    pe.wait_ge(sem("hid_ready"), 2 * (n + 1))
                    u = banks.take(pe, stage, b, "u")
                    for j in range(4):
                        for k in range(2):
                            last = mm_(u[:, j * D:(j + 1) * D], hid[:, n % 2, k, j * P:(j + 1) * P], wout[f][:, e, k, :],
                                       start=(k == 0), stop=(k == 1))
                    banks.fill(last, stage, b, "u")
                elif stage == "x1_out":
                    pe.wait_ge(sem("x1_zT"), b + 1)
                    if b == 0:
                        pe.wait_ge(sem("cmean_ready"), 1)
                    u = banks.take(pe, stage, b, "u")
                    mm_(u[:, 0:D], zT[:, b, :], w1T[:, 0, :], start=True, stop=False)
                    banks.fill(mm_(u[:, 0:D], cmeanB[:, b, :], w1T[:, 1, :], start=False, stop=True), stage, b, "u")
                elif stage == "f1_scale":
                    pe.wait_ge(sem("mx_ready"), 1)
                    u = banks.take(pe, stage, 0, "x_t")
                    banks.fill(tr(u[0:1, 0:P], mx[:, 0:1], ident[:, :]), stage, 0, "x_t")
                    pe.wait_ge(sem("m1_ready"), 1)
                    u = banks.take(pe, stage, 0, "x_b")
                    banks.fill(one(u[:, 0:1], ones[0:1, :], m1b[0:1, 0:1]), stage, 0, "x_b")
                elif stage == "f1_up":
                    cch, g = b
                    pe.wait_ge(sem("xq_ready"), 1)
                    for i, name in enumerate(("up", "gate")):
                        u = banks.take(pe, stage, b, name)
                        banks.fill(one(u, w8T[:, i, cch * P:(cch + 1) * P], xq[:, g * BANK:(g + 1) * BANK]), stage, b, name)
                elif stage == "f1_mid":
                    for i, name in enumerate(("ug", "gs", "o")):
                        n = 2 if name == "ug" else 1
                        pe.wait_ge(sem("mx_ready"), i + 2)
                        u = banks.take(pe, stage, 0, name + "_t")
                        banks.fill(tr(u[0:n, 0:P], mx[:, 0:n], ident[:, :]), stage, 0, name + "_t")
                        pe.wait_ge(sem("m1_ready"), i + 2)
                        u = banks.take(pe, stage, 0, name + "_b")
                        banks.fill(one(u[:, 0:n], ones[0:n, :], m1b[0:n, 0:n]), stage, 0, name + "_b")
                elif stage == "f1_down":
                    if b == 0:
                        pe.wait_ge(sem("o_ready"), 1)
                    u = banks.take(pe, stage, b, "u")
                    for k in range(3):
                        last = mm_(u[:, 0:D], sg[:, k, b * P:(b + 1) * P], w8T[:, 2, k * P:(k + 1) * P], start=(k == 0), stop=(k == 2))
                    banks.fill(last, stage, b, "u")
                elif stage in ("a_kv", "b_kv", "c_kv"):
                    m = stage[0]
                    u = banks.take(pe, stage, b, "qkv")
                    if m == "a":
                        if b == 0:
                            loaded(pe, "l2")
                        pe.wait_ge(sem("x2_zT"), b + 1)
                        last = one(u[:, 0:3 * D], zT[:, b, :], wA[:, :, :].rearrange("p i d -> p (i d)"))
                    elif m == "b":
                        last = one(u[:, D:3 * D], cT[:, b, :], wB[:, 1:3, :].rearrange("p i d -> p (i d)"))
                    else:
                        if b == 0:
                            loaded(pe, "l3")
                        pe.wait_ge(sem("x3_zT"), b + 1)
                        one(u[:, 0:D], zT[:, b, :], wC[:, 0, :])
                        last = one(u[:, D:3 * D], cT[:, b, :], wC[:, 1:3, :].rearrange("p i d -> p (i d)"))
                    banks.fill(last, stage, b, "qkv")
                elif stage == "b_q":
                    pe.wait_ge(sem("a_out"), b + 1)
                    u = banks.take(pe, stage, b, "t")
                    banks.fill(tr(u[:, 0:P], t1[:, b, :], ident[:, :]), stage, b, "t")
                    pe.wait_ge(sem("bq_T"), b + 1)
                    u = banks.take(pe, stage, b, "q")
                    banks.fill(one(u[:, 0:D], atT[:, 0, :], wB[:, 0, :]), stage, b, "q")
                elif stage in ("a_stack", "b_stack", "c_stack"):
                    m = stage[0]
                    pe.wait_ge(sem(m + "_stacks"), b + 1)
                    u = as16(banks.take(pe, stage, b, "qk"))
                    for i, st in enumerate((qs, ks)):
                        for j in range(4):
                            o = (4 * i + j) * P
                            last = tr(u[:, o:o + P], st[:, b, 4 * j:4 * j + 4, :].rearrange("p h s -> p (h s)"), ident16[:, :])
                    banks.fill(last, stage, b, "qk")
                elif stage in ("a_max", "b_max", "c_max"):
                    m = stage[0]
                    pe.wait_ge(sem(m + "_qkT"), b + 1)
                    us = [banks.take(pe, stage, b, f"s{i}") for i in range(4)]
                    if m == "a":
                        for u in us:
                            mm_(u, identb[:, :], maskQ[:, :, :].rearrange("p h q -> p (h q)"), start=True, stop=False)
                    for j in range(4):
                        for i in range(4):
                            r = 32 * i
                            last = mm_(us[i][:, j * P:(j + 1) * P], qkT[r:r + DA, b, j, :], qkT[r:r + DA, b, 4 + j, :],
                                       start=(m != "a"), stop=(j == 3 or m != "a"))
                            if j == 3:
                                banks.fill(last, stage, b, f"s{i}")
                elif stage in ("a_again", "b_again", "c_again"):
                    m = stage[0]
                    pe.wait_ge(sem(m + "_negmax"), b + 1)
                    u = as16(banks.take(pe, stage, b, "q"))
                    for j in range(4):
                        last = tr(u[:, j * P:(j + 1) * P], qs[:, b, 4 * j:4 * j + 4, :].rearrange("p h s -> p (h s)"), ident16[:, :])
                    banks.fill(last, stage, b, "q")
                elif stage in ("a_exp", "b_exp", "c_exp"):
                    m = stage[0]
                    n = 3 * DA + 2
                    pe.wait_ge(sem(m + "_q2T"), b + 1)
                    us = [banks.take(pe, stage, b, f"t{i}") for i in range(4)]
                    if m == "a":
                        for u in us:
                            mm_(u, identb[:, :], maskT[:, :, :].rearrange("p h q -> p (h q)"), start=True, stop=False)
                    for j in range(4):
                        for i in range(4):
                            r = 32 * i
                            last = mm_(us[i][:, j * P:(j + 1) * P], qkT[r:r + n, b, 4 + j, :], q2T[r:r + n, b, j, :],
                                       start=(m != "a"), stop=(j == 3 or m != "a"))
                            if j == 3:
                                banks.fill(last, stage, b, f"t{i}")
                elif stage in ("a_av", "b_av", "c_av"):
                    m = stage[0]
                    n = pt_turn[m, b]
                    u = banks.take(pe, stage, b, "av")
                    for i in range(HA):
                        h = 4 * (i % 4) + i // 4
                        if i % 4 == 0:
                            pe.wait_ge(sem("pt_ready"), 4 * n + i // 4 + 1)
                        last = one(u[:, h * (DA + 1):(h + 1) * (DA + 1)], pt[:, n % 2, h, :], v9[:, b, h, :])
                    banks.fill(last, stage, b, "av")
                elif stage in ("a_wo", "b_wo", "c_wo"):
                    m = stage[0]
                    pe.wait_ge(sem(m + "_at"), b + 1)
                    u = banks.take(pe, stage, b, "t")
                    banks.fill(tr(u[:, 0:P], at[:, b, :], ident[:, :]), stage, b, "t")
                    pe.wait_ge(sem(m + "_atT"), b + 1)
                    u = banks.take(pe, stage, b, "wo")
                    banks.fill(one(u[:, 0:D], atT[:, 0, :], {"a": woA, "b": woB, "c": woC}[m][:, :]), stage, b, "wo")
                elif stage == "b_f":
                    pe.wait_ge(sem("b_out"), b + 1)
                    u = banks.take(pe, stage, b, "t")
                    banks.fill(tr(u[:, 0:P], t1[:, b, :], ident[:, :]), stage, b, "t")
                    pe.wait_ge(sem("bf_T"), b + 1)
                    u = banks.take(pe, stage, b, "f")
                    banks.fill(one(u[:, 0:D], atT[:, 0, :], wf[:, :]), stage, b, "f")
                elif stage == "f3_up":
                    pe.wait_ge(sem("gT_ready"), 2)
                    pe.wait_ge(sem("sel_ready"), 1)
                    xg = zT[:, 4 * b:4 * b + 4, :].rearrange("p b q -> p (b q)")
                    for k in range(5):
                        u = banks.take(pe, stage, b, f"h{k}")
                        if k < 4:
                            banks.fill(one(u, w31[:, 2 * k:2 * k + 2, :].rearrange("p e h -> p (e h)"), xg), stage, b, f"h{k}")
                            u = banks.take(pe, stage, b, f"gate{k}")
                            banks.fill(one(u, sel[:, k, :], gT[:, 4 * b:4 * b + 4, :].rearrange("p b q -> p (b q)")), stage, b, f"gate{k}")
                        else:
                            banks.fill(one(u[0:64, :], ws1[:, :], xg), stage, b, f"h{k}")
                elif stage == "f3_down":
                    pe.wait_ge(sem("h3_gated"), 4 * (b + 1))
                    pe.wait_ge(sem("h3_ready"), 5 * (b + 1))
                    u = banks.take(pe, stage, b, "o")
                    for j in range(4):
                        o = u[:, j * D:(j + 1) * D]
                        for k in range(4):
                            mm_(o, h3[:, k, j * P:(j + 1) * P], w32[:, k, :], start=(k == 0), stop=False)
                        mm_(o, h3[0:64, 4, j * P:(j + 1) * P], ws2[:, :], start=False, stop=False)
                        last = mm_(o, gT[:, 4 * b + j, :], b32[:, :], start=False, stop=True)
                    banks.fill(last, stage, b, "o")

        @block.scalar
        def _(act_):
            ch = Chain(act_, sem("act_step"))
            A = nc.scalar.activation

            def copy_free(stage, b, name, out, view, signal):
                u = banks.get(act_, stage, b, name)
                ch.do(A(out, view(u), ACT.Copy), banks.freed(stage, b, name))
                ch.sync()
                act_.sem_inc(signal, 1)

            for stage, b in order:
                if stage == "setup":
                    loaded(act_, "x0")
                    ch.do(A(tg[:, :], tg[:, :], ACT.Tanh), sem("tg_ready"))
                    for i in range(2):
                        copy_free(stage, b, f"ctx{i}", cT[:, 4 * i:4 * i + 4, :], lambda u: u.rearrange("p (b q) -> p b q", b=4), sem("wT_ready"))
                    copy_free(stage, b, "gate_w", wifT[:, :, :], lambda u: u[:, 0:6 * H0].rearrange("p (i g) -> p i g", i=3), sem("wT_ready"))
                    copy_free(stage, b, "w1", w1T[:, :, :], lambda u: u[:, 0:2 * D].rearrange("p (i g) -> p i g", i=2), sem("wT_ready"))
                    for i in range(3):
                        copy_free(stage, b, f"l1_{i}", w8T[:, i, :], lambda u: u[:, 0:I1], sem("wT_ready"))
                    copy_free(stage, b, "router", routerT[:, :], lambda u: u[:, 0:NE], sem("wT_ready"))
                elif stage in ("x0_z", "f0_z", "x1_z", "f1_z", "x2_z", "f2_z", "x3_z", "f3_z"):
                    copy_free(stage, b, "u", zT[:, b, :], lambda u: u[:, 0:P], sem(stage[:2] + "_zT"))
                    if stage in ("f0_z", "f2_z"):
                        ch.do(A(zTh[:, b, :], zT[:, b, :], ACT.Copy), sem("zTh_ready"))
                elif stage == "x0_forget":
                    act_.wait_ge(sem("abs_f"), 1)
                    ch.do(A(ga[:, :, :], ga[:, :, :], ACT.Exp, scale=-1.0))
                    ch.sync()
                    ch.do(A(gb[:, :, :], ga[:, :, :], ACT.Ln, bias=1.0), sem("softplus"))
                    act_.wait_ge(sem("md_ready"), 1)
                    ch.do(A(floor[:, :, :], gb[:, :, :], ACT.Exp, scale=-1.0), sem("floor_ready"))
                elif stage == "x0_stack":
                    if b >= 2:
                        act_.wait_ge(sem("cc_ready"), 2 * (b - 1))
                    copy_free(stage, b, "qk", qk0[:, b % 2, :, :], lambda u: as16(u).rearrange("p (s q) -> p s q", s=8), sem("qk0_T"))
                    act_.sem_inc(sem("x0_stacked"), 1)
                    copy_free(stage, b, "am", am[:, b % 2, :, :], lambda u: as16(u).rearrange("p (s q) -> p s q", s=8), sem("am_T"))
                elif stage == "x0_score":
                    for j in range(2):
                        if b >= 1:
                            act_.wait_ge(sem("cc_ready"), 2 * b + j - 1)
                        u = banks.get(act_, stage, b, f"e{j}")
                        ch.do(A(dec[:, j, :, :], u.rearrange("p (h q) -> p h q", h=4), ACT.Exp), banks.freed(stage, b, f"e{j}"))
                        ch.sync()
                        act_.sem_inc(sem("dec_ready"), 1)
                elif stage in ("f0_route", "f2_route", "f3_route"):
                    n = {"f0_route": 1, "f2_route": 2, "f3_route": 3}[stage]
                    act_.wait_ge(sem("logit_ready"), n)
                    ch.do(A(pr[:, :, :], lg[:, :, :], ACT.Exp, scale=-1.0 if n == 3 else 1.0), sem("route_exp"))
                    if n == 3:
                        for g in range(2):
                            copy_free(stage, 0, f"gt{g}", gT[:, 4 * g:4 * g + 4, :], lambda u: u[0:NE, :].rearrange("p (b q) -> p b q", b=4), sem("gT_ready"))
                elif stage in ("f0_up", "f2_up"):
                    e, g = b
                    n = (0 if stage == "f0_up" else NE * FPS) + e * FPS + g
                    for k in range(2):
                        if n >= 2:
                            act_.wait_ge(sem("hid_ready"), 2 * (n - 2) + k + 1)
                        u = banks.get(act_, stage, b, f"a{k}")
                        ch.do(A(act[:, n % 2, k, :], u, ACT.Gelu if stage == "f0_up" else ACT.Silu),
                              banks.freed(stage, b, f"a{k}"))
                        ch.sync()
                        act_.sem_inc(sem("act_ready"), 1)
                elif stage == "f1_mid":
                    act_.wait_ge(sem("gateq_ready"), 1)
                    ch.do(A(sg[:, :, :], gt[:, :, :], ACT.Sigmoid), sem("sig_ready"))
                elif stage in ("a_stack", "b_stack", "c_stack"):
                    copy_free(stage, b, "qk", qkT[:, b, :, :], lambda u: as16(u).rearrange("p (s q) -> p s q", s=8), sem(stage[0] + "_qkT"))
                elif stage in ("a_again", "b_again", "c_again"):
                    copy_free(stage, b, "q", q2T[:, b, :, :], lambda u: as16(u)[:, 0:4 * P].rearrange("p (s q) -> p s q", s=4), sem(stage[0] + "_q2T"))
                elif stage in ("a_exp", "b_exp", "c_exp"):
                    m = stage[0]
                    n = pt_turn[m, b]
                    if n >= 2:
                        act_.wait_ge(sem("pt_used"), n - 1)
                    scale = {"a": P ** -0.5, "b": P ** -0.5, "c": DA ** -0.5}[m]
                    for j in range(4):
                        u = banks.get(act_, stage, b, f"t{j}")
                        ch.do(A(pt[:, n % 2, :, :].rearrange("p (i g) q -> p g i q", g=4)[:, j], u.rearrange("p (h q) -> p h q", h=4), ACT.Exp, scale=scale), banks.freed(stage, b, f"t{j}"))
                        ch.sync()
                        act_.sem_inc(sem("pt_ready"), 1)
                elif stage in ("a_wo", "b_wo", "c_wo"):
                    copy_free(stage, b, "t", atT[:, 0, :], lambda u: u[:, 0:P], sem(stage[0] + "_atT"))
                elif stage == "b_q":
                    copy_free(stage, b, "t", atT[:, 0, :], lambda u: u[:, 0:P], sem("bq_T"))
                elif stage == "b_f":
                    copy_free(stage, b, "t", atT[:, 0, :], lambda u: u[:, 0:P], sem("bf_T"))
                elif stage == "f3_up":
                    for k in range(5):
                        if b:
                            act_.wait_ge(sem("f3_stored"), 1)
                        u = banks.get(act_, stage, b, f"h{k}")
                        r = P if k < 4 else 64
                        bias = b31[:, k:k + 1] if k < 4 else bs1[:, :]
                        ch.do(A(h3[0:r, k, :], u[0:r, :], ACT.Gelu, bias=bias), banks.freed(stage, b, f"h{k}"))
                        ch.sync()
                        act_.sem_inc(sem("h3_ready"), 1)

        @block.vector
        def _(dve):
            ch = Chain(dve, sem("dve_step"))
            v = nc.vector
            tt, ts, stt = v.tensor_tensor, v.tensor_scalar, v.scalar_tensor_tensor

            def free_of(*key):
                return banks.freed(*key)

            def get(stage, b, name):
                return banks.get(dve, stage, b, name)

            def norm_stats(src, b):
                ch.do(v.bn_stats(stats[:, b, :], src))
                ch.sync()
                ch.do(v.bn_aggr(mv[:, b, :], stats[:, b, :]), sem("stats_ready"))

            def normalise(turn, out, src, b, signal):
                dve.wait_ge(sem("stats_ready"), turn)
                dve.wait_ge(sem("rstd_ready"), turn)
                ch.do(ts(out, src, mv[:, b, 0:1], rstd[:, b:b + 1], ALU.subtract, ALU.mult), signal)

            def split_q(m, b, src, i):
                st = (qs, ks)[i][:, b, :, :]
                src = src.rearrange("p (h d) -> p h d", h=HA)
                lo = 2 if i == 0 else 1
                hi2 = 1 if i == 0 else 2
                ch.do(v.tensor_copy(st[:, :, 0:DA], src))
                ch.do(v.tensor_copy(st[:, :, hi2 * DA:(hi2 + 1) * DA], src))
                ch.sync()
                ch.do(tt(st[:, :, lo * DA:(lo + 1) * DA], src, st[:, :, 0:DA], ALU.subtract))

            def pick(i, probs):
                ch.sync()
                ch.do(v.tensor_reduce(top[:, :, 0], probs, AX.X, ALU.max))
                ch.sync()
                ch.do(tt(eq[:, :, :], probs, bc(top[:, :, :], [P, NB, NE]), ALU.is_equal))
                ch.sync()
                ch.do(tt(eq[:, :, :], eq[:, :, :], rank[:, :, :], ALU.mult))
                ch.sync()
                ch.do(v.tensor_reduce(top[:, :, 0], eq[:, :, :], AX.X, ALU.max))
                ch.sync()
                ch.do(tt(oh[:, i, :, :], eq[:, :, :], bc(top[:, :, :], [P, NB, NE]), ALU.is_equal),
                      sem("oh_ready") if i else None)

            def top2():
                pick(0, pr[:, :, :])
                ch.sync()
                ch.do(ts(p2[:, :, :], oh[:, 0, :, :], -3.0e38, None, ALU.mult))
                ch.sync()
                ch.do(tt(p2[:, :, :], p2[:, :, :], pr[:, :, :], ALU.add))
                pick(1, p2[:, :, :])

            def global_scale(n, unit, cols, stage):
                u = get(stage, 0, unit + "_t")
                ch.do(v.tensor_reduce(m1[0:cols, 0:1], u[0:cols, 0:P], AX.X, ALU.max), free_of(stage, 0, unit + "_t"))
                ch.sync()
                if cols == 2:
                    ch.do(ts(m1b[0:2, 0:2], ident[0:2, 0:2], m1[0:2, 0:1], None, ALU.mult), sem("m1_ready"))
                else:
                    ch.do(v.tensor_copy(m1b[0:1, 0:1], m1[0:1, 0:1]), sem("m1_ready"))
                u = get(stage, 0, unit + "_b")
                ch.do(ts(sc[:, 0:cols], u[:, 0:cols], 1.0 / QMAX, 1e-12, ALU.mult, ALU.max), free_of(stage, 0, unit + "_b"))
                ch.sync()
                ch.do(v.reciprocal(sc[:, 4:4 + cols], sc[:, 0:cols]))
                ch.sync()

            def quantise(out, src, col, signal=None, lo=-QMAX - 1.0, hi=QMAX):
                ch.do(ts(out, src, sc[:, 4 + col:5 + col], MAGIC, ALU.mult, ALU.add))
                ch.sync()
                ch.do(ts(out, out, MAGIC + hi, MAGIC + lo, ALU.min, ALU.max))
                ch.sync()
                ch.do(ts(out, out, -MAGIC, sc[:, col:col + 1], ALU.add, ALU.mult), signal)

            for stage, b in order:
                if stage == "setup":
                    dve.wait_ge(sem("wT_ready"), 2)
                    ch.do(v.tensor_reduce(cmean[:, :], cT[:, :, :], AX.X, ALU.add))
                    ch.sync()
                    ch.do(ts(cmean[:, :], cmean[:, :], 1.0 / P, None, ALU.mult))
                    ch.sync()
                    ch.do(v.tensor_copy(cmeanB[:, :, :], bc(cmean[:, :].unsqueeze(2), [P, NB, P])), sem("cmean_ready"))
                    loaded(dve, "l1")
                    blocks = wq8[:, :, :, :].rearrange("p i c (n k) -> p i (c n) k", k=32)
                    for i in range(3):
                        ch.do(v.tensor_reduce(w8s[:, i, :], blocks[:, i, :, :], AX.X, ALU.max, apply_absolute_value=True))
                        ch.sync()
                        ch.do(ts(w8s[:, i, :], w8s[:, i, :], 1.0 / QMAX4, 1e-12, ALU.mult, ALU.max))
                        ch.sync()
                        ch.do(v.reciprocal(w8r[:, i, :], w8s[:, i, :]))
                        ch.sync()
                        w = blocks[:, i, :, :]
                        ch.do(tt(w, w, bc(w8r[:, i, :].unsqueeze(2), [P, 12, 32]), ALU.mult))
                        ch.sync()
                        ch.do(ts(w, w, MAGIC, MAGIC + QMAX4, ALU.add, ALU.min))
                        ch.sync()
                        ch.do(ts(w, w, MAGIC - QMAX4 - 1.0, -MAGIC, ALU.max, ALU.add))
                        ch.sync()
                        ch.do(tt(w, w, bc(w8s[:, i, :].unsqueeze(2), [P, 12, 32]), ALU.mult), sem("w8_ready"))
                elif stage in ("x0_norm", "f0_norm", "x1_norm", "f1_norm", "x2_norm", "f2_norm", "x3_norm", "f3_norm"):
                    if stage == "x0_norm":
                        loaded(dve, "x")
                    norm_stats(x[:, b, :], b)
                elif stage in ("x0_z", "f0_z", "x1_z", "f1_z", "x2_z", "f2_z", "x3_z", "f3_z"):
                    normalise(norm_turn[stage[:2] + "_norm", b], z[:, b, :], x[:, b, :], b, sem("z_ready"))
                elif stage == "x0_forget":
                    u = get("x0_gate", 0, "gates")[:, 0:2 * NB * H0].rearrange("p (b g) -> p b g", b=NB)
                    loaded(dve, "x0")
                    ch.do(tt(gi[:, :, :], u[:, :, 0:H0], bc(ifb[:, 0:H0].unsqueeze(1), [P, NB, H0]), ALU.add))
                    ch.do(tt(gf[:, :, :], u[:, :, H0:2 * H0], bc(ifb[:, H0:2 * H0].unsqueeze(1), [P, NB, H0]), ALU.add),
                          free_of("x0_gate", 0, "gates"))
                    ch.sync()
                    ch.do(stt(ga[:, :, :], gf[:, :, :], -1.0, gf[:, :, :], ALU.mult, ALU.max), sem("abs_f"))
                    dve.wait_ge(sem("softplus"), 1)
                    ch.do(stt(gf[:, :, :], gf[:, :, :], 0.0, gb[:, :, :], ALU.min, ALU.subtract), sem("log_forget"))
                    u = get(stage, 0, "csum")[:, 0:NB * H0].rearrange("p (b h) -> p b h", b=NB)
                    ch.do(v.tensor_copy(cs[:, :, :], u))
                    ch.do(tt(ga[:, :, :], gi[:, :, :], u, ALU.subtract), free_of(stage, 0, "csum"))
                    ch.sync()
                    dve.sem_inc(sem("a_ready"), 1)
                    u = get(stage, 0, "at")
                    ch.do(v.tensor_copy(aT[:, :], u[0:NB * H0, 0:P]), free_of(stage, 0, "at"))
                    ch.sync()
                    ch.do(v.tensor_tensor_scan(mT[:, :], aT[:, :], aT[:, :], -3.0e38, ALU.max, ALU.max), sem("mT_ready"))
                    u = get(stage, 0, "m")[:, 0:NB * H0].rearrange("p (b h) -> p b h", b=NB)
                    ch.do(ts(mm[:, :, :], u, -1.0, None, ALU.mult))
                    ch.do(tt(gb[:, :, :], cs[:, :, :], u, ALU.add), free_of(stage, 0, "m"))
                    ch.sync()
                    dve.sem_inc(sem("md_ready"), 1)
                    dve.wait_ge(sem("const_ready"), 1)
                    for src, st, o in ((ga, ast, 0), (mm, mst, 3)):
                        s2 = src[:, :, :].rearrange("p b h -> p (b h)")
                        ch.do(v.tensor_copy(st[:, :, o], s2))
                        ch.sync()
                        ch.do(tt(s2, s2, st[:, :, o], ALU.subtract))
                        ch.sync()
                        ch.do(v.tensor_copy(st[:, :, o + 1], s2))
                        ch.sync()
                        ch.do(tt(st[:, :, o + 2], s2, st[:, :, o + 1], ALU.subtract), sem("am_ready") if o else None)
                elif stage == "x0_stack":
                    if b >= 2:
                        dve.wait_ge(sem("x0_stacked"), b - 1)
                    qq = q0[:, b % 2, :, :]
                    zb = z[:, b, :].rearrange("p (h d) -> p h d", h=H0)
                    ch.do(v.tensor_copy(qq[:, :, 0:D0], zb))
                    ch.do(v.tensor_copy(qq[:, :, D0:2 * D0], zb))
                    ch.sync()
                    ch.do(tt(qq[:, :, 2 * D0:3 * D0], zb, qq[:, :, 0:D0], ALU.subtract), sem("q0_ready"))
                elif stage == "x0_score":
                    if b >= 2:
                        dve.wait_ge(sem("cc_used"), b - 1)
                    for j in range(2):
                        dve.wait_ge(sem("dec_ready"), 2 * b + j + 1)
                        u = get(stage, b, f"s{j}").rearrange("p (h q) -> p h q", h=4)
                        ch.do(stt(cc[:, b % 2, :, :].rearrange("p (i g) q -> p g i q", g=2)[:, j], u, D0 ** -0.5, dec[:, j, :, :], ALU.mult, ALU.mult),
                              free_of(stage, b, f"s{j}"))
                        ch.sync()
                        dve.sem_inc(sem("cc_ready"), 1)
                elif stage == "x0_value":
                    u = get(stage, b, "u")[:, 0:H0 * (D0 + 1)].rearrange("p (h d) -> p h d", h=H0)
                    dve.sem_inc(sem("cc_used"), 1)
                    if b == 0:
                        dve.wait_ge(sem("floor_ready"), 1)
                    ch.do(v.tensor_reduce(nrm[:, :], u[:, :, D0:D0 + 1], AX.X, ALU.max, apply_absolute_value=True))
                    ch.sync()
                    ch.do(tt(nrm[:, :], nrm[:, :], floor[:, b, :], ALU.max))
                    ch.sync()
                    ch.do(ts(nrm[:, :], nrm[:, :], 1e-6, None, ALU.add))
                    ch.sync()
                    ch.do(v.reciprocal(nrm[:, :], nrm[:, :]))
                    ch.sync()
                    h3d = hh[:, b, :].rearrange("p (h d) -> p h d", h=H0)
                    ch.do(tt(h3d, u[:, :, 0:D0], bc(nrm[:, :].unsqueeze(2), [P, H0, D0]), ALU.mult), free_of(stage, b, "u"))
                    ch.sync()
                    ch.do(v.tensor_reduce(hm[:, :], h3d, AX.X, ALU.add))
                    ch.sync()
                    ch.do(ts(hm[:, :], hm[:, :], 1.0 / D0, None, ALU.mult))
                    ch.sync()
                    ch.do(tt(h3d, h3d, bc(hm[:, :].unsqueeze(2), [P, H0, D0]), ALU.subtract))
                    ch.sync()
                    ch.do(tt(sq[:, :], hh[:, b, :], hh[:, b, :], ALU.mult))
                    ch.sync()
                    ch.do(v.tensor_reduce(hv[:, b, :], sq[:, :].rearrange("p (h d) -> p h d", h=H0), AX.X, ALU.add))
                    ch.sync()
                    ch.do(ts(hv[:, b, :], hv[:, b, :], 1.0 / D0, 1e-5, ALU.mult, ALU.add), sem("hv_ready"))
                elif stage == "x0_group":
                    if b == 0:
                        loaded(dve, "rows")
                        dve.wait_ge(sem("tg_ready"), 1)
                    dve.wait_ge(sem("hr_ready"), b + 1)
                    h3d = hh[:, b, :].rearrange("p (h d) -> p h d", h=H0)
                    ch.do(tt(h3d, h3d, bc(hr[:, b, :].unsqueeze(2), [P, H0, D0]), ALU.mult))
                    ch.sync()
                    ch.do(tt(hh[:, b, :], hh[:, b, :], vec("L0_xattn_gn_w"), ALU.mult))
                    ch.sync()
                    ch.do(tt(hh[:, b, :], hh[:, b, :], vec("L0_xattn_gn_b"), ALU.add))
                    ch.sync()
                    ch.do(stt(x[:, b, :], hh[:, b, :], tg[:, 0:1], x[:, b, :], ALU.mult, ALU.add))
                    ch.sync()
                elif stage in ("f0_route", "f2_route", "f3_route"):
                    n = {"f0_route": 1, "f2_route": 2, "f3_route": 3}[stage]
                    name = "u" if n == 2 else "logit"
                    u = get(stage, 0, name)[:, 0:NB * NE].rearrange("p (b e) -> p b e", b=NB)
                    if n < 3:
                        ch.do(v.tensor_reduce(top[:, :, 0], u, AX.X, ALU.max))
                        ch.sync()
                        ch.do(tt(lg[:, :, :], u, bc(top[:, :, :], [P, NB, NE]), ALU.subtract), free_of(stage, 0, name))
                    else:
                        ch.do(v.tensor_copy(lg[:, :, :], u), free_of(stage, 0, name))
                    ch.sync()
                    dve.sem_inc(sem("logit_ready"), 1)
                    dve.wait_ge(sem("route_exp"), n)
                    if n < 3:
                        ch.do(v.tensor_reduce(gsum[:, :, 0], pr[:, :, :], AX.X, ALU.add))
                        ch.sync()
                        ch.do(v.reciprocal(gsum[:, :, :], gsum[:, :, :]))
                        ch.sync()
                        ch.do(tt(pr[:, :, :], pr[:, :, :], bc(gsum[:, :, :], [P, NB, NE]), ALU.mult))
                    else:
                        loaded(dve, "l3")
                        ch.do(ts(pr[:, :, :], pr[:, :, :], 1.0, None, ALU.add))
                        ch.sync()
                        ch.do(v.reciprocal(pr[:, :, :], pr[:, :, :]))
                        ch.sync()
                        ch.do(ts(pr[:, :, :], pr[:, :, :], rscale[:, 0:1], None, ALU.mult))
                    top2()
                    if n == 1:
                        u = get(stage, 0, "cum")[:, 0:2 * NB * NE].rearrange("p (k b e) -> p k b e", k=2, b=NB)
                        w = get(stage, 0, "total")[:, 0:2 * NB * NE].rearrange("p (k b e) -> p k b e", k=2, b=NB)
                        for k in range(2):
                            ch.do(v.tensor_copy(tot[:, k * NE:(k + 1) * NE, :], w[:, k, :, :].rearrange("p b e -> p e b")),
                                  free_of(stage, 0, "total") if k else None)
                            ch.do(v.tensor_copy(cum[:, k, :, :], u[:, k, :, :]), free_of(stage, 0, "cum") if k else None)
                        ch.sync()
                        dve.wait_ge(*free_of(stage, 0, "total"))
                        ch.do(v.tensor_tensor_scan(inc[:, :, :].rearrange("p e b -> p (e b)"), reset[:, :, :].rearrange("p e b -> p (e b)"),
                                                   tot[:, :, :].rearrange("p e b -> p (e b)"), 0.0, ALU.mult, ALU.add))
                        ch.sync()
                        ch.do(tt(tot[:, :, :], inc[:, :, :], tot[:, :, :], ALU.subtract))
                        ch.sync()
                        ch.do(tt(tot[:, NE:2 * NE, :], tot[:, NE:2 * NE, :], bc(inc[:, 0:NE, NB - 1:NB], [P, NE, NB]), ALU.add))
                        ch.sync()
                        for k in range(2):
                            ch.do(tt(cum[:, k, :, :], cum[:, k, :, :], tot[:, k * NE:(k + 1) * NE, :].rearrange("p e b -> p b e"), ALU.add))
                        ch.sync()
                        ch.do(stt(oh[:, :, :, :].rearrange("p k b e -> p (k b e)"), cum[:, :, :, :].rearrange("p k b e -> p (k b e)"),
                                  CAP + 0.5, oh[:, :, :, :].rearrange("p k b e -> p (k b e)"), ALU.is_lt, ALU.mult))
                    ch.sync()
                    ch.do(tt(gate[:, :, :], oh[:, 0, :, :], oh[:, 1, :, :], ALU.add))
                    ch.sync()
                    ch.do(tt(gate[:, :, :], gate[:, :, :], pr[:, :, :], ALU.mult))
                    ch.sync()
                    ch.do(v.tensor_reduce(gsum[:, :, 0], gate[:, :, :], AX.X, ALU.add))
                    ch.sync()
                    if n == 1:
                        ch.do(ts(gsum[:, :, :], gsum[:, :, :], 1e-9, None, ALU.max))
                    elif n == 2:
                        ch.do(ts(gsum[:, :, :], gsum[:, :, :], 1e-6, None, ALU.add))
                    ch.sync()
                    ch.do(v.reciprocal(gsum[:, :, :], gsum[:, :, :]))
                    ch.sync()
                    ch.do(tt(gate[:, :, :], gate[:, :, :], bc(gsum[:, :, :], [P, NB, NE]), ALU.mult), sem("gate_ready"))
                elif stage in ("f0_up", "f2_up"):
                    e, g = b
                    n = (0 if stage == "f0_up" else NE * FPS) + e * FPS + g
                    for k in range(2):
                        dve.wait_ge(sem("act_ready"), 2 * n + k + 1)
                        if n >= 2:
                            dve.wait_ge(sem("hid_used"), n - 1)
                        u = get(stage, b, f"g{k}")
                        ch.do(tt(hid[:, n % 2, k, :], act[:, n % 2, k, :], u, ALU.mult), free_of(stage, b, f"g{k}"))
                        ch.sync()
                        dve.sem_inc(sem("hid_ready"), 1)
                elif stage in ("f0_down", "f2_down"):
                    e, g = b
                    u = get(stage, b, "u")
                    dve.sem_inc(sem("hid_used"), 1)
                    for j in range(4):
                        bb = 4 * g + j
                        s = gate[:, bb, e:e + 1]
                        ps = u[:, j * D:(j + 1) * D]
                        fr = free_of(stage, b, "u") if j == 3 else None
                        if e == 0:
                            ch.do(ts(acc[:, bb, :], ps, s, None, ALU.mult), fr)
                        else:
                            ch.do(stt(acc[:, bb, :], ps, s, acc[:, bb, :], ALU.mult, ALU.add), fr)
                    ch.sync()
                    if e == NE - 1:
                        k = 4 if stage == "f0_down" else 6
                        ch.do(stt(x[:, 4 * g:4 * g + 4, :], acc[:, 4 * g:4 * g + 4, :], tg[:, k:k + 1], x[:, 4 * g:4 * g + 4, :], ALU.mult, ALU.add))
                        ch.sync()
                elif stage == "x1_out":
                    u = get(stage, b, "u")
                    ch.do(tt(t1[:, b, :], u[:, 0:D], vec("L1_xattn_b"), ALU.add), free_of(stage, b, "u"))
                    ch.sync()
                    ch.do(stt(x[:, b, :], t1[:, b, :], tg[:, 1:2], x[:, b, :], ALU.mult, ALU.add))
                    ch.sync()
                elif stage == "f1_scale":
                    ch.sync()
                    ch.do(v.tensor_reduce(mx[:, 0:1], z[:, :, :].rearrange("p b d -> p (b d)"), AX.X, ALU.max, apply_absolute_value=True), sem("mx_ready"))
                    global_scale(0, "x", 1, stage)
                    dve.wait_ge(sem("f1_zT"), NB)
                    quantise(xq[:, :], zT[:, :, :].rearrange("p b q -> p (b q)"), 0, sem("xq_ready"))
                elif stage == "f1_up":
                    cch, g = b
                    ch.do(v.tensor_copy(up[:, cch, g * BANK:(g + 1) * BANK], get(stage, b, "up")), free_of(stage, b, "up"))
                    ch.do(v.tensor_copy(gt[:, cch, g * BANK:(g + 1) * BANK], get(stage, b, "gate")), free_of(stage, b, "gate"))
                elif stage == "f1_mid":
                    ch.sync()
                    flat = [s[:, :, :].rearrange("p c q -> p (c q)") for s in (up, gt, sg)]
                    u_, g_, s_ = flat
                    ch.do(v.tensor_reduce(mx[:, 0:1], u_, AX.X, ALU.max, apply_absolute_value=True))
                    ch.do(v.tensor_reduce(mx[:, 1:2], g_, AX.X, ALU.max, apply_absolute_value=True), sem("mx_ready"))
                    global_scale(1, "ug", 2, stage)
                    quantise(g_, g_, 1, sem("gateq_ready"))
                    quantise(u_, u_, 0)
                    dve.wait_ge(sem("sig_ready"), 1)
                    ch.do(ts(s_, s_, 65536.0, MAGIC, ALU.mult, ALU.add))
                    ch.sync()
                    ch.do(ts(s_, s_, MAGIC + 65535.0, MAGIC, ALU.min, ALU.max))
                    ch.sync()
                    ch.do(ts(s_, s_, -MAGIC, 1.0 / 65536.0, ALU.add, ALU.mult))
                    ch.sync()
                    ch.do(tt(g_, g_, s_, ALU.mult))
                    ch.sync()
                    ch.do(v.tensor_reduce(mx[:, 0:1], g_, AX.X, ALU.max, apply_absolute_value=True), sem("mx_ready"))
                    global_scale(2, "gs", 1, stage)
                    quantise(g_, g_, 0)
                    ch.sync()
                    ch.do(tt(s_, g_, u_, ALU.mult))
                    ch.sync()
                    ch.do(v.tensor_reduce(mx[:, 0:1], s_, AX.X, ALU.max, apply_absolute_value=True), sem("mx_ready"))
                    global_scale(3, "o", 1, stage)
                    quantise(s_, s_, 0, sem("o_ready"))
                elif stage == "f1_down":
                    u = get(stage, b, "u")
                    ch.do(stt(x[:, b, :], u[:, 0:D], tg[:, 5:6], x[:, b, :], ALU.mult, ALU.add), free_of(stage, b, "u"))
                    ch.sync()
                elif stage in ("a_kv", "b_kv", "c_kv"):
                    m = stage[0]
                    if m == "a" and b == 0:
                        dve.wait_ge(sem("v9_ones"), 1)
                    u = get(stage, b, "qkv")
                    f = free_of(stage, b, "qkv")
                    if m == "c":
                        w = q32[:, b % 2, :, :]
                        ch.do(tt(w, u[:, 0:3 * D].rearrange("p (i d) -> p i d", i=3), bqkv[:, :, :], ALU.add), f)
                        ch.sync()
                        q_, k_, v_ = (w[:, i, :] for i in range(3))
                        split_q(m, b, q_, 0)
                        split_q(m, b, k_, 1)
                        ch.do(v.tensor_copy(v9[:, b, :, 0:DA], v_.rearrange("p (h d) -> p h d", h=HA)), sem("c_stacks"))
                    else:
                        q_, k_, v_ = (u[:, i * D:(i + 1) * D] for i in range(3))
                        if m == "a":
                            split_q(m, b, q_, 0)
                        split_q(m, b, k_, 1)
                        ch.do(v.tensor_copy(v9[:, b, :, 0:DA], v_.rearrange("p (h d) -> p h d", h=HA)), f)
                        ch.sync()
                        dve.sem_inc(sem(m + "_stacks"), 1)
                elif stage == "b_q":
                    u = get(stage, b, "q")
                    split_q("b", b, u[:, 0:D], 0)
                    ch.sync()
                    dve.sem_inc(free_of(stage, b, "q")[0], 1)
                elif stage in ("a_max", "b_max", "c_max"):
                    m = stage[0]
                    for j in range(4):
                        u = get(stage, b, f"s{j}").rearrange("p (h k) -> p h k", h=4)
                        ch.do(v.tensor_reduce(nmax[:, b, :].rearrange("p (i g) -> p g i", g=4)[:, j], u, AX.X, ALU.max, negate=True), free_of(stage, b, f"s{j}"))
                    ch.sync()
                    for j in range(3):
                        dve.wait_ge(*free_of(stage, b, f"s{j}"))
                    ch.do(v.tensor_copy(qs[:, b, :, 3 * DA], nmax[:, b, :]))
                    ch.sync()
                    ch.do(tt(qs[:, b, :, 3 * DA + 1], nmax[:, b, :], qs[:, b, :, 3 * DA], ALU.subtract), sem(m + "_negmax"))
                elif stage in ("a_av", "b_av", "c_av"):
                    m = stage[0]
                    u = get(stage, b, "av")[:, 0:HA * (DA + 1)].rearrange("p (h d) -> p h d", h=HA)
                    dve.sem_inc(sem("pt_used"), 1)
                    ch.do(v.reciprocal(rden[:, :], u[:, :, DA]))
                    ch.sync()
                    ch.do(tt(at[:, b, :].rearrange("p (h d) -> p h d", h=HA), u[:, :, 0:DA], bc(rden[:, :].unsqueeze(2), [P, HA, DA]), ALU.mult),
                          free_of(stage, b, "av"))
                    ch.sync()
                    dve.sem_inc(sem(m + "_at"), 1)
                elif stage in ("a_wo", "b_wo"):
                    m = stage[0]
                    u = get(stage, b, "wo")
                    ch.do(tt(t2[:, b, :], u[:, 0:D], vec("L2_xattn_bo1" if m == "a" else "L2_xattn_bo2"), ALU.add), free_of(stage, b, "wo"))
                    ch.sync()
                    if m == "a":
                        ch.do(stt(t2[:, b, :], t2[:, b, :], 0.0, z[:, b, :], ALU.max, ALU.add))
                    else:
                        ch.do(ts(t2[:, b, :], t2[:, b, :], 0.0, 2.0, ALU.max, ALU.mult))
                    ch.sync()
                elif stage in ("a_norm", "b_norm"):
                    m = stage[0]
                    norm_stats(t2[:, b, :], b)
                    normalise(norm_turn[stage, b], t1[:, b, :], t2[:, b, :], b, None)
                    ch.sync()
                    g_, b_ = ("L2_xattn_g1", "L2_xattn_b1") if m == "a" else ("L2_xattn_g2", "L2_xattn_b2")
                    ch.do(tt(t1[:, b, :], t1[:, b, :], vec(g_), ALU.mult))
                    ch.sync()
                    ch.do(tt(t1[:, b, :], t1[:, b, :], vec(b_), ALU.add), sem(m + "_out"))
                elif stage == "b_f":
                    u = get(stage, b, "f")
                    ch.do(tt(t2[:, b, :], u[:, 0:D], vec("L2_xattn_bf"), ALU.add), free_of(stage, b, "f"))
                    ch.sync()
                    ch.do(stt(t2[:, b, :], t2[:, b, :], 0.0, t1[:, b, :], ALU.max, ALU.add))
                    ch.sync()
                elif stage == "b_last":
                    norm_stats(t2[:, b, :], b)
                    normalise(norm_turn[stage, b], t1[:, b, :], t2[:, b, :], b, None)
                    ch.sync()
                    ch.do(tt(t1[:, b, :], t1[:, b, :], vec("L2_xattn_g3"), ALU.mult))
                    ch.sync()
                    ch.do(tt(t1[:, b, :], t1[:, b, :], vec("L2_xattn_b3"), ALU.add))
                    ch.sync()
                    ch.do(stt(x[:, b, :], t1[:, b, :], tg[:, 2:3], x[:, b, :], ALU.mult, ALU.add))
                    ch.sync()
                elif stage == "c_wo":
                    u = get(stage, b, "wo")
                    ch.do(tt(t2[:, b, :], u[:, 0:D], vec("L3_xattn_bo"), ALU.add), free_of(stage, b, "wo"))
                    ch.sync()
                    ch.do(stt(x[:, b, :], t2[:, b, :], tg[:, 3:4], x[:, b, :], ALU.mult, ALU.add))
                    ch.sync()
                elif stage == "f3_up":
                    for k in range(4):
                        dve.wait_ge(sem("h3_ready"), 5 * b + k + 1)
                        u = get(stage, b, f"gate{k}")
                        ch.do(tt(h3[:, k, :], h3[:, k, :], u, ALU.mult), free_of(stage, b, f"gate{k}"))
                        ch.sync()
                        dve.sem_inc(sem("h3_gated"), 1)
                elif stage == "f3_down":
                    u = get(stage, b, "o").rearrange("p (j d) -> p j d", j=4)
                    dve.sem_inc(sem("f3_stored"), 1)
                    ch.do(tt(t2[:, 4 * b:4 * b + 4, :], u, bc(vec("L3_ffn_bs2").unsqueeze(1), [P, 4, D]), ALU.add), free_of(stage, b, "o"))
                    ch.sync()
                    for j in range(4):
                        bb = 4 * b + j
                        ch.do(stt(x[:, bb, :], t2[:, bb, :], tg[:, 7:8], x[:, bb, :], ALU.mult, ALU.add), sem("x_final"))


_INS = ["x", "ctx_1024", "g_xattn", "g_ffn", "L0_xattn_Wi_w", "L0_xattn_Wi_b", "L0_xattn_Wf_w", "L0_xattn_Wf_b",
        "L0_xattn_gn_w", "L0_xattn_gn_b", "L0_ffn_Wg", "L0_ffn_W_in", "L0_ffn_W_out", "L1_xattn_W", "L1_xattn_b",
        "L1_ffn_w_gate", "L1_ffn_w_up", "L1_ffn_w_down", "L2_xattn_Wk1", "L2_xattn_Wv1", "L2_xattn_Wq1",
        "L2_xattn_Wo1", "L2_xattn_bo1", "L2_xattn_Wk2", "L2_xattn_Wv2", "L2_xattn_Wq2", "L2_xattn_Wo2",
        "L2_xattn_bo2", "L2_xattn_Wf", "L2_xattn_bf", "L2_xattn_g1", "L2_xattn_b1", "L2_xattn_g2", "L2_xattn_b2",
        "L2_xattn_g3", "L2_xattn_b3", "L2_ffn_router_w", "L2_ffn_w13", "L2_ffn_w2", "L3_xattn_Wq", "L3_xattn_bq",
        "L3_xattn_Wk", "L3_xattn_bk", "L3_xattn_Wv", "L3_xattn_bv", "L3_xattn_Wo", "L3_xattn_bo", "L3_ffn_gate_W",
        "L3_ffn_W1", "L3_ffn_b1", "L3_ffn_W2", "L3_ffn_b2", "L3_ffn_Ws1", "L3_ffn_bs1", "L3_ffn_Ws2",
        "L3_ffn_bs2", "L3_ffn_route_scale"]


def kernel(**inputs):
    import numpy as _np
    import concourse.bacc as _bacc
    from concourse import mybir as _mybir
    from concourse.bass_utils import run_bass_kernel_spmd as _run

    nc = _bacc.Bacc("TRN2", target_bir_lowering=False, num_devices=1)
    arrays, tensors = {}, {}
    for name in _INS:
        a = _np.ascontiguousarray(inputs[name])
        if a.ndim == 0:
            a = a.reshape(1)
        arrays[f"in_{name}"] = a
        tensors[name] = nc.dram_tensor(f"in_{name}", a.shape, _mybir.dt.from_np(a.dtype), kind="ExternalInput").ap()
    tensors["out"] = nc.dram_tensor("out", (8, 128, 128), _mybir.dt.float32, kind="ExternalOutput").ap()
    gated_stack(nc, tensors)
    r = _run(nc, [arrays], core_ids=[0])
    return r.results[0]["out"]
```

```python
from contextlib import ExitStack

import concourse.bass as bass
from concourse import mybir

F32 = mybir.dt.float32
F16 = mybir.dt.float16
BF16 = mybir.dt.bfloat16
ALU = mybir.AluOpType
ACT = mybir.ActivationFunctionType
AX = mybir.AxisListType

NB = 8
P = 128
D = 128
NE = 8
F = 256
CAP = 320
I1 = 384
H0, D0 = 8, 16
HA, DA = 16, 8
SLOT0, SLOTA = 64, 32
PSUM_BANKS, BANK = 8, 512
MASKED = -1.0e30
MAGIC = 12582912.0
QMAX = 32767.0
QMAX4 = 7.0
FPS = 2
HALF = 4


NORMS = {"x0_norm": 1e-5, "x0_group": 1e-5, "x1_norm": 1e-5, "x1_out": 1e-5, "f1_down": 1e-5, "a_wo": 1e-6,
         "b_wo": 1e-6, "b_f": 1e-6, "b_last": 1e-5, "x3_norm": 1e-5, "c_wo": 1e-5}
NORM_OF = {"x0_z": "x0_norm", "f0_z": "x0_group", "x1_z": "x1_norm", "f1_z": "x1_out", "x2_z": "f1_down",
           "a_norm": "a_wo", "b_norm": "b_wo", "b_last": "b_f", "f2_z": "b_last", "x3_z": "x3_norm", "f3_z": "c_wo"}
Z_STAGES = ("x0_z", "f0_z", "x1_z", "f1_z", "x2_z", "f2_z", "x3_z", "f3_z")
T_STAGES = tuple(s[:2] + "_t" for s in Z_STAGES)


def schedule():
    out = [("setup", 0)]

    def skew(names, items, forward=False, extra=()):
        extra = list(extra)
        for t in range(len(items) + len(names) - 1):
            for s in range(len(names)) if forward else reversed(range(len(names))):
                if 0 <= t - s < len(items):
                    out.append((names[s], items[t - s]))
            if extra:
                out.append(extra.pop(0))
        out.extend(extra)

    batches = list(range(NB))
    experts = [(e, g) for e in range(NE) for g in range(FPS)]
    skew(["x0_norm", "x0_z", "x0_t", "x0_gate"], batches)
    out.append(("x0_forget", 0))
    skew(["x0_split", "x0_stack", "x0_score", "x0_value", "x0_group", "f0_z", "f0_t"], batches,
         extra=[("split0", e) for e in range(NE)] + [("w1", 0)] + [("w8", i) for i in range(3)])
    out.append(("f0_route", 0))
    skew(["f0_up", "f0_down"], experts, forward=True, extra=[("router", 0)] + [("split2", e) for e in range(NE)])
    skew(["x1_norm", "x1_z", "x1_t", "x1_out", "f1_z", "f1_t"], batches)
    out.append(("f1_scale", 0))
    skew(["f1_up"], [(c, g) for c in range(3) for g in range(FPS)])
    out.append(("f1_mid", 0))
    att = ["stack", "max", "again", "exp", "av", "wt"]
    skew(["f1_down", "x2_z", "x2_t", "a_kv"] + ["a_" + s for s in att[:-1]] + ["b_kv", "a_wt", "a_wo", "a_norm", "b_qt", "b_q"]
         + ["b_" + s for s in att] + ["b_wo", "b_norm", "b_ft", "b_f", "b_last", "f2_z", "f2_t"], batches)
    out.append(("f2_route", 0))
    skew(["f2_up", "f2_down"], experts, forward=True)
    skew(["x3_norm", "x3_z", "x3_t", "c_kv"] + ["c_" + s for s in att] + ["c_wo", "f3_z", "f3_t"], batches)
    out.append(("f3_route", 0))
    skew(["f3_up", "f3_down"], [0, 1])
    return out


UNITS = {
    "setup": ["ctx0", "ctx1", "gate_w"], "w1": ["u"], "w8": ["u"], "router": ["u"],
    "x0_forget": ["csum", "at", "m"], "x0_stack": ["qk", "am"], "x0_score": ["e0", "e1", "s0", "s1"],
    "x0_value": ["u"], "f0_route": ["logit", "cum", "total"], "x1_out": ["u"], "f1_scale": ["x_t", "x_b"],
    "f1_up": ["up", "gate"], "f1_mid": ["ug_t", "ug_b", "gs_t", "gs_b", "o_t", "o_b"], "f1_down": ["u"],
    "b_qt": ["t"], "b_q": ["q"], "b_ft": ["t"], "b_f": ["f"], "f2_route": ["logit"],
    "f3_route": ["logit", "gt0", "gt1"], "f3_up": ["h0", "gate0", "h1", "gate1", "h2", "gate2", "h3", "gate3", "h4"],
    "f3_down": ["o"],
}
UNITS |= {t: ["u"] for t in T_STAGES}
UNITS |= {f + "_up": ["a0", "g0", "a1", "g1"] for f in ("f0", "f2")} | {f + "_down": ["u"] for f in ("f0", "f2")}
for _m in "abc":
    UNITS |= {_m + "_kv": ["qkv"], _m + "_stack": ["qk"], _m + "_max": [f"s{i}" for i in range(4)],
              _m + "_again": ["q"], _m + "_exp": [f"t{i}" for i in range(4)], _m + "_av": ["av"],
              _m + "_wt": ["t"], _m + "_wo": ["wo"]}


def psum_units(stage, item):
    if stage == "x0_gate":
        return ["gates"] if item == 0 else []
    return UNITS.get(stage, [])


class Banks:

    def __init__(self, order, psum, full, free):
        self.psum, self.full, self.free = psum, full, free
        self.place = {}
        n = 0
        for stage, item in order:
            for name in psum_units(stage, item):
                self.place[stage, item, name] = (n % PSUM_BANKS, n // PSUM_BANKS)
                n += 1

    def tile(self, *key):
        k, _ = self.place[key]
        return self.psum[:, k * BANK:(k + 1) * BANK]

    def take(self, pe, *key):
        k, turn = self.place[key]
        if turn:
            pe.wait_ge(self.free[k], turn)
        return self.psum[:, k * BANK:(k + 1) * BANK]

    def freed(self, *key):
        k, turn = self.place[key]
        return self.free[k], turn + 1

    def fill(self, ins, *key):
        ins.then_inc(self.full[self.place[key][0]], 1)

    def get(self, eng, *key):
        k, turn = self.place[key]
        eng.wait_ge(self.full[k], turn + 1)
        return self.psum[:, k * BANK:(k + 1) * BANK]


class Chain:

    def __init__(self, eng, own):
        self.eng, self.own, self.count, self.last = eng, own, {}, None

    def do(self, ins, sem=None):
        sem = self.own if sem is None else sem
        if isinstance(sem, tuple):
            ins.then_inc(sem[0], 1)
            self.last = sem
            return
        ins.then_inc(sem, 1)
        n = self.count[sem.name] = self.count.get(sem.name, 0) + 1
        self.last = (sem, n)

    def sync(self):
        self.eng.wait_ge(*self.last)


def bc(ap, shape):
    return ap.to_broadcast(list(shape))


def gated_stack(nc, t):
    order = schedule()
    with ExitStack() as ctx:
        def sb(name, shape, dt=F32):
            return ctx.enter_context(nc.sbuf_tensor(name, shape, dt))

        sems = {}

        def sem(name):
            if name not in sems:
                sems[name] = ctx.enter_context(nc.semaphore(name))
            return sems[name]

        x = sb("x", [P, NB, D])
        z = sb("z", [P, NB, D])
        zT = sb("zT", [P, NB, P])
        zTh = sb("zTh", [P, NB, P], F16)
        zTl = sb("zTl", [P, NB, P], F16)
        c = sb("c", [P, NB, D])
        cT = sb("cT", [P, NB, P])
        ident = sb("ident", [P, P])
        ident16 = sb("ident16", [P, P], F16)
        identb = sb("identb", [P, P], BF16)
        ones = sb("ones", [P, P])
        tri = sb("tri", [P, P])
        maskT = sb("maskT", [P, 4, P], BF16)
        maskQ = sb("maskQ", [P, 4, P], BF16)
        mhalf = sb("mhalf", [P, 8])
        reset = sb("reset", [P, 2 * NE, NB])
        rank = sb("rank", [P, NB, NE])
        tg = sb("tg", [P, 8])
        wifT = sb("wifT", [P, 3, 2 * H0])
        ifb = sb("ifb", [P, 2 * H0])
        wg0 = sb("wg0", [P, NE])
        stage_f32 = sb("stage_f32", [P, NE * 2 * F])
        split = {"f0": sb("split0", [P, 2 * NE * 2 * F // 2]), "f2": sb("split2", [P, 2 * NE * 2 * F // 2])}
        phase = sb("phase", [P, 8192])
        work = sb("work", [P, 4096])
        win = stage_f32[:, :].rearrange("p (e f) -> p e f", e=NE)
        winh = {k: t_[:, 0:NE * F].bitcast(F16).rearrange("p (e f) -> p e f", e=NE) for k, t_ in split.items()}
        winl = {k: t_[:, NE * F:2 * NE * F].bitcast(F16).rearrange("p (e f) -> p e f", e=NE) for k, t_ in split.items()}

        def carve(region, *tiles):
            at_, out = 0, []
            for shape, dt in tiles:
                n = 1
                for k in shape:
                    n *= k
                words = n if dt == F32 else n // 2
                v_ = region[:, at_:at_ + words]
                if dt != F32:
                    v_ = v_.bitcast(dt)
                names = " ".join("abcd"[:len(shape)])
                if len(shape) > 1:
                    v_ = v_.rearrange(f"p ({names}) -> p {names}", **{"abcd"[i]: shape[i] for i in range(1, len(shape))})
                out.append(v_)
                at_ += words
            assert at_ <= region.shape[1]
            return out
        wout = {"f0": sb("wout0", [P, NE, 2, D]), "f2": sb("wout2", [P, NE, 2, D])}
        t1 = sb("t1", [P, NB, D])
        t1f = t1[:, :, :].rearrange("p b d -> p (b d)")
        wif = t1f[0:2 * H0, 0:3 * D]
        w1T = sb("w1T", [P, 2, D])
        cmean = sb("cmean", [P, NB])
        cmeanB = sb("cmeanB", [P, NB, P])
        at = sb("at", [P, NB + 1, D])
        wq8 = at[:, :, :].rearrange("p (i c) d -> p i c d", i=3)
        w8T = sb("w8T", [P, 3, I1])
        w8s = sb("w8s", [P, 3, 12])
        w8r = sb("w8r", [P, 3, 12])
        wA = sb("wA", [P, 3, D])
        woA = sb("woA", [P, D])
        wB = sb("wB", [P, 3, D])
        woB = sb("woB", [P, D])
        wf = sb("wf", [P, D])
        router = sb("router", [NE, D])
        routerT = sb("routerT", [P, NE])
        wC = sb("wC", [P, 3, D])
        woC = sb("woC", [P, D])
        wg3 = sb("wg3", [P, NE])
        w31 = sb("w31", [P, NE, 64])
        w32 = sb("w32", [P, 4, D])
        b31 = sb("b31", [P, 4])
        b32 = sb("b32", [NE, D])
        ws1 = sb("ws1", [P, 64])
        ws2 = sb("ws2", [64, D])
        bs1 = sb("bs1", [64, 1])
        rscale = sb("rscale", [P, 1])
        sel = sb("sel", [NE, 4, P])
        vecs = ["L0_xattn_gn_w", "L0_xattn_gn_b", "L1_xattn_b", "L2_xattn_bo1", "L2_xattn_g1",
                "L2_xattn_b1", "L2_xattn_bo2", "L2_xattn_g2", "L2_xattn_b2", "L2_xattn_bf",
                "L2_xattn_g3", "L2_xattn_b3", "L3_xattn_bo", "L3_ffn_bs2"]
        rows = sb("rows", [P, len(vecs), D])
        bqkv = sb("bqkv", [P, 3, D])

        def vec(name):
            return rows[:, vecs.index(name), :]

        stats = sb("stats", [P, NB, 6])
        mv = sb("mv", [P, NB, 2])
        vr = sb("vr", [P, NB])
        rstd = sb("rstd", [P, NB])
        gi = sb("gi", [P, NB, H0])
        gf = sb("gf", [P, NB, H0])
        ga = sb("ga", [P, NB, H0])
        gb = sb("gb", [P, NB, H0])
        cs = sb("cs", [P, NB, H0])
        aT = sb("aT", [NB * H0, P])
        mT = sb("mT", [NB * H0, P])
        mm = sb("mm", [P, NB, H0])
        floor = sb("floor", [P, NB, H0])
        nrm = sb("nrm", [P, H0])
        hm = sb("hm", [P, H0])
        sq = sb("sq", [P, D])
        hv = sb("hv", [P, NB, H0])
        hr = sb("hr", [P, NB, H0])
        lg = sb("lg", [P, NB, NE])
        pr = sb("pr", [P, NB, NE])
        p2 = sb("p2", [P, NB, NE])
        eq = sb("eq", [P, NB, NE])
        top = sb("top", [P, NB, 1])
        oh = sb("oh", [P, 2, NB, NE])
        cum = sb("cum", [P, 2, NB, NE])
        tot = sb("tot", [P, 2 * NE, NB])
        inc = sb("inc", [P, 2 * NE, NB])
        gate = sb("gate", [P, NB, NE])
        gsum = sb("gsum", [P, NB, 1])
        mx = sb("mx", [P, 2])
        m1 = sb("m1", [2, 2])
        m1b = sb("m1b", [2, 2])
        sc = sb("sc", [P, 8])
        qs = sb("qs", [P, NB, HA, SLOTA], F16)
        ks = sb("ks", [P, NB, HA, SLOTA], F16)
        nmax = sb("nmax", [P, NB, HA])
        rden = sb("rden", [P, HA])
        t2 = c
        hh = t1
        acc = at
        mst, am, q0, k0, qk0, dec, cc = carve(
            phase, ((NB * H0, SLOT0), F16), ((2, 8, P), F16), ((2, H0, SLOT0), F16),
            ((2, H0, SLOT0), F16), ((2, 8, P), F16), ((2, 4, P), F32), ((2, H0, P), F32))
        xq, up, gt = carve(phase, ((NB * P,), F32), ((3, NB * P), F32), ((3, NB * P), F32))
        pt, qkT = carve(phase, ((2, HA, P), F32), ((NB, 8, P), F16))
        act, hid = carve(work, ((2, 2, BANK), F32), ((2, 2, BANK), F32))
        v0, ast, w1 = carve(work, ((NB, H0, D0 + 1), F32), ((NB * H0, SLOT0), F16), ((2 * D,), F32))
        at_names = ("a_wt", "b_qt", "b_wt", "b_ft", "c_wt")
        atT = dict(zip(at_names, carve(work, *[((P,), F32)] * len(at_names))))
        (h3,) = carve(work, ((5, BANK), F32))
        (sg,) = carve(split["f0"], ((3, NB * P), F32))
        q2T, q32, v9 = carve(stage_f32, ((NB, 4, P), F16), ((2, 3, D), F32), ((NB, HA, DA + 1), F32))
        gT = cmeanB[0:NE, :, :]
        psum = ctx.enter_context(nc.psum_tensor("psum", [P, PSUM_BANKS * BANK], F32))
        full = [sem(f"bank{k}_full") for k in range(PSUM_BANKS)]
        free = [sem(f"bank{k}_free") for k in range(PSUM_BANKS)]
        banks = Banks(order, psum, full, free)

        norms_ = [o for o in order if o[0] in NORMS]
        norm_turn = {o: n + 1 for n, o in enumerate(norms_)}
        pt_turn = {(s[0], b): n for n, (s, b) in enumerate(o for o in order if o[0] in ("a_exp", "b_exp", "c_exp"))}
        assert list(pt_turn) == [(s[0], b) for s, b in order if s in ("a_av", "b_av", "c_av")]

        def as16(tile):
            return tile.bitcast(F16)

        done = sem("stored")
        n_loads = {}

        block = ctx.enter_context(nc.Block())

        loads = [
            ("x", x[:, :, :], t["x"].rearrange("b p d -> p b d")),
            ("x", c[:, :, :], t["ctx_1024"].rearrange("b p d -> p b d")),
            ("x0", wif[0:H0, :], t["L0_xattn_Wi_w"]),
            ("x0", wif[H0:2 * H0, :], t["L0_xattn_Wf_w"]),
            ("x0", ifb[:, 0:H0], t["L0_xattn_Wi_b"].partition_broadcast(P)),
            ("x0", ifb[:, H0:2 * H0], t["L0_xattn_Wf_b"].partition_broadcast(P)),
            ("x0", tg[:, 0:4], t["g_xattn"].partition_broadcast(P)),
            ("x0", tg[:, 4:8], t["g_ffn"].partition_broadcast(P)),
            ("x0", wg0[:, :], t["L0_ffn_Wg"]),
            ("win", win, t["L0_ffn_W_in"].rearrange("e h f -> h e f")),
        ] + [("rows", rows[:, i, :], t[n].partition_broadcast(P)) for i, n in enumerate(vecs)] + [
            ("wout", wout["f0"][:, :, :, :], t["L0_ffn_W_out"].rearrange("e (c p) h -> p e c h", p=P)),
            ("l1", w1[:, :], t["L1_xattn_W"]),
            ("l1", wq8[:, 0, :, :], t["L1_ffn_w_up"].rearrange("(c p) d -> p c d", p=P)),
            ("l1", wq8[:, 1, :, :], t["L1_ffn_w_gate"].rearrange("(c p) d -> p c d", p=P)),
            ("l1", wq8[:, 2, :, :], t["L1_ffn_w_down"].rearrange("p (c d) -> p c d", c=3)),
            ("l1", router[:, :], t["L2_ffn_router_w"]),
        ] + [("l2", w[:, i, :].rearrange("e (h d) -> e h d", h=HA), t[f"L2_xattn_W{n}{m}"].rearrange("h e d -> e h d"))
             for w, m in ((wA, 1), (wB, 2)) for i, n in enumerate("qkv")] + [
            ("l2", woA[:, :], t["L2_xattn_Wo1"]),
            ("l2", woB[:, :], t["L2_xattn_Wo2"]),
            ("l2", wf[:, :], t["L2_xattn_Wf"]),
            ("win2", win, t["L2_ffn_w13"].rearrange("e h f -> h e f")),
            ("win2", wout["f2"][:, :, :, :], t["L2_ffn_w2"].rearrange("e (c p) h -> p e c h", p=P)),
        ] + [("l3", wC[:, i, :], t[f"L3_xattn_W{n}"]) for i, n in enumerate("qkv")] \
          + [("l3", bqkv[:, i, :], t[f"L3_xattn_b{n}"].partition_broadcast(P)) for i, n in enumerate("qkv")] + [
            ("l3", woC[:, :], t["L3_xattn_Wo"]),
            ("l3", wg3[:, :], t["L3_ffn_gate_W"]),
            ("l3", w31[:, :, :], t["L3_ffn_W1"].rearrange("e d h -> d e h")),
            ("l3", w32[:, :, :], t["L3_ffn_W2"].rearrange("(c two) h d -> (two h) c d", two=2)),
            ("l3", b31[:, :], t["L3_ffn_b1"].rearrange("(c two) h -> (two h) c", two=2)),
            ("l3", b32[:, :], t["L3_ffn_b2"]),
            ("l3", ws1[:, :], t["L3_ffn_Ws1"]),
            ("l3", ws2[:, :], t["L3_ffn_Ws2"]),
            ("l3", bs1[:, :], t["L3_ffn_bs1"].rearrange("(h o) -> h o", o=1)),
            ("l3", rscale[:, :], t["L3_ffn_route_scale"].partition_broadcast(P)),
        ]
        for g, _, _ in loads:
            n_loads[g] = n_loads.get(g, 0) + 16

        def loaded(eng, *groups):
            for g in groups:
                eng.wait_ge(sem("loaded_" + g), n_loads[g])

        @block.sync
        def _(sp):
            with nc.allow_non_contiguous_dma(reason="weights laid out once"):
                for g, dst, src in loads:
                    if g == "win2" and dst is win:
                        sp.wait_ge(sem("win_split"), NE)
                    sp.dma_start(dst, src).then_inc(sem("loaded_" + g), 16)
            for b in range(NB):
                sp.wait_ge(sem("x_final"), (b // HALF + 1) * HALF)
                sp.dma_start(t["out"][b], x[:, b, :]).then_inc(done, 16)
            sp.wait_ge(done, 16 * NB)

        @block.gpsimd
        def _(pool):
            ch = Chain(pool, sem("pool_step"))

            def rsqrt(col, eps, ready):
                pool.wait_ge(*ready)
                ch.do(pool.tensor_scalar(vr[:, col:col + 1], mv[:, col, 1:2], eps, None, ALU.add))
                ch.sync()
                ch.do(pool.tensor_tensor(rstd[:, col:col + 1], vr[:, col:col + 1], mhalf[:, 0:1], ALU.pow),
                      sem("rstd_ready"))

            for stage, b in order:
                if stage == "setup":
                    ch.do(pool.memset(ident[:, :], 0.0))
                    ch.do(pool.memset(mhalf[:, :], -0.5))
                    ch.sync()
                    ch.do(pool.affine_select(out=ident[:, :], in_=ident[:, :], compare_op=ALU.not_equal, fill=1.0,
                                             base=0, pattern=[[-1, P]], channel_multiplier=1), sem("ident_ready"))
                    ch.do(pool.memset(tri[:, :], 1.0))
                    ch.do(pool.memset(maskT[:, :, :], 0.0))
                    ch.do(pool.memset(maskQ[:, :, :], 0.0))
                    ch.sync()
                    ch.do(pool.affine_select(out=tri[:, :], in_=tri[:, :], compare_op=ALU.is_ge, fill=0.0,
                                             base=0, pattern=[[1, P]], channel_multiplier=-1))
                    ch.do(pool.affine_select(out=maskT[:, :, :], in_=maskT[:, :, :], compare_op=ALU.is_ge,
                                             fill=MASKED, base=0, pattern=[[0, 4], [1, P]], channel_multiplier=-1))
                    ch.do(pool.affine_select(out=maskQ[:, :, :], in_=maskQ[:, :, :], compare_op=ALU.is_ge,
                                             fill=MASKED, base=0, pattern=[[0, 4], [-1, P]], channel_multiplier=1),
                          sem("const_ready"))
                elif stage == "x0_forget":
                    ch.do(pool.memset(reset[:, :, :], 1.0))
                    ch.sync()
                    ch.do(pool.memset(reset[:, :, 0:1], 0.0))
                    for e in range(NE):
                        ch.do(pool.memset(rank[:, :, e:e + 1], float(NE - e)), sem("route_consts") if e == NE - 1 else None)
                    ch.do(pool.memset(sel[:, :, :], 1.0))
                    ch.sync()
                    ch.do(pool.affine_select(out=sel[:, :, :], in_=sel[:, :, :], compare_op=ALU.is_ge, fill=0.0,
                                             base=0, pattern=[[P, 4], [1, P]], channel_multiplier=-64))
                    ch.sync()
                    ch.do(pool.affine_select(out=sel[:, :, :], in_=sel[:, :, :], compare_op=ALU.is_ge, fill=0.0,
                                             base=63, pattern=[[-P, 4], [-1, P]], channel_multiplier=64), sem("sel_ready"))
                elif stage == "x0_split":
                    if b == 0:
                        loaded(pool, "x")
                        dve_memsets = sem("stack_zeros")
                        pool.wait_ge(dve_memsets, 1)
                    cb = c[:, b, :].rearrange("p (h d) -> p h d", h=H0)
                    ch.do(pool.tensor_copy(v0[:, b, :, 0:D0], cb), sem("v0_ready"))
                    kk = k0[:, b % 2, :, :]
                    pool.wait_ge(sem("k0_high"), b + 1)
                    ch.do(pool.tensor_tensor(kk[:, :, D0:2 * D0], cb, kk[:, :, 0:D0], ALU.subtract), sem("k0_ready"))
                elif stage in ("split0", "split2"):
                    f = "f0" if stage == "split0" else "f2"
                    pool.wait_ge(sem("win_high"), (NE if f == "f2" else 0) + b + 1)
                    ch.do(pool.tensor_tensor(winl[f][:, b, :], win[:, b, :], winh[f][:, b, :], ALU.subtract),
                          sem("win_split"))
                elif stage in ("f0_t", "f2_t"):
                    l = {"f0_t": 0, "f2_t": 1}[stage]
                    pool.wait_ge(sem("zTh_ready"), l * NB + b + 1)
                    ch.do(pool.tensor_tensor(zTl[:, b, :], zT[:, b, :], zTh[:, b, :], ALU.subtract), sem("zTl_ready"))
                elif stage == "f1_scale":
                    pool.wait_ge(sem("win_split"), 2 * NE)
                    ch.do(pool.memset(v9[:, :, :, DA:DA + 1], 1.0), sem("v9_ones"))
                elif stage == "x0_value":
                    pool.wait_ge(sem("hv_ready"), b + 1)
                    ch.do(pool.tensor_tensor(hr[:, b, :], hv[:, b, :], mhalf[:, :], ALU.pow), sem("hr_ready"))
                if stage in NORMS:
                    rsqrt(b, NORMS[stage], (sem("stats_ready"), norm_turn[stage, b]))

        @block.tensor
        def _(pe):
            mm_ = nc.tensor.matmul
            tr = nc.tensor.transpose

            def one(out, a, b_):
                return mm_(out, a, b_, start=True, stop=True)

            def to_T(key, b):
                pe.wait_ge(sem(key[:2] + "_z"), b + 1)
                u = banks.take(pe, key, b, "u")
                banks.fill(tr(u[:, 0:P], z[:, b, :], ident[:, :]), key, b, "u")

            for stage, b in order:
                if stage == "setup":
                    pe.wait_ge(sem("ident_ready"), 1)
                    loaded(pe, "x")
                    for i in range(2):
                        u = banks.take(pe, "setup", 0, f"ctx{i}")
                        for j in range(4):
                            last = tr(u[:, j * P:(j + 1) * P], c[:, 4 * i + j, :], ident[:, :])
                        banks.fill(last, "setup", 0, f"ctx{i}")
                    loaded(pe, "x0")
                    u = banks.take(pe, "setup", 0, "gate_w")
                    for j in range(3):
                        last = tr(u[:, j * 2 * H0:(j + 1) * 2 * H0], wif[:, j * D:(j + 1) * D], ident[0:2 * H0, 0:2 * H0])
                    banks.fill(last, "setup", 0, "gate_w")
                elif stage == "w1":
                    loaded(pe, "l1")
                    u = banks.take(pe, stage, b, "u")
                    for j in range(2):
                        last = tr(u[:, j * D:(j + 1) * D], w1[:, j * D:(j + 1) * D], ident[:, :])
                    banks.fill(last, stage, b, "u")
                elif stage == "w8":
                    pe.wait_ge(sem("w8_ready"), b + 1)
                    u = banks.take(pe, stage, b, "u")
                    for j in range(3):
                        last = tr(u[:, j * P:(j + 1) * P], wq8[:, b, j, :], ident[:, :])
                    banks.fill(last, stage, b, "u")
                elif stage == "router":
                    loaded(pe, "l1")
                    u = banks.take(pe, stage, b, "u")
                    banks.fill(tr(u[:, 0:NE], router[:, :], ident[0:NE, 0:NE]), stage, b, "u")
                elif stage in T_STAGES:
                    to_T(stage, b)
                elif stage == "x0_gate":
                    pe.wait_ge(sem("x0_zT"), b + 1)
                    if b == 0:
                        u0 = banks.take(pe, "x0_gate", 0, "gates")
                        pe.wait_ge(sem("wT_ready"), 3)
                    o = u0[:, b * 2 * H0:(b + 1) * 2 * H0]
                    mm_(o, zT[:, b, :], wifT[:, 0, :], start=True, stop=False)
                    mm_(o, cT[:, b, :], wifT[:, 1, :], start=False, stop=False)
                    last = mm_(o, cT[:, b, :], wifT[:, 2, :], start=False, stop=True)
                    if b == NB - 1:
                        banks.fill(last, "x0_gate", 0, "gates")
                elif stage == "x0_forget":
                    pe.wait_ge(sem("const_ready"), 1)
                    pe.wait_ge(sem("log_forget"), 1)
                    u = banks.take(pe, stage, 0, "csum")
                    banks.fill(one(u[:, 0:NB * H0], tri[:, :], gf[:, :, :]), stage, 0, "csum")
                    pe.wait_ge(sem("a_ready"), 1)
                    u = banks.take(pe, stage, 0, "at")
                    banks.fill(tr(u[0:NB * H0, 0:P], ga[:, :, :].rearrange("p b h -> p (b h)"), ident[:, :]), stage, 0, "at")
                    pe.wait_ge(sem("mT_ready"), 1)
                    u = banks.take(pe, stage, 0, "m")
                    banks.fill(tr(u[:, 0:NB * H0], mT[:, :], ident[0:NB * H0, 0:NB * H0]), stage, 0, "m")
                elif stage == "x0_stack":
                    if b == 0:
                        pe.wait_ge(sem("ident16_ready"), 2)
                    pe.wait_ge(sem("q0_ready"), b + 1)
                    pe.wait_ge(sem("k0_ready"), b + 1)
                    u = as16(banks.take(pe, stage, b, "qk"))
                    for i, st in enumerate((q0, k0)):
                        for j in range(4):
                            o = (4 * i + j) * P
                            last = tr(u[:, o:o + P], st[:, b % 2, 2 * j:2 * j + 2, :].rearrange("p h s -> p (h s)"), ident16[:, :])
                    banks.fill(last, stage, b, "qk")
                    u = as16(banks.take(pe, stage, b, "am"))
                    pe.wait_ge(sem("am_ready"), 1)
                    for i, st in enumerate((ast, mst)):
                        for j in range(4):
                            h = b * H0 + 2 * j
                            o = (4 * i + j) * P
                            last = tr(u[:, o:o + P], st[:, h:h + 2, :].rearrange("p h s -> p (h s)"), ident16[:, :])
                    banks.fill(last, stage, b, "am")
                elif stage == "x0_score":
                    if b == 0:
                        pe.wait_ge(sem("ident16_ready"), 2)
                    pe.wait_ge(sem("qk0_T"), b + 1)
                    pe.wait_ge(sem("am_T"), b + 1)
                    us = [banks.take(pe, stage, b, f"e{g}") for g in range(2)]
                    for g in range(2):
                        mm_(us[g], identb[:, :], maskT[:, :, :].rearrange("p h q -> p (h q)"), start=True, stop=False)
                    for j in range(4):
                        for g in range(2):
                            r = 64 * g
                            last = mm_(us[g][:, j * P:(j + 1) * P], am[r:r + 6, b % 2, j, :], am[r:r + 6, b % 2, 4 + j, :],
                                       start=False, stop=(j == 3))
                            if j == 3:
                                banks.fill(last, stage, b, f"e{g}")
                    us = [banks.take(pe, stage, b, f"s{g}") for g in range(2)]
                    for j in range(4):
                        for g in range(2):
                            r = 64 * g
                            last = one(us[g][:, j * P:(j + 1) * P], qk0[r:r + 48, b % 2, 4 + j, :], qk0[r:r + 48, b % 2, j, :])
                            if j == 3:
                                banks.fill(last, stage, b, f"s{g}")
                elif stage == "x0_value":
                    pe.wait_ge(sem("cc_ready"), 2 * (b + 1))
                    pe.wait_ge(sem("v0_ready"), b + 1)
                    u = banks.take(pe, stage, b, "u")
                    for h in range(H0):
                        last = one(u[:, h * (D0 + 1):(h + 1) * (D0 + 1)], cc[:, b % 2, h, :], v0[:, b, h, :])
                    banks.fill(last, stage, b, "u")
                elif stage in ("f0_route", "f2_route", "f3_route"):
                    w = {"f0_route": wg0, "f2_route": routerT, "f3_route": wg3}[stage]
                    if stage == "f2_route":
                        pe.wait_ge(sem("router_T"), 1)
                    l = {"f0_route": 1, "f2_route": 2, "f3_route": 3}[stage]
                    if stage == "f3_route":
                        loaded(pe, "l3")
                    pe.wait_ge(sem(stage[:2] + "_zT"), NB)
                    name = "logit"
                    u = banks.take(pe, stage, 0, name)
                    for b_ in range(NB):
                        last = one(u[:, b_ * NE:(b_ + 1) * NE], zT[:, b_, :], w[:, :])
                    banks.fill(last, stage, 0, name)
                    if stage == "f0_route":
                        pe.wait_ge(sem("oh_ready"), 1)
                        u = banks.take(pe, stage, 0, "cum")
                        banks.fill(one(u[:, 0:2 * NB * NE], tri[:, :], oh[:, :, :, :].rearrange("p k b e -> p (k b e)")), stage, 0, "cum")
                        u = banks.take(pe, stage, 0, "total")
                        banks.fill(one(u[:, 0:2 * NB * NE], ones[:, :], oh[:, :, :, :].rearrange("p k b e -> p (k b e)")), stage, 0, "total")
                    if stage == "f3_route":
                        pe.wait_ge(sem("gate_ready"), 3)
                        for g in range(2):
                            u = banks.take(pe, stage, 0, f"gt{g}")
                            for j in range(4):
                                last = tr(u[0:NE, j * P:(j + 1) * P], gate[:, 4 * g + j, :], ident[:, :])
                            banks.fill(last, stage, 0, f"gt{g}")
                elif stage in ("f0_up", "f2_up"):
                    e, g = b
                    l = {"f0": 0, "f2": 1}[stage[:2]]
                    pe.wait_ge(sem("zTl_ready"), l * NB + 4 * (g + 1) if e == 0 else (l + 1) * NB)
                    pe.wait_ge(sem("win_split"), l * NE + e + 1)
                    cols = slice(4 * g, 4 * g + 4)
                    xh = zTh[:, cols, :].rearrange("p b q -> p (b q)")
                    xl = zTl[:, cols, :].rearrange("p b q -> p (b q)")
                    for i, name in enumerate(("a0", "g0", "a1", "g1")):
                        u = banks.take(pe, stage, b, name)
                        f = (i // 2) * P + (i % 2) * F
                        mm_(u, winh[stage[:2]][:, e, f:f + P], xh, start=True, stop=False)
                        mm_(u, winh[stage[:2]][:, e, f:f + P], xl, start=False, stop=False)
                        last = mm_(u, winl[stage[:2]][:, e, f:f + P], xh, start=False, stop=True)
                        banks.fill(last, stage, b, name)
                elif stage in ("f0_down", "f2_down"):
                    e, g = b
                    f = stage[:2]
                    l = {"f0": 0, "f2": 1}[f]
                    n = l * NE * FPS + e * FPS + g
                    if e == 0 and g == 0:
                        loaded(pe, "wout" if f == "f0" else "win2")
                    pe.wait_ge(sem("hid_ready"), 2 * (n + 1))
                    u = banks.take(pe, stage, b, "u")
                    for j in range(4):
                        for k in range(2):
                            last = mm_(u[:, j * D:(j + 1) * D], hid[:, n % 2, k, j * P:(j + 1) * P], wout[f][:, e, k, :],
                                       start=(k == 0), stop=(k == 1))
                    banks.fill(last, stage, b, "u")
                elif stage == "x1_out":
                    pe.wait_ge(sem("x1_zT"), b + 1)
                    if b == 0:
                        pe.wait_ge(sem("cmean_ready"), 1)
                        pe.wait_ge(sem("w1_T"), 1)
                    u = banks.take(pe, stage, b, "u")
                    mm_(u[:, 0:D], zT[:, b, :], w1T[:, 0, :], start=True, stop=False)
                    banks.fill(mm_(u[:, 0:D], cmeanB[:, b, :], w1T[:, 1, :], start=False, stop=True), stage, b, "u")
                elif stage == "f1_scale":
                    pe.wait_ge(sem("mx_ready"), 1)
                    u = banks.take(pe, stage, 0, "x_t")
                    banks.fill(tr(u[0:1, 0:P], mx[:, 0:1], ident[:, :]), stage, 0, "x_t")
                    pe.wait_ge(sem("m1_ready"), 1)
                    u = banks.take(pe, stage, 0, "x_b")
                    banks.fill(one(u[:, 0:1], ones[0:1, :], m1b[0:1, 0:1]), stage, 0, "x_b")
                elif stage == "f1_up":
                    cch, g = b
                    pe.wait_ge(sem("xq_ready"), 1)
                    pe.wait_ge(sem("w8_T"), 3)
                    for i, name in enumerate(("up", "gate")):
                        u = banks.take(pe, stage, b, name)
                        banks.fill(one(u, w8T[:, i, cch * P:(cch + 1) * P], xq[:, g * BANK:(g + 1) * BANK]), stage, b, name)
                elif stage == "f1_mid":
                    for i, name in enumerate(("ug", "gs", "o")):
                        n = 2 if name == "ug" else 1
                        pe.wait_ge(sem("mx_ready"), i + 2)
                        u = banks.take(pe, stage, 0, name + "_t")
                        banks.fill(tr(u[0:n, 0:P], mx[:, 0:n], ident[:, :]), stage, 0, name + "_t")
                        pe.wait_ge(sem("m1_ready"), i + 2)
                        u = banks.take(pe, stage, 0, name + "_b")
                        banks.fill(one(u[:, 0:n], ones[0:n, :], m1b[0:n, 0:n]), stage, 0, name + "_b")
                elif stage == "f1_down":
                    if b == 0:
                        pe.wait_ge(sem("o_ready"), 1)
                    u = banks.take(pe, stage, b, "u")
                    for k in range(3):
                        last = mm_(u[:, 0:D], sg[:, k, b * P:(b + 1) * P], w8T[:, 2, k * P:(k + 1) * P], start=(k == 0), stop=(k == 2))
                    banks.fill(last, stage, b, "u")
                elif stage in ("a_kv", "b_kv", "c_kv"):
                    m = stage[0]
                    u = banks.take(pe, stage, b, "qkv")
                    if m == "a":
                        if b == 0:
                            loaded(pe, "l2")
                        pe.wait_ge(sem("x2_zT"), b + 1)
                        last = one(u[:, 0:3 * D], zT[:, b, :], wA[:, :, :].rearrange("p i d -> p (i d)"))
                    elif m == "b":
                        last = one(u[:, D:3 * D], cT[:, b, :], wB[:, 1:3, :].rearrange("p i d -> p (i d)"))
                    else:
                        if b == 0:
                            loaded(pe, "l3")
                        pe.wait_ge(sem("x3_zT"), b + 1)
                        one(u[:, 0:D], zT[:, b, :], wC[:, 0, :])
                        last = one(u[:, D:3 * D], cT[:, b, :], wC[:, 1:3, :].rearrange("p i d -> p (i d)"))
                    banks.fill(last, stage, b, "qkv")
                elif stage in ("b_qt", "b_ft"):
                    pe.wait_ge(sem("a_out" if stage == "b_qt" else "b_out"), b + 1)
                    u = banks.take(pe, stage, b, "t")
                    banks.fill(tr(u[:, 0:P], t1[:, b, :], ident[:, :]), stage, b, "t")
                elif stage == "b_q":
                    pe.wait_ge(sem("b_qt_T"), b + 1)
                    u = banks.take(pe, stage, b, "q")
                    banks.fill(one(u[:, 0:D], atT["b_qt"][:, :], wB[:, 0, :]), stage, b, "q")
                elif stage in ("a_stack", "b_stack", "c_stack"):
                    m = stage[0]
                    pe.wait_ge(sem(m + "_stacks"), b + 1)
                    if m == "b":
                        pe.wait_ge(sem("b_qs"), b + 1)
                    u = as16(banks.take(pe, stage, b, "qk"))
                    for i, st in enumerate((qs, ks)):
                        for j in range(4):
                            o = (4 * i + j) * P
                            last = tr(u[:, o:o + P], st[:, b, 4 * j:4 * j + 4, :].rearrange("p h s -> p (h s)"), ident16[:, :])
                    banks.fill(last, stage, b, "qk")
                elif stage in ("a_max", "b_max", "c_max"):
                    m = stage[0]
                    pe.wait_ge(sem(m + "_qkT"), b + 1)
                    us = [banks.take(pe, stage, b, f"s{i}") for i in range(4)]
                    if m == "a":
                        for u in us:
                            mm_(u, identb[:, :], maskQ[:, :, :].rearrange("p h q -> p (h q)"), start=True, stop=False)
                    for j in range(4):
                        for i in range(4):
                            r = 32 * i
                            last = mm_(us[i][:, j * P:(j + 1) * P], qkT[r:r + DA, b, j, :], qkT[r:r + DA, b, 4 + j, :],
                                       start=(m != "a"), stop=(j == 3 or m != "a"))
                            if j == 3:
                                banks.fill(last, stage, b, f"s{i}")
                elif stage in ("a_again", "b_again", "c_again"):
                    m = stage[0]
                    pe.wait_ge(sem(m + "_negmax"), b + 1)
                    u = as16(banks.take(pe, stage, b, "q"))
                    for j in range(4):
                        last = tr(u[:, j * P:(j + 1) * P], qs[:, b, 4 * j:4 * j + 4, :].rearrange("p h s -> p (h s)"), ident16[:, :])
                    banks.fill(last, stage, b, "q")
                elif stage in ("a_exp", "b_exp", "c_exp"):
                    m = stage[0]
                    n = 3 * DA + 2
                    pe.wait_ge(sem(m + "_q2T"), b + 1)
                    us = [banks.take(pe, stage, b, f"t{i}") for i in range(4)]
                    if m == "a":
                        for u in us:
                            mm_(u, identb[:, :], maskT[:, :, :].rearrange("p h q -> p (h q)"), start=True, stop=False)
                    for j in range(4):
                        for i in range(4):
                            r = 32 * i
                            last = mm_(us[i][:, j * P:(j + 1) * P], qkT[r:r + n, b, 4 + j, :], q2T[r:r + n, b, j, :],
                                       start=(m != "a"), stop=(j == 3 or m != "a"))
                            if j == 3:
                                banks.fill(last, stage, b, f"t{i}")
                elif stage in ("a_av", "b_av", "c_av"):
                    m = stage[0]
                    n = pt_turn[m, b]
                    u = banks.take(pe, stage, b, "av")
                    for i in range(HA):
                        h = 4 * (i % 4) + i // 4
                        if i % 4 == 0:
                            pe.wait_ge(sem("pt_ready"), 4 * n + i // 4 + 1)
                        last = one(u[:, h * (DA + 1):(h + 1) * (DA + 1)], pt[:, n % 2, h, :], v9[:, b, h, :])
                    banks.fill(last, stage, b, "av")
                elif stage in ("a_wt", "b_wt", "c_wt"):
                    pe.wait_ge(sem(stage[0] + "_at"), b + 1)
                    u = banks.take(pe, stage, b, "t")
                    banks.fill(tr(u[:, 0:P], at[:, b, :], ident[:, :]), stage, b, "t")
                elif stage in ("a_wo", "b_wo", "c_wo"):
                    m = stage[0]
                    pe.wait_ge(sem(m + "_wt_T"), b + 1)
                    u = banks.take(pe, stage, b, "wo")
                    banks.fill(one(u[:, 0:D], atT[m + "_wt"][:, :], {"a": woA, "b": woB, "c": woC}[m][:, :]), stage, b, "wo")
                elif stage == "b_f":
                    pe.wait_ge(sem("b_ft_T"), b + 1)
                    u = banks.take(pe, stage, b, "f")
                    banks.fill(one(u[:, 0:D], atT["b_ft"][:, :], wf[:, :]), stage, b, "f")
                elif stage == "f3_up":
                    pe.wait_ge(sem("gT_ready"), 2)
                    pe.wait_ge(sem("sel_ready"), 1)
                    xg = zT[:, 4 * b:4 * b + 4, :].rearrange("p b q -> p (b q)")
                    for k in range(5):
                        u = banks.take(pe, stage, b, f"h{k}")
                        if k < 4:
                            banks.fill(one(u, w31[:, 2 * k:2 * k + 2, :].rearrange("p e h -> p (e h)"), xg), stage, b, f"h{k}")
                            u = banks.take(pe, stage, b, f"gate{k}")
                            banks.fill(one(u, sel[:, k, :], gT[:, 4 * b:4 * b + 4, :].rearrange("p b q -> p (b q)")), stage, b, f"gate{k}")
                        else:
                            banks.fill(one(u[0:64, :], ws1[:, :], xg), stage, b, f"h{k}")
                elif stage == "f3_down":
                    pe.wait_ge(sem("h3_gated"), 4 * (b + 1))
                    pe.wait_ge(sem("h3_ready"), 5 * (b + 1))
                    u = banks.take(pe, stage, b, "o")
                    for j in range(4):
                        o = u[:, j * D:(j + 1) * D]
                        for k in range(4):
                            mm_(o, h3[:, k, j * P:(j + 1) * P], w32[:, k, :], start=(k == 0), stop=False)
                        mm_(o, h3[0:64, 4, j * P:(j + 1) * P], ws2[:, :], start=False, stop=False)
                        last = mm_(o, gT[:, 4 * b + j, :], b32[:, :], start=False, stop=True)
                    banks.fill(last, stage, b, "o")

        @block.scalar
        def _(act_):
            ch = Chain(act_, sem("act_step"))
            A = nc.scalar.activation

            def copy_free(stage, b, name, out, view, signal):
                u = banks.get(act_, stage, b, name)
                ch.do(A(out, view(u), ACT.Copy), banks.freed(stage, b, name))
                ch.sync()
                act_.sem_inc(signal, 1)

            for stage, b in order:
                if stage == "setup":
                    loaded(act_, "x0")
                    ch.do(A(tg[:, :], tg[:, :], ACT.Tanh), sem("tg_ready"))
                    act_.wait_ge(sem("ident_ready"), 1)
                    ch.do(A(ident16[:, :], ident[:, :], ACT.Copy), sem("ident16_ready"))
                    ch.do(A(identb[:, :], ident[:, :], ACT.Copy), sem("ident16_ready"))
                    for i in range(2):
                        copy_free(stage, b, f"ctx{i}", cT[:, 4 * i:4 * i + 4, :], lambda u: u.rearrange("p (b q) -> p b q", b=4), sem("wT_ready"))
                    copy_free(stage, b, "gate_w", wifT[:, :, :], lambda u: u[:, 0:6 * H0].rearrange("p (i g) -> p i g", i=3), sem("wT_ready"))
                elif stage == "w1":
                    copy_free(stage, b, "u", w1T[:, :, :], lambda u: u[:, 0:2 * D].rearrange("p (i g) -> p i g", i=2), sem("w1_T"))
                elif stage == "w8":
                    copy_free(stage, b, "u", w8T[:, b, :], lambda u: u[:, 0:I1], sem("w8_T"))
                elif stage == "router":
                    copy_free(stage, b, "u", routerT[:, :], lambda u: u[:, 0:NE], sem("router_T"))
                elif stage in T_STAGES:
                    copy_free(stage, b, "u", zT[:, b, :], lambda u: u[:, 0:P], sem(stage[:2] + "_zT"))
                    if stage in ("f0_t", "f2_t"):
                        ch.do(A(zTh[:, b, :], zT[:, b, :], ACT.Copy), sem("zTh_ready"))
                elif stage == "x0_split":
                    if b == 0:
                        act_.wait_ge(sem("stack_zeros"), 1)
                    cb = c[:, b, :].rearrange("p (h d) -> p h d", h=H0)
                    kk = k0[:, b % 2, :, :]
                    ch.do(A(kk[:, :, 0:D0], cb, ACT.Copy))
                    ch.do(A(kk[:, :, 2 * D0:3 * D0], cb, ACT.Copy), sem("k0_high"))
                elif stage in ("split0", "split2"):
                    f = "f0" if stage == "split0" else "f2"
                    if b == 0:
                        loaded(act_, "win" if f == "f0" else "win2")
                    ch.do(A(winh[f][:, b, :], win[:, b, :], ACT.Copy), sem("win_high"))
                elif stage == "x0_forget":
                    act_.wait_ge(sem("abs_f"), 1)
                    ch.do(A(ga[:, :, :], ga[:, :, :], ACT.Exp, scale=-1.0))
                    ch.sync()
                    ch.do(A(gb[:, :, :], ga[:, :, :], ACT.Ln, bias=1.0), sem("softplus"))
                    act_.wait_ge(sem("md_ready"), 1)
                    ch.do(A(floor[:, :, :], gb[:, :, :], ACT.Exp, scale=-1.0), sem("floor_ready"))
                elif stage == "x0_stack":
                    if b >= 2:
                        act_.wait_ge(sem("cc_ready"), 2 * (b - 1))
                    copy_free(stage, b, "qk", qk0[:, b % 2, :, :], lambda u: as16(u).rearrange("p (s q) -> p s q", s=8), sem("qk0_T"))
                    act_.sem_inc(sem("x0_stacked"), 1)
                    copy_free(stage, b, "am", am[:, b % 2, :, :], lambda u: as16(u).rearrange("p (s q) -> p s q", s=8), sem("am_T"))
                elif stage == "x0_score":
                    for j in range(2):
                        if b >= 1:
                            act_.wait_ge(sem("cc_ready"), 2 * b + j - 1)
                        u = banks.get(act_, stage, b, f"e{j}")
                        ch.do(A(dec[:, j, :, :], u.rearrange("p (h q) -> p h q", h=4), ACT.Exp), banks.freed(stage, b, f"e{j}"))
                        ch.sync()
                        act_.sem_inc(sem("dec_ready"), 1)
                elif stage in ("f0_route", "f2_route", "f3_route"):
                    n = {"f0_route": 1, "f2_route": 2, "f3_route": 3}[stage]
                    act_.wait_ge(sem("logit_ready"), n)
                    ch.do(A(pr[:, :, :], lg[:, :, :], ACT.Exp, scale=-1.0 if n == 3 else 1.0), sem("route_exp"))
                    if n == 3:
                        for g in range(2):
                            copy_free(stage, 0, f"gt{g}", gT[:, 4 * g:4 * g + 4, :], lambda u: u[0:NE, :].rearrange("p (b q) -> p b q", b=4), sem("gT_ready"))
                elif stage in ("f0_up", "f2_up"):
                    e, g = b
                    n = (0 if stage == "f0_up" else NE * FPS) + e * FPS + g
                    for k in range(2):
                        if n >= 2:
                            act_.wait_ge(sem("hid_ready"), 2 * (n - 2) + k + 1)
                        u = banks.get(act_, stage, b, f"a{k}")
                        ch.do(A(act[:, n % 2, k, :], u, ACT.Gelu if stage == "f0_up" else ACT.Silu),
                              banks.freed(stage, b, f"a{k}"))
                        ch.sync()
                        act_.sem_inc(sem("act_ready"), 1)
                elif stage == "f1_mid":
                    act_.wait_ge(sem("gateq_ready"), 1)
                    ch.do(A(sg[:, :, :], gt[:, :, :], ACT.Sigmoid), sem("sig_ready"))
                elif stage in ("a_stack", "b_stack", "c_stack"):
                    copy_free(stage, b, "qk", qkT[:, b, :, :], lambda u: as16(u).rearrange("p (s q) -> p s q", s=8), sem(stage[0] + "_qkT"))
                elif stage in ("a_again", "b_again", "c_again"):
                    copy_free(stage, b, "q", q2T[:, b, :, :], lambda u: as16(u)[:, 0:4 * P].rearrange("p (s q) -> p s q", s=4), sem(stage[0] + "_q2T"))
                elif stage in ("a_exp", "b_exp", "c_exp"):
                    m = stage[0]
                    n = pt_turn[m, b]
                    if n >= 2:
                        act_.wait_ge(sem("pt_used"), n - 1)
                    scale = {"a": P ** -0.5, "b": P ** -0.5, "c": DA ** -0.5}[m]
                    for j in range(4):
                        u = banks.get(act_, stage, b, f"t{j}")
                        ch.do(A(pt[:, n % 2, :, :].rearrange("p (i g) q -> p g i q", g=4)[:, j], u.rearrange("p (h q) -> p h q", h=4), ACT.Exp, scale=scale), banks.freed(stage, b, f"t{j}"))
                        ch.sync()
                        act_.sem_inc(sem("pt_ready"), 1)
                elif stage in atT:
                    copy_free(stage, b, "t", atT[stage][:, :], lambda u: u[:, 0:P], sem(stage + "_T"))
                elif stage == "f3_up":
                    for k in range(5):
                        if b:
                            act_.wait_ge(sem("f3_stored"), 1)
                        u = banks.get(act_, stage, b, f"h{k}")
                        r = P if k < 4 else 64
                        bias = b31[:, k:k + 1] if k < 4 else bs1[:, :]
                        ch.do(A(h3[0:r, k, :], u[0:r, :], ACT.Gelu, bias=bias), banks.freed(stage, b, f"h{k}"))
                        ch.sync()
                        act_.sem_inc(sem("h3_ready"), 1)

        @block.vector
        def _(dve):
            ch = Chain(dve, sem("dve_step"))
            v = nc.vector
            tt, ts, stt = v.tensor_tensor, v.tensor_scalar, v.scalar_tensor_tensor

            def free_of(*key):
                return banks.freed(*key)

            def get(stage, b, name):
                return banks.get(dve, stage, b, name)

            def norm_stats(src, b):
                ch.do(v.bn_stats(stats[:, b, :], src))
                ch.sync()
                ch.do(v.bn_aggr(mv[:, b, :], stats[:, b, :]), sem("stats_ready"))

            def normalise(stage, out, src, b, signal):
                turn = norm_turn[NORM_OF[stage], b]
                dve.wait_ge(sem("stats_ready"), turn)
                dve.wait_ge(sem("rstd_ready"), turn)
                ch.do(ts(out, src, mv[:, b, 0:1], rstd[:, b:b + 1], ALU.subtract, ALU.mult), signal)

            def twice(out, src, n):
                ch.do(v.tensor_copy(out, bc(src.unsqueeze(2), [P, n, 2, src.shape[-1]])))

            def split_q(m, b, src, i, signal=None):
                st = (qs, ks)[i][:, b, :, :]
                src = src.rearrange("p (h d) -> p h d", h=HA)
                lo = 2 if i == 0 else 1
                hi2 = 1 if i == 0 else 2
                twice(st[:, :, 0:4 * DA].rearrange("p h (s d) -> p h s d", d=DA)[:, :, 0:hi2 + 1:hi2, :], src, HA)
                ch.sync()
                ch.do(tt(st[:, :, lo * DA:(lo + 1) * DA], src, st[:, :, 0:DA], ALU.subtract), signal)

            def pick(i, probs):
                ch.sync()
                ch.do(v.tensor_reduce(top[:, :, 0], probs, AX.X, ALU.max))
                ch.sync()
                ch.do(tt(eq[:, :, :], probs, bc(top[:, :, :], [P, NB, NE]), ALU.is_equal))
                ch.sync()
                ch.do(tt(eq[:, :, :], eq[:, :, :], rank[:, :, :], ALU.mult))
                ch.sync()
                ch.do(v.tensor_reduce(top[:, :, 0], eq[:, :, :], AX.X, ALU.max))
                ch.sync()
                ch.do(tt(oh[:, i, :, :], eq[:, :, :], bc(top[:, :, :], [P, NB, NE]), ALU.is_equal),
                      sem("oh_ready") if i else None)

            def top2():
                dve.wait_ge(sem("route_consts"), 1)
                pick(0, pr[:, :, :])
                ch.sync()
                ch.do(ts(p2[:, :, :], oh[:, 0, :, :], -3.0e38, None, ALU.mult))
                ch.sync()
                ch.do(tt(p2[:, :, :], p2[:, :, :], pr[:, :, :], ALU.add))
                pick(1, p2[:, :, :])

            def global_scale(n, unit, cols, stage):
                u = get(stage, 0, unit + "_t")
                ch.do(v.tensor_reduce(m1[0:cols, 0:1], u[0:cols, 0:P], AX.X, ALU.max), free_of(stage, 0, unit + "_t"))
                ch.sync()
                if cols == 2:
                    ch.do(ts(m1b[0:2, 0:2], ident[0:2, 0:2], m1[0:2, 0:1], None, ALU.mult), sem("m1_ready"))
                else:
                    ch.do(v.tensor_copy(m1b[0:1, 0:1], m1[0:1, 0:1]), sem("m1_ready"))
                u = get(stage, 0, unit + "_b")
                ch.do(ts(sc[:, 0:cols], u[:, 0:cols], 1.0 / QMAX, 1e-12, ALU.mult, ALU.max), free_of(stage, 0, unit + "_b"))
                ch.sync()
                ch.do(v.reciprocal(sc[:, 4:4 + cols], sc[:, 0:cols]))
                ch.sync()

            def quantise(out, src, col, signal=None):
                ch.do(ts(out, src, sc[:, 4 + col:5 + col], MAGIC, ALU.mult, ALU.add))
                ch.sync()
                ch.do(ts(out, out, -MAGIC, sc[:, col:col + 1], ALU.add, ALU.mult), signal)

            for stage, b in order:
                if stage == "setup":
                    for st_ in (ast, mst):
                        ch.do(v.memset(st_.rearrange("p h s -> p (h s)").bitcast(F32), 0.0))
                    ch.do(v.memset(q0[:, :, :, 3 * D0:SLOT0], 0.0))
                    ch.do(v.memset(k0[:, :, :, 3 * D0:SLOT0], 0.0))
                    ch.do(v.memset(v0[:, :, :, D0:D0 + 1], 1.0), sem("stack_zeros"))
                    ch.sync()
                    ch.do(v.memset(ast[:, :, 3:6], 1.0))
                    ch.do(v.memset(mst[:, :, 0:3], 1.0))
                    ch.do(v.memset(ones[:, :], 1.0), sem("ones_ready"))
                elif stage == "x0_split":
                    if b == 0:
                        ch.do(v.memset(qs[:, :, :, 3 * DA:4 * DA], 0.0))
                        ch.do(v.memset(ks[:, :, :, 3 * DA + 2:4 * DA], 0.0))
                        ch.do(v.memset(ks[:, :, :, 3 * DA:3 * DA + 2], 1.0))
                    qq = q0[:, b % 2, :, :]
                    zb = z[:, b, :].rearrange("p (h d) -> p h d", h=H0)
                    if b >= 2:
                        dve.wait_ge(sem("x0_stacked"), b - 1)
                    twice(qq[:, :, 0:2 * D0].rearrange("p h (s d) -> p h s d", d=D0), zb, H0)
                    ch.sync()
                    ch.do(tt(qq[:, :, 2 * D0:3 * D0], zb, qq[:, :, 0:D0], ALU.subtract), sem("q0_ready"))
                elif stage == "w1":
                    ch.do(v.tensor_reduce(cmean[:, :], cT[:, :, :], AX.X, ALU.add))
                    ch.sync()
                    ch.do(ts(cmean[:, :], cmean[:, :], 1.0 / P, None, ALU.mult))
                    ch.sync()
                    ch.do(v.tensor_copy(cmeanB[:, :, :], bc(cmean[:, :].unsqueeze(2), [P, NB, P])), sem("cmean_ready"))
                elif stage == "w8":
                    if b == 0:
                        loaded(dve, "l1")
                    w = wq8[:, b, :, :].rearrange("p c (n k) -> p (c n) k", k=32)
                    ch.do(v.tensor_reduce(w8s[:, b, :], w, AX.X, ALU.max, apply_absolute_value=True))
                    ch.sync()
                    ch.do(ts(w8s[:, b, :], w8s[:, b, :], 1.0 / QMAX4, 1e-12, ALU.mult, ALU.max))
                    ch.sync()
                    ch.do(v.reciprocal(w8r[:, b, :], w8s[:, b, :]))
                    ch.sync()
                    ch.do(tt(w, w, bc(w8r[:, b, :].unsqueeze(2), [P, 12, 32]), ALU.mult))
                    ch.sync()
                    ch.do(ts(w, w, MAGIC, -MAGIC, ALU.add, ALU.add))
                    ch.sync()
                    ch.do(tt(w, w, bc(w8s[:, b, :].unsqueeze(2), [P, 12, 32]), ALU.mult), sem("w8_ready"))
                elif stage == "x0_norm":
                    if b == 0:
                        loaded(dve, "x")
                    norm_stats(x[:, b, :], b)
                elif stage in ("x1_norm", "x3_norm"):
                    norm_stats(x[:, b, :], b)
                elif stage in Z_STAGES:
                    normalise(stage, z[:, b, :], x[:, b, :], b, sem(stage))
                elif stage == "x0_forget":
                    u = get("x0_gate", 0, "gates")[:, 0:2 * NB * H0].rearrange("p (b g) -> p b g", b=NB)
                    loaded(dve, "x0")
                    ch.do(tt(gi[:, :, :], u[:, :, 0:H0], bc(ifb[:, 0:H0].unsqueeze(1), [P, NB, H0]), ALU.add))
                    ch.do(tt(gf[:, :, :], u[:, :, H0:2 * H0], bc(ifb[:, H0:2 * H0].unsqueeze(1), [P, NB, H0]), ALU.add),
                          free_of("x0_gate", 0, "gates"))
                    ch.sync()
                    ch.do(stt(ga[:, :, :], gf[:, :, :], -1.0, gf[:, :, :], ALU.mult, ALU.max), sem("abs_f"))
                    dve.wait_ge(sem("softplus"), 1)
                    ch.do(stt(gf[:, :, :], gf[:, :, :], 0.0, gb[:, :, :], ALU.min, ALU.subtract), sem("log_forget"))
                    u = get(stage, 0, "csum")[:, 0:NB * H0].rearrange("p (b h) -> p b h", b=NB)
                    ch.do(v.tensor_copy(cs[:, :, :], u))
                    ch.do(tt(ga[:, :, :], gi[:, :, :], u, ALU.subtract), free_of(stage, 0, "csum"))
                    ch.sync()
                    dve.sem_inc(sem("a_ready"), 1)
                    u = get(stage, 0, "at")
                    ch.do(v.tensor_copy(aT[:, :], u[0:NB * H0, 0:P]), free_of(stage, 0, "at"))
                    ch.sync()
                    ch.do(v.tensor_tensor_scan(mT[:, :], aT[:, :], aT[:, :], -3.0e38, ALU.max, ALU.max), sem("mT_ready"))
                    u = get(stage, 0, "m")[:, 0:NB * H0].rearrange("p (b h) -> p b h", b=NB)
                    ch.do(ts(mm[:, :, :], u, -1.0, None, ALU.mult))
                    ch.do(tt(gb[:, :, :], cs[:, :, :], u, ALU.add), free_of(stage, 0, "m"))
                    ch.sync()
                    dve.sem_inc(sem("md_ready"), 1)
                    for src, st, o in ((ga, ast, 0), (mm, mst, 3)):
                        s2 = src[:, :, :].rearrange("p b h -> p (b h)")
                        ch.do(v.tensor_copy(st[:, :, o], s2))
                        ch.sync()
                        ch.do(tt(s2, s2, st[:, :, o], ALU.subtract))
                        ch.sync()
                        ch.do(v.tensor_copy(st[:, :, o + 1], s2))
                        ch.sync()
                        ch.do(tt(st[:, :, o + 2], s2, st[:, :, o + 1], ALU.subtract), sem("am_ready") if o else None)
                elif stage == "x0_score":
                    if b >= 2:
                        dve.wait_ge(sem("cc_used"), b - 1)
                    for j in range(2):
                        dve.wait_ge(sem("dec_ready"), 2 * b + j + 1)
                        u = get(stage, b, f"s{j}").rearrange("p (h q) -> p h q", h=4)
                        ch.do(stt(cc[:, b % 2, :, :].rearrange("p (i g) q -> p g i q", g=2)[:, j], u, D0 ** -0.5, dec[:, j, :, :], ALU.mult, ALU.mult),
                              free_of(stage, b, f"s{j}"))
                        ch.sync()
                        dve.sem_inc(sem("cc_ready"), 1)
                elif stage == "x0_value":
                    u = get(stage, b, "u")[:, 0:H0 * (D0 + 1)].rearrange("p (h d) -> p h d", h=H0)
                    dve.sem_inc(sem("cc_used"), 1)
                    if b == 0:
                        dve.wait_ge(sem("floor_ready"), 1)
                    ch.do(v.tensor_reduce(nrm[:, :], u[:, :, D0:D0 + 1], AX.X, ALU.max, apply_absolute_value=True))
                    ch.sync()
                    ch.do(tt(nrm[:, :], nrm[:, :], floor[:, b, :], ALU.max))
                    ch.sync()
                    ch.do(ts(nrm[:, :], nrm[:, :], 1e-6, None, ALU.add))
                    ch.sync()
                    ch.do(v.reciprocal(nrm[:, :], nrm[:, :]))
                    ch.sync()
                    h3d = hh[:, b, :].rearrange("p (h d) -> p h d", h=H0)
                    ch.do(tt(h3d, u[:, :, 0:D0], bc(nrm[:, :].unsqueeze(2), [P, H0, D0]), ALU.mult), free_of(stage, b, "u"))
                    ch.sync()
                    ch.do(v.tensor_reduce(hm[:, :], h3d, AX.X, ALU.add))
                    ch.sync()
                    ch.do(ts(hm[:, :], hm[:, :], 1.0 / D0, None, ALU.mult))
                    ch.sync()
                    ch.do(tt(h3d, h3d, bc(hm[:, :].unsqueeze(2), [P, H0, D0]), ALU.subtract))
                    ch.sync()
                    ch.do(tt(sq[:, :], hh[:, b, :], hh[:, b, :], ALU.mult))
                    ch.sync()
                    ch.do(v.tensor_reduce(hv[:, b, :], sq[:, :].rearrange("p (h d) -> p h d", h=H0), AX.X, ALU.add))
                    ch.sync()
                    ch.do(ts(hv[:, b, :], hv[:, b, :], 1.0 / D0, 1e-5, ALU.mult, ALU.add), sem("hv_ready"))
                elif stage == "x0_group":
                    if b == 0:
                        loaded(dve, "rows")
                        dve.wait_ge(sem("tg_ready"), 1)
                    dve.wait_ge(sem("hr_ready"), b + 1)
                    h3d = hh[:, b, :].rearrange("p (h d) -> p h d", h=H0)
                    ch.do(tt(h3d, h3d, bc(hr[:, b, :].unsqueeze(2), [P, H0, D0]), ALU.mult))
                    ch.sync()
                    ch.do(tt(hh[:, b, :], hh[:, b, :], vec("L0_xattn_gn_w"), ALU.mult))
                    ch.sync()
                    ch.do(tt(hh[:, b, :], hh[:, b, :], vec("L0_xattn_gn_b"), ALU.add))
                    ch.sync()
                    ch.do(stt(x[:, b, :], hh[:, b, :], tg[:, 0:1], x[:, b, :], ALU.mult, ALU.add))
                    ch.sync()
                    norm_stats(x[:, b, :], b)
                elif stage in ("f0_route", "f2_route", "f3_route"):
                    n = {"f0_route": 1, "f2_route": 2, "f3_route": 3}[stage]
                    name = "logit"
                    u = get(stage, 0, name)[:, 0:NB * NE].rearrange("p (b e) -> p b e", b=NB)
                    if n < 3:
                        ch.do(v.tensor_reduce(top[:, :, 0], u, AX.X, ALU.max))
                        ch.sync()
                        ch.do(tt(lg[:, :, :], u, bc(top[:, :, :], [P, NB, NE]), ALU.subtract), free_of(stage, 0, name))
                    else:
                        ch.do(v.tensor_copy(lg[:, :, :], u), free_of(stage, 0, name))
                    ch.sync()
                    dve.sem_inc(sem("logit_ready"), 1)
                    dve.wait_ge(sem("route_exp"), n)
                    if n < 3:
                        ch.do(v.tensor_reduce(gsum[:, :, 0], pr[:, :, :], AX.X, ALU.add))
                        ch.sync()
                        ch.do(v.reciprocal(gsum[:, :, :], gsum[:, :, :]))
                        ch.sync()
                        ch.do(tt(pr[:, :, :], pr[:, :, :], bc(gsum[:, :, :], [P, NB, NE]), ALU.mult))
                    else:
                        loaded(dve, "l3")
                        ch.do(ts(pr[:, :, :], pr[:, :, :], 1.0, None, ALU.add))
                        ch.sync()
                        ch.do(v.reciprocal(pr[:, :, :], pr[:, :, :]))
                        ch.sync()
                        ch.do(ts(pr[:, :, :], pr[:, :, :], rscale[:, 0:1], None, ALU.mult))
                    top2()
                    if n == 1:
                        u = get(stage, 0, "cum")[:, 0:2 * NB * NE].rearrange("p (k b e) -> p k b e", k=2, b=NB)
                        w = get(stage, 0, "total")[:, 0:2 * NB * NE].rearrange("p (k b e) -> p k b e", k=2, b=NB)
                        for k in range(2):
                            ch.do(v.tensor_copy(tot[:, k * NE:(k + 1) * NE, :], w[:, k, :, :].rearrange("p b e -> p e b")),
                                  free_of(stage, 0, "total") if k else None)
                            ch.do(v.tensor_copy(cum[:, k, :, :], u[:, k, :, :]), free_of(stage, 0, "cum") if k else None)
                        ch.sync()
                        dve.wait_ge(*free_of(stage, 0, "total"))
                        ch.do(v.tensor_tensor_scan(inc[:, :, :].rearrange("p e b -> p (e b)"), reset[:, :, :].rearrange("p e b -> p (e b)"),
                                                   tot[:, :, :].rearrange("p e b -> p (e b)"), 0.0, ALU.mult, ALU.add))
                        ch.sync()
                        ch.do(tt(tot[:, :, :], inc[:, :, :], tot[:, :, :], ALU.subtract))
                        ch.sync()
                        ch.do(tt(tot[:, NE:2 * NE, :], tot[:, NE:2 * NE, :], bc(inc[:, 0:NE, NB - 1:NB], [P, NE, NB]), ALU.add))
                        ch.sync()
                        for k in range(2):
                            ch.do(tt(cum[:, k, :, :], cum[:, k, :, :], tot[:, k * NE:(k + 1) * NE, :].rearrange("p e b -> p b e"), ALU.add))
                        ch.sync()
                        ch.do(stt(oh[:, :, :, :].rearrange("p k b e -> p (k b e)"), cum[:, :, :, :].rearrange("p k b e -> p (k b e)"),
                                  CAP + 0.5, oh[:, :, :, :].rearrange("p k b e -> p (k b e)"), ALU.is_lt, ALU.mult))
                    ch.sync()
                    ch.do(tt(gate[:, :, :], oh[:, 0, :, :], oh[:, 1, :, :], ALU.add))
                    ch.sync()
                    ch.do(tt(gate[:, :, :], gate[:, :, :], pr[:, :, :], ALU.mult))
                    ch.sync()
                    ch.do(v.tensor_reduce(gsum[:, :, 0], gate[:, :, :], AX.X, ALU.add))
                    ch.sync()
                    if n == 1:
                        ch.do(ts(gsum[:, :, :], gsum[:, :, :], 1e-9, None, ALU.max))
                    elif n == 2:
                        ch.do(ts(gsum[:, :, :], gsum[:, :, :], 1e-6, None, ALU.add))
                    ch.sync()
                    ch.do(v.reciprocal(gsum[:, :, :], gsum[:, :, :]))
                    ch.sync()
                    ch.do(tt(gate[:, :, :], gate[:, :, :], bc(gsum[:, :, :], [P, NB, NE]), ALU.mult), sem("gate_ready"))
                elif stage in ("f0_up", "f2_up"):
                    e, g = b
                    n = (0 if stage == "f0_up" else NE * FPS) + e * FPS + g
                    for k in range(2):
                        dve.wait_ge(sem("act_ready"), 2 * n + k + 1)
                        if n >= 2:
                            dve.wait_ge(sem("hid_used"), n - 1)
                        u = get(stage, b, f"g{k}")
                        ch.do(tt(hid[:, n % 2, k, :], act[:, n % 2, k, :], u, ALU.mult), free_of(stage, b, f"g{k}"))
                        ch.sync()
                        dve.sem_inc(sem("hid_ready"), 1)
                elif stage in ("f0_down", "f2_down"):
                    e, g = b
                    u = get(stage, b, "u")
                    dve.sem_inc(sem("hid_used"), 1)
                    for j in range(4):
                        bb = 4 * g + j
                        s = gate[:, bb, e:e + 1]
                        ps = u[:, j * D:(j + 1) * D]
                        fr = free_of(stage, b, "u") if j == 3 else None
                        if e == 0:
                            ch.do(ts(acc[:, bb, :], ps, s, None, ALU.mult), fr)
                        else:
                            ch.do(stt(acc[:, bb, :], ps, s, acc[:, bb, :], ALU.mult, ALU.add), fr)
                    ch.sync()
                    if e == NE - 1:
                        k = 4 if stage == "f0_down" else 6
                        ch.do(stt(x[:, 4 * g:4 * g + 4, :], acc[:, 4 * g:4 * g + 4, :], tg[:, k:k + 1], x[:, 4 * g:4 * g + 4, :], ALU.mult, ALU.add))
                        ch.sync()
                elif stage == "x1_out":
                    u = get(stage, b, "u")
                    ch.do(tt(t1[:, b, :], u[:, 0:D], vec("L1_xattn_b"), ALU.add), free_of(stage, b, "u"))
                    ch.sync()
                    ch.do(stt(x[:, b, :], t1[:, b, :], tg[:, 1:2], x[:, b, :], ALU.mult, ALU.add))
                    ch.sync()
                    norm_stats(x[:, b, :], b)
                elif stage == "f1_scale":
                    ch.sync()
                    ch.do(v.tensor_reduce(mx[:, 0:1], z[:, :, :].rearrange("p b d -> p (b d)"), AX.X, ALU.max, apply_absolute_value=True), sem("mx_ready"))
                    global_scale(0, "x", 1, stage)
                    dve.wait_ge(sem("f1_zT"), NB)
                    quantise(xq[:, :], zT[:, :, :].rearrange("p b q -> p (b q)"), 0, sem("xq_ready"))
                elif stage == "f1_up":
                    cch, g = b
                    ch.do(v.tensor_copy(up[:, cch, g * BANK:(g + 1) * BANK], get(stage, b, "up")), free_of(stage, b, "up"))
                    ch.do(v.tensor_copy(gt[:, cch, g * BANK:(g + 1) * BANK], get(stage, b, "gate")), free_of(stage, b, "gate"))
                elif stage == "f1_mid":
                    ch.sync()
                    flat = [s[:, :, :].rearrange("p c q -> p (c q)") for s in (up, gt, sg)]
                    u_, g_, s_ = flat
                    ch.do(v.tensor_reduce(mx[:, 0:1], u_, AX.X, ALU.max, apply_absolute_value=True))
                    ch.do(v.tensor_reduce(mx[:, 1:2], g_, AX.X, ALU.max, apply_absolute_value=True), sem("mx_ready"))
                    global_scale(1, "ug", 2, stage)
                    quantise(g_, g_, 1, sem("gateq_ready"))
                    quantise(u_, u_, 0)
                    dve.wait_ge(sem("sig_ready"), 1)
                    ch.do(ts(s_, s_, 65536.0, MAGIC, ALU.mult, ALU.add))
                    ch.sync()
                    ch.do(ts(s_, s_, MAGIC + 65535.0, MAGIC, ALU.min, ALU.max))
                    ch.sync()
                    ch.do(ts(s_, s_, -MAGIC, 1.0 / 65536.0, ALU.add, ALU.mult))
                    ch.sync()
                    ch.do(tt(g_, g_, s_, ALU.mult))
                    ch.sync()
                    ch.do(v.tensor_reduce(mx[:, 0:1], g_, AX.X, ALU.max, apply_absolute_value=True), sem("mx_ready"))
                    global_scale(2, "gs", 1, stage)
                    quantise(g_, g_, 0)
                    ch.sync()
                    ch.do(tt(s_, g_, u_, ALU.mult))
                    ch.sync()
                    ch.do(v.tensor_reduce(mx[:, 0:1], s_, AX.X, ALU.max, apply_absolute_value=True), sem("mx_ready"))
                    global_scale(3, "o", 1, stage)
                    quantise(s_, s_, 0, sem("o_ready"))
                elif stage == "f1_down":
                    u = get(stage, b, "u")
                    ch.do(stt(x[:, b, :], u[:, 0:D], tg[:, 5:6], x[:, b, :], ALU.mult, ALU.add), free_of(stage, b, "u"))
                    ch.sync()
                    norm_stats(x[:, b, :], b)
                elif stage in ("a_kv", "b_kv", "c_kv"):
                    m = stage[0]
                    if m == "a" and b == 0:
                        dve.wait_ge(sem("v9_ones"), 1)
                    u = get(stage, b, "qkv")
                    f = free_of(stage, b, "qkv")
                    if m == "c":
                        w = q32[:, b % 2, :, :]
                        ch.do(tt(w, u[:, 0:3 * D].rearrange("p (i d) -> p i d", i=3), bqkv[:, :, :], ALU.add), f)
                        ch.sync()
                        q_, k_, v_ = (w[:, i, :] for i in range(3))
                        split_q(m, b, q_, 0)
                        split_q(m, b, k_, 1)
                        ch.do(v.tensor_copy(v9[:, b, :, 0:DA], v_.rearrange("p (h d) -> p h d", h=HA)), sem("c_stacks"))
                    else:
                        q_, k_, v_ = (u[:, i * D:(i + 1) * D] for i in range(3))
                        if m == "a":
                            split_q(m, b, q_, 0)
                        split_q(m, b, k_, 1)
                        ch.do(v.tensor_copy(v9[:, b, :, 0:DA], v_.rearrange("p (h d) -> p h d", h=HA)), f)
                        ch.sync()
                        dve.sem_inc(sem(m + "_stacks"), 1)
                elif stage == "b_q":
                    u = get(stage, b, "q")
                    split_q("b", b, u[:, 0:D], 0, free_of(stage, b, "q"))
                    ch.sync()
                    dve.sem_inc(sem("b_qs"), 1)
                elif stage in ("a_max", "b_max", "c_max"):
                    m = stage[0]
                    for j in range(4):
                        u = get(stage, b, f"s{j}").rearrange("p (h k) -> p h k", h=4)
                        ch.do(v.tensor_reduce(nmax[:, b, :].rearrange("p (i g) -> p g i", g=4)[:, j], u, AX.X, ALU.max, negate=True), free_of(stage, b, f"s{j}"))
                    ch.sync()
                    for j in range(3):
                        dve.wait_ge(*free_of(stage, b, f"s{j}"))
                    ch.do(v.tensor_copy(qs[:, b, :, 3 * DA], nmax[:, b, :]))
                    ch.sync()
                    ch.do(tt(qs[:, b, :, 3 * DA + 1], nmax[:, b, :], qs[:, b, :, 3 * DA], ALU.subtract), sem(m + "_negmax"))
                elif stage in ("a_av", "b_av", "c_av"):
                    m = stage[0]
                    u = get(stage, b, "av")[:, 0:HA * (DA + 1)].rearrange("p (h d) -> p h d", h=HA)
                    dve.sem_inc(sem("pt_used"), 1)
                    ch.do(v.reciprocal(rden[:, :], u[:, :, DA]))
                    ch.sync()
                    ch.do(tt(at[:, b, :].rearrange("p (h d) -> p h d", h=HA), u[:, :, 0:DA], bc(rden[:, :].unsqueeze(2), [P, HA, DA]), ALU.mult),
                          free_of(stage, b, "av"))
                    ch.sync()
                    dve.sem_inc(sem(m + "_at"), 1)
                elif stage in ("a_wo", "b_wo"):
                    m = stage[0]
                    u = get(stage, b, "wo")
                    ch.do(tt(t2[:, b, :], u[:, 0:D], vec("L2_xattn_bo1" if m == "a" else "L2_xattn_bo2"), ALU.add), free_of(stage, b, "wo"))
                    ch.sync()
                    if m == "a":
                        ch.do(stt(t2[:, b, :], t2[:, b, :], 0.0, z[:, b, :], ALU.max, ALU.add))
                    else:
                        ch.do(ts(t2[:, b, :], t2[:, b, :], 0.0, 2.0, ALU.max, ALU.mult))
                    ch.sync()
                    norm_stats(t2[:, b, :], b)
                elif stage in ("a_norm", "b_norm"):
                    m = stage[0]
                    normalise(stage, t1[:, b, :], t2[:, b, :], b, None)
                    ch.sync()
                    g_, b_ = ("L2_xattn_g1", "L2_xattn_b1") if m == "a" else ("L2_xattn_g2", "L2_xattn_b2")
                    ch.do(tt(t1[:, b, :], t1[:, b, :], vec(g_), ALU.mult))
                    ch.sync()
                    ch.do(tt(t1[:, b, :], t1[:, b, :], vec(b_), ALU.add), sem(m + "_out"))
                elif stage == "b_f":
                    u = get(stage, b, "f")
                    ch.do(tt(t2[:, b, :], u[:, 0:D], vec("L2_xattn_bf"), ALU.add), free_of(stage, b, "f"))
                    ch.sync()
                    ch.do(stt(t2[:, b, :], t2[:, b, :], 0.0, t1[:, b, :], ALU.max, ALU.add))
                    ch.sync()
                    norm_stats(t2[:, b, :], b)
                elif stage == "b_last":
                    normalise(stage, t1[:, b, :], t2[:, b, :], b, None)
                    ch.sync()
                    ch.do(tt(t1[:, b, :], t1[:, b, :], vec("L2_xattn_g3"), ALU.mult))
                    ch.sync()
                    ch.do(tt(t1[:, b, :], t1[:, b, :], vec("L2_xattn_b3"), ALU.add))
                    ch.sync()
                    ch.do(stt(x[:, b, :], t1[:, b, :], tg[:, 2:3], x[:, b, :], ALU.mult, ALU.add))
                    ch.sync()
                    norm_stats(x[:, b, :], b)
                elif stage == "c_wo":
                    u = get(stage, b, "wo")
                    ch.do(tt(t2[:, b, :], u[:, 0:D], vec("L3_xattn_bo"), ALU.add), free_of(stage, b, "wo"))
                    ch.sync()
                    ch.do(stt(x[:, b, :], t2[:, b, :], tg[:, 3:4], x[:, b, :], ALU.mult, ALU.add))
                    ch.sync()
                    norm_stats(x[:, b, :], b)
                elif stage == "f3_up":
                    for k in range(4):
                        dve.wait_ge(sem("h3_ready"), 5 * b + k + 1)
                        u = get(stage, b, f"gate{k}")
                        ch.do(tt(h3[:, k, :], h3[:, k, :], u, ALU.mult), free_of(stage, b, f"gate{k}"))
                        ch.sync()
                        dve.sem_inc(sem("h3_gated"), 1)
                elif stage == "f3_down":
                    u = get(stage, b, "o").rearrange("p (j d) -> p j d", j=4)
                    dve.sem_inc(sem("f3_stored"), 1)
                    ch.do(tt(t2[:, 4 * b:4 * b + 4, :], u, bc(vec("L3_ffn_bs2").unsqueeze(1), [P, 4, D]), ALU.add), free_of(stage, b, "o"))
                    ch.sync()
                    for j in range(4):
                        bb = 4 * b + j
                        ch.do(stt(x[:, bb, :], t2[:, bb, :], tg[:, 7:8], x[:, bb, :], ALU.mult, ALU.add), sem("x_final"))


_INS = ["x", "ctx_1024", "g_xattn", "g_ffn", "L0_xattn_Wi_w", "L0_xattn_Wi_b", "L0_xattn_Wf_w", "L0_xattn_Wf_b",
        "L0_xattn_gn_w", "L0_xattn_gn_b", "L0_ffn_Wg", "L0_ffn_W_in", "L0_ffn_W_out", "L1_xattn_W", "L1_xattn_b",
        "L1_ffn_w_gate", "L1_ffn_w_up", "L1_ffn_w_down", "L2_xattn_Wk1", "L2_xattn_Wv1", "L2_xattn_Wq1",
        "L2_xattn_Wo1", "L2_xattn_bo1", "L2_xattn_Wk2", "L2_xattn_Wv2", "L2_xattn_Wq2", "L2_xattn_Wo2",
        "L2_xattn_bo2", "L2_xattn_Wf", "L2_xattn_bf", "L2_xattn_g1", "L2_xattn_b1", "L2_xattn_g2", "L2_xattn_b2",
        "L2_xattn_g3", "L2_xattn_b3", "L2_ffn_router_w", "L2_ffn_w13", "L2_ffn_w2", "L3_xattn_Wq", "L3_xattn_bq",
        "L3_xattn_Wk", "L3_xattn_bk", "L3_xattn_Wv", "L3_xattn_bv", "L3_xattn_Wo", "L3_xattn_bo", "L3_ffn_gate_W",
        "L3_ffn_W1", "L3_ffn_b1", "L3_ffn_W2", "L3_ffn_b2", "L3_ffn_Ws1", "L3_ffn_bs1", "L3_ffn_Ws2",
        "L3_ffn_bs2", "L3_ffn_route_scale"]


def kernel(**inputs):
    import numpy as _np
    import concourse.bacc as _bacc
    from concourse import mybir as _mybir
    from concourse.bass_utils import run_bass_kernel_spmd as _run

    nc = _bacc.Bacc("TRN2", target_bir_lowering=False, num_devices=1)
    arrays, tensors = {}, {}
    for name in _INS:
        a = _np.ascontiguousarray(inputs[name])
        if a.ndim == 0:
            a = a.reshape(1)
        arrays[f"in_{name}"] = a
        tensors[name] = nc.dram_tensor(f"in_{name}", a.shape, _mybir.dt.from_np(a.dtype), kind="ExternalInput").ap()
    tensors["out"] = nc.dram_tensor("out", (8, 128, 128), _mybir.dt.float32, kind="ExternalOutput").ap()
    gated_stack(nc, tensors)
    r = _run(nc, [arrays], core_ids=[0])
    return r.results[0]["out"]
```

```python
from contextlib import ExitStack

import concourse.bass as bass
from concourse import mybir

F32 = mybir.dt.float32
F16 = mybir.dt.float16
BF16 = mybir.dt.bfloat16
ALU = mybir.AluOpType
ACT = mybir.ActivationFunctionType
AX = mybir.AxisListType

NB = 8
P = 128
D = 128
NE = 8
F = 256
CAP = 320
I1 = 384
H0, D0 = 8, 16
HA, DA = 16, 8
SLOT0, SLOTA = 64, 32
PSUM_BANKS, BANK = 8, 512
MASKED = -1.0e30
MAGIC = 12582912.0
QMAX = 32767.0
QMAX4 = 7.0
FPS = 2
HALF = 4


NORMS = {"x0_norm": 1e-5, "x0_group": 1e-5, "x1_norm": 1e-5, "x1_out": 1e-5, "f1_down": 1e-5, "a_wo": 1e-6,
         "b_wo": 1e-6, "b_f": 1e-6, "b_last": 1e-5, "x3_norm": 1e-5, "c_wo": 1e-5}
NORM_OF = {"x0_z": "x0_norm", "f0_z": "x0_group", "x1_z": "x1_norm", "f1_z": "x1_out", "x2_z": "f1_down",
           "a_norm": "a_wo", "b_norm": "b_wo", "b_last": "b_f", "f2_z": "b_last", "x3_z": "x3_norm", "f3_z": "c_wo"}
Z_STAGES = ("x0_z", "f0_z", "x1_z", "f1_z", "x2_z", "f2_z", "x3_z", "f3_z")
T_STAGES = tuple(s[:2] + "_t" for s in Z_STAGES)


ATT = ["stack", "max", "again", "exp", "av", "wt"]
CHAINS = {
    "n0": ["x0_norm", "x0_z", "x0_t", "x0_gate"],
    "fg": ["x0_forget"],
    "s0": ["split0"],
    "w1": ["w1"],
    "w8": ["w8"],
    "x0": ["x0_split", "x0_stack", "x0_score", "x0_cut", "x0_value", "x0_group", "f0_z", "f0_t"],
    "r0": ["f0_route"],
    "rt": ["router"],
    "s2": ["split2"],
    "f0": ["f0_up", "f0_cut", "f0_down"],
    "so": ["split_out"],
    "x1": ["x1_norm", "x1_z", "x1_t", "x1_out", "f1_z", "f1_t"],
    "q1": ["f1_scale"],
    "u1": ["f1_up"],
    "g1": ["f1_gate", "f1_prod", "f1_out"],
    "x2": ["f1_down", "x2_z", "x2_t", "a_kv"] + ["a_" + s for s in ATT[:-1]] + ["b_kv", "a_wt", "a_wo", "a_norm", "b_qt", "b_q"]
          + ["b_" + s for s in ATT] + ["b_wo", "b_norm", "b_ft", "b_f", "b_last", "f2_z", "f2_t"],
    "r2": ["f2_route"],
    "f2": ["f2_up", "f2_cut", "f2_down"],
    "x3": ["x3_norm", "x3_z", "x3_t", "c_kv"] + ["c_" + s for s in ATT] + ["c_wo", "f3_z", "f3_t"],
    "r3": ["f3_route", "f3_up", "f3_gt", "f3_gate", "f3_down"],
}
BATCHES = [(b, b, b // HALF) for b in range(NB)]
EXPERTS = [((e, g), e, g) for g in range(FPS) for e in range(NE)]
HALVES = [(g, 0, g) for g in range(FPS)]
ITEMS = {
    "n0": BATCHES, "x0": BATCHES, "x1": BATCHES, "x2": BATCHES, "x3": BATCHES, "f0": EXPERTS, "f2": EXPERTS,
    "r2": HALVES, "r3": HALVES,
    "s0": [(e, e, 0) for e in range(NE)], "so": [(e, e, 0) for e in range(NE)], "s2": [(e, e, 0) for e in range(NE)],
    "w8": [(i, i, 0) for i in range(3)], "u1": [((c, g), FPS * c + g, 0) for c in range(3) for g in range(FPS)],
}
START = {
    "x0_norm": -6.97, "x0_z": -3.11, "x0_t": -1.76, "x0_gate": -0.54,
    "x0_forget": 13.47,
    "split0": 18.08,
    "w1": 26.45,
    "w8": 22.32,
    "x0_split": 12.8, "x0_stack": 13.8, "x0_score": 14.8, "x0_cut": 15.8, "x0_value": 16.8, "x0_group": 17.8,
    "f0_z": 18.8, "f0_t": 20.98,
    "f0_route": 28.19,
    "router": 33.32,
    "split2": 28.54,
    "f0_up": 30.5, "f0_cut": 31.0, "f0_down": 33.1,
    "split_out": 54.81,
    "x1_norm": 50.86, "x1_z": 52.25, "x1_t": 53.06, "x1_out": 53.89, "f1_z": 55.06, "f1_t": 56.06,
    "f1_scale": 72.66,
    "f1_up": 72.91,
    "f1_gate": 76.74, "f1_prod": 78.7, "f1_out": 79.67,
    "f1_down": 90.28, "x2_z": 91.56, "x2_t": 92.59, "a_kv": 93.59, "a_stack": 94.59, "a_max": 95.67,
    "a_again": 97.09, "a_exp": 98.02, "a_av": 99.59, "b_kv": 101.09, "a_wt": 102.09, "a_wo": 103.09,
    "a_norm": 104.09, "b_qt": 105.09, "b_q": 106.15, "b_stack": 107.03, "b_max": 108.13, "b_again": 109.63,
    "b_exp": 110.63, "b_av": 112.15, "b_wt": 113.56, "b_wo": 114.33, "b_norm": 115.56, "b_ft": 116.56,
    "b_f": 117.56, "b_last": 118.45, "f2_z": 119.56, "f2_t": 120.56,
    "f2_route": 125.8,
    "f2_up": 126.03, "f2_cut": 126.88, "f2_down": 128.65,
    "x3_norm": 142.38, "x3_z": 143.38, "x3_t": 144.21, "c_kv": 145.38, "c_stack": 146.38, "c_max": 147.22,
    "c_again": 148.88, "c_exp": 149.81, "c_av": 151.33, "c_wt": 152.79, "c_wo": 153.88, "f3_z": 154.84,
    "f3_t": 155.88,
    "f3_route": 165.8, "f3_up": 166.32, "f3_gt": 166.88, "f3_gate": 173.33, "f3_down": 174.1,
}
PERIOD = {"n0": 1.0, "s0": 0.79, "w8": 1.1, "x0": 1.0, "s2": 1.07, "f0": 2.0,
          "so": 0.5, "x1": 0.49, "u1": 0.62, "x2": 1.26, "f2": 1.95, "x3": 1.44}
GAP = {"f0": 7.63, "x1": 11.6, "x2": 0.94, "r2": 6.75, "f2": 7.64, "x3": 2.18, "r3": 5.17}


def schedule():
    steps = []
    for phase, names in CHAINS.items():
        for s, name in enumerate(names):
            for item, turn, half in ITEMS.get(phase, [(0, 0, 0)]):
                place = START[name] + turn * PERIOD.get(phase, 0.0) + half * GAP.get(phase, 0.0)
                steps.append((place, -s, name, item))
    return [("setup", 0)] + [(name, item) for _, _, name, item in sorted(steps, key=lambda step: step[:2])]


UNITS = {
    "setup": ["ctx0", "ctx1", "gate_w"], "w1": ["u"], "w8": ["u"], "router": ["u"],
    "x0_forget": ["csum", "at", "m"], "x0_stack": ["qk", "am"], "x0_score": ["e0", "e1", "s0", "s1"],
    "x0_value": ["u"], "f0_route": ["logit", "cum", "total"], "x1_out": ["u"], "f1_scale": ["t", "b"],
    "f1_up": ["up", "gate"], "f1_gate": ["t", "b"], "f1_prod": ["t", "b"], "f1_out": ["t", "b"], "f1_down": ["u"],
    "b_qt": ["t"], "b_q": ["q"], "b_ft": ["t"], "b_f": ["f"], "f2_route": ["logit"],
    "f3_route": ["logit"], "f3_gt": ["gt"], "f3_up": [f"h{k}" for k in range(5)],
    "f3_gate": [f"gate{k}" for k in range(4)],
    "f3_down": ["o"],
}
UNITS |= {t: ["u"] for t in T_STAGES}
UNITS |= {f + "_up": ["a0", "g0", "a1", "g1"] for f in ("f0", "f2")} | {f + "_down": ["u"] for f in ("f0", "f2")}
for _m in "abc":
    UNITS |= {_m + "_kv": ["qkv"], _m + "_stack": ["qk"], _m + "_max": [f"s{i}" for i in range(4)],
              _m + "_again": ["q"], _m + "_exp": [f"t{i}" for i in range(4)], _m + "_av": ["av"],
              _m + "_wt": ["t"], _m + "_wo": ["wo"]}


def psum_units(stage, item):
    if stage == "x0_gate":
        return ["gates"] if item == 0 else []
    return UNITS.get(stage, [])


class Banks:

    def __init__(self, order, psum, full, free):
        self.psum, self.full, self.free = psum, full, free
        self.place = {}
        n = 0
        for stage, item in order:
            for name in psum_units(stage, item):
                self.place[stage, item, name] = (n % PSUM_BANKS, n // PSUM_BANKS)
                n += 1

    def tile(self, *key):
        k, _ = self.place[key]
        return self.psum[:, k * BANK:(k + 1) * BANK]

    def take(self, pe, *key):
        k, turn = self.place[key]
        if turn:
            pe.wait_ge(self.free[k], turn)
        return self.psum[:, k * BANK:(k + 1) * BANK]

    def freed(self, *key):
        k, turn = self.place[key]
        return self.free[k], turn + 1

    def fill(self, ins, *key):
        ins.then_inc(self.full[self.place[key][0]], 1)

    def get(self, eng, *key):
        k, turn = self.place[key]
        eng.wait_ge(self.full[k], turn + 1)
        return self.psum[:, k * BANK:(k + 1) * BANK]


class Chain:

    def __init__(self, eng, own):
        self.eng, self.own, self.count, self.last = eng, own, {}, None

    def do(self, ins, sem=None):
        sem = self.own if sem is None else sem
        if isinstance(sem, tuple):
            ins.then_inc(sem[0], 1)
            self.last = sem
            return
        ins.then_inc(sem, 1)
        n = self.count[sem.name] = self.count.get(sem.name, 0) + 1
        self.last = (sem, n)

    def sync(self):
        self.eng.wait_ge(*self.last)


def bc(ap, shape):
    return ap.to_broadcast(list(shape))


def gated_stack(nc, t):
    order = schedule()
    with ExitStack() as ctx:
        def sb(name, shape, dt=F32):
            return ctx.enter_context(nc.sbuf_tensor(name, shape, dt))

        sems = {}

        def sem(name):
            if name not in sems:
                sems[name] = ctx.enter_context(nc.semaphore(name))
            return sems[name]

        x = sb("x", [P, NB, D])
        z = sb("z", [P, NB, D])
        zT = sb("zT", [P, NB, P])
        zTh = sb("zTh", [P, NB, P], F16)
        zTl = sb("zTl", [P, NB, P], F16)
        c = sb("c", [P, NB, D])
        cT = sb("cT", [P, NB, P])
        ident = sb("ident", [P, P])
        ident16 = sb("ident16", [P, P], F16)
        identb = sb("identb", [P, P], BF16)
        ones = sb("ones", [P, P])
        tri = sb("tri", [P, P])
        maskT = sb("maskT", [P, 4, P], BF16)
        maskQ = sb("maskQ", [P, 4, P], BF16)
        mhalf = sb("mhalf", [P, 8])
        reset = sb("reset", [P, 2 * NE, NB])
        rank = sb("rank", [P, NB, NE])
        tg = sb("tg", [P, 8])
        wifT = sb("wifT", [P, 3, 2 * H0])
        ifb = sb("ifb", [P, 2 * H0])
        wg0 = sb("wg0", [P, NE])
        stage_f32 = sb("stage_f32", [P, NE * 2 * F])
        split = {"f0": sb("split0", [P, 2 * NE * 2 * F // 2]), "f2": sb("split2", [P, 2 * NE * 2 * F // 2])}
        phase = sb("phase", [P, 8192])
        work = sb("work", [P, 4096])
        win = stage_f32[:, :].rearrange("p (e f) -> p e f", e=NE)
        winh = {k: t_[:, 0:NE * F].bitcast(F16).rearrange("p (e f) -> p e f", e=NE) for k, t_ in split.items()}
        winl = {k: t_[:, NE * F:2 * NE * F].bitcast(F16).rearrange("p (e f) -> p e f", e=NE) for k, t_ in split.items()}

        def carve(region, *tiles):
            at_, out = 0, []
            for shape, dt in tiles:
                n = 1
                for k in shape:
                    n *= k
                words = n if dt == F32 else n // 2
                v_ = region[:, at_:at_ + words]
                if dt != F32:
                    v_ = v_.bitcast(dt)
                names = " ".join("abcd"[:len(shape)])
                if len(shape) > 1:
                    v_ = v_.rearrange(f"p ({names}) -> p {names}", **{"abcd"[i]: shape[i] for i in range(1, len(shape))})
                out.append(v_)
                at_ += words
            assert at_ <= region.shape[1]
            return out
        wout = sb("wout", [P, NE, 2, D])
        wout16 = sb("wout16", [P, 2, NE, 2, D], F16)
        t1 = sb("t1", [P, NB, D])
        t1f = t1[:, :, :].rearrange("p b d -> p (b d)")
        wif = t1f[0:2 * H0, 0:3 * D]
        w1T = sb("w1T", [P, 2, D])
        cmean = sb("cmean", [P, NB])
        cmeanB = sb("cmeanB", [P, NB, P])
        at = sb("at", [P, NB + 1, D])
        wq8 = at[:, :, :].rearrange("p (i c) d -> p i c d", i=3)
        w8T = sb("w8T", [P, 3, I1])
        w8s = sb("w8s", [P, 3, 12])
        w8r = sb("w8r", [P, 3, 12])
        wA = sb("wA", [P, 3, D])
        woA = sb("woA", [P, D])
        wB = sb("wB", [P, 3, D])
        woB = sb("woB", [P, D])
        wf = sb("wf", [P, D])
        router = sb("router", [NE, D])
        routerT = sb("routerT", [P, NE])
        wC = sb("wC", [P, 3, D])
        woC = sb("woC", [P, D])
        wg3 = sb("wg3", [P, NE])
        w31 = sb("w31", [P, NE, 64])
        w32 = sb("w32", [P, 4, D])
        b31 = sb("b31", [P, 4])
        b32 = sb("b32", [NE, D])
        ws1 = sb("ws1", [P, 64])
        ws2 = sb("ws2", [64, D])
        bs1 = sb("bs1", [64, 1])
        rscale = sb("rscale", [P, 1])
        sel = sb("sel", [NE, 4, P])
        vecs = ["L0_xattn_gn_w", "L0_xattn_gn_b", "L1_xattn_b", "L2_xattn_bo1", "L2_xattn_g1",
                "L2_xattn_b1", "L2_xattn_bo2", "L2_xattn_g2", "L2_xattn_b2", "L2_xattn_bf",
                "L2_xattn_g3", "L2_xattn_b3", "L3_xattn_bo", "L3_ffn_bs2"]
        rows = sb("rows", [P, len(vecs), D])
        bqkv = sb("bqkv", [P, 3, D])

        def vec(name):
            return rows[:, vecs.index(name), :]

        stats = sb("stats", [P, NB, 6])
        mv = sb("mv", [P, NB, 2])
        vr = sb("vr", [P, NB])
        rstd = sb("rstd", [P, NB])
        gi = sb("gi", [P, NB, H0])
        gf = sb("gf", [P, NB, H0])
        ga = sb("ga", [P, NB, H0])
        gb = sb("gb", [P, NB, H0])
        cs = sb("cs", [P, NB, H0])
        aT = sb("aT", [NB * H0, P])
        mT = sb("mT", [NB * H0, P])
        mm = sb("mm", [P, NB, H0])
        floor = sb("floor", [P, NB, H0])
        nrm = sb("nrm", [P, H0])
        hm = sb("hm", [P, H0])
        sq = sb("sq", [P, D])
        hv = sb("hv", [P, NB, H0])
        hr = sb("hr", [P, NB, H0])
        lg = sb("lg", [P, NB, NE])
        pr = sb("pr", [P, NB, NE])
        p2 = sb("p2", [P, NB, NE])
        eq = sb("eq", [P, NB, NE])
        top = sb("top", [P, NB, 1])
        oh = sb("oh", [P, 2, NB, NE])
        cum = sb("cum", [P, 2, NB, NE])
        tot = sb("tot", [P, 2 * NE, NB])
        inc = sb("inc", [P, 2 * NE, NB])
        gate = sb("gate", [P, NB, NE])
        gsum = sb("gsum", [P, NB, 1])
        mx = sb("mx", [P, 2])
        magic = sb("magic", [P, 1])
        primer = sb("primer", [P, 1])
        m1 = sb("m1", [2, 2])
        m1b = sb("m1b", [2, 2])
        part = sb("part", [P, 2, NB])
        q_cols = ["x", "up", "gate", "prod", "out"]
        q_scale = sb("q_scale", [P, len(q_cols)])
        q_unit = sb("q_unit", [P, len(q_cols)])
        q_inv = sb("q_inv", [P, len(q_cols)])
        q_last = sb("q_last", [P, 1])
        qs = sb("qs", [P, NB, HA, SLOTA], F16)
        ks = sb("ks", [P, NB, HA, SLOTA], F16)
        nmax = sb("nmax", [P, NB, HA])
        rden = sb("rden", [P, HA])
        t2 = c
        hh = t1
        acc = at
        mst, am, q0, k0, qk0, ch0, cl0 = carve(
            phase, ((NB * H0, SLOT0), F16), ((2, 8, P), F16), ((2, H0, SLOT0), F16),
            ((2, H0, SLOT0), F16), ((2, 8, P), F16), ((2, H0, P), F16), ((2, H0, P), F16))
        xq, up, gt = carve(phase, ((NB * P,), F32), ((3, NB * P), F32), ((3, NB * P), F32))
        ph, pl, qkT = carve(phase, ((2, HA, P), F16), ((2, HA, P), F16), ((NB, 8, P), F16))
        act, hidh, hidl = carve(work, ((2, 2, BANK), F32), ((2, 2, BANK), F16), ((2, 2, BANK), F16))
        v0, ast, w1 = carve(work, ((NB, H0, 2 * D0 + 1), F16), ((NB * H0, SLOT0), F16), ((2 * D,), F32))
        at_names = ("a_wt", "b_qt", "b_wt", "b_ft", "c_wt")
        sg, *at_tiles = carve(split["f0"], ((3, NB * P), F32), *[((P,), F32)] * len(at_names))
        h3s = [carve(split[f], ((5, BANK), F32))[0] for f in ("f0", "f2")]
        atT = dict(zip(at_names, at_tiles))
        q2T, q32, vA = carve(stage_f32, ((NB, 4, P), F16), ((2, 3, D), F32), ((NB, HA, 2 * DA + 1), F16))
        p32 = wout[:, :, :, :].rearrange("p (j e) c d -> p j (e c d)", j=4)
        (dec,) = carve(split["f2"], ((4, 4, P), F32))
        dec = dec.rearrange("p (b j) h q -> p b j h q", b=2)
        gT = cmeanB[0:NE, :, :]
        q_of = {n: i for i, n in enumerate(q_cols)}

        def col(tile, name, n=1):
            return tile[:, q_of[name]:q_of[name] + n]

        psum = ctx.enter_context(nc.psum_tensor("psum", [P, PSUM_BANKS * BANK], F32))
        full = [sem(f"bank{k}_full") for k in range(PSUM_BANKS)]
        free = [sem(f"bank{k}_free") for k in range(PSUM_BANKS)]
        banks = Banks(order, psum, full, free)

        def turns(*stages):
            return {o: n for n, o in enumerate(o for o in order if o[0] in stages)}

        route_turn = turns("f0_route", "f2_route", "f3_route")
        up_turn = turns("f0_up", "f2_up")
        down_turn = turns("f0_down", "f2_down")
        assert [(s[:2], b) for s, b in up_turn] == [(s[:2], b) for s, b in down_turn]
        norms_ = [o for o in order if o[0] in NORMS]
        norm_turn = {o: n + 1 for n, o in enumerate(norms_)}
        pt_turn = {(s[0], b): n for n, (s, b) in enumerate(o for o in order if o[0] in ("a_exp", "b_exp", "c_exp"))}
        assert list(pt_turn) == [(s[0], b) for s, b in order if s in ("a_av", "b_av", "c_av")]

        def groups(tile, n):
            return tile.rearrange("p (i g) q -> p g i q", g=n)

        def as16(tile):
            return tile.bitcast(F16)

        done = sem("stored")
        n_loads = {}

        block = ctx.enter_context(nc.Block())

        loads = [
            ("x", x[:, :, :], t["x"].rearrange("b p d -> p b d")),
            ("x", c[:, :, :], t["ctx_1024"].rearrange("b p d -> p b d")),
            ("x0", wif[0:H0, :], t["L0_xattn_Wi_w"]),
            ("x0", wif[H0:2 * H0, :], t["L0_xattn_Wf_w"]),
            ("x0", ifb[:, 0:H0], t["L0_xattn_Wi_b"].partition_broadcast(P)),
            ("x0", ifb[:, H0:2 * H0], t["L0_xattn_Wf_b"].partition_broadcast(P)),
            ("x0", tg[:, 0:4], t["g_xattn"].partition_broadcast(P)),
            ("x0", tg[:, 4:8], t["g_ffn"].partition_broadcast(P)),
            ("x0", wg0[:, :], t["L0_ffn_Wg"]),
            ("win", win, t["L0_ffn_W_in"].rearrange("e h f -> h e f")),
        ] + [("rows", rows[:, i, :], t[n].partition_broadcast(P)) for i, n in enumerate(vecs)] + [
            ("wout", wout[:, :, :, :], t["L0_ffn_W_out"].rearrange("e (c p) h -> p e c h", p=P)),
            ("l1", w1[:, :], t["L1_xattn_W"]),
            ("l1", wq8[:, 0, :, :], t["L1_ffn_w_up"].rearrange("(c p) d -> p c d", p=P)),
            ("l1", wq8[:, 1, :, :], t["L1_ffn_w_gate"].rearrange("(c p) d -> p c d", p=P)),
            ("l1", wq8[:, 2, :, :], t["L1_ffn_w_down"].rearrange("p (c d) -> p c d", c=3)),
            ("l1", router[:, :], t["L2_ffn_router_w"]),
        ] + [("l2", w[:, i, :].rearrange("e (h d) -> e h d", h=HA), t[f"L2_xattn_W{n}{m}"].rearrange("h e d -> e h d"))
             for w, m in ((wA, 1), (wB, 2)) for i, n in enumerate("qkv")] + [
            ("l2", woA[:, :], t["L2_xattn_Wo1"]),
            ("l2", woB[:, :], t["L2_xattn_Wo2"]),
            ("l2", wf[:, :], t["L2_xattn_Wf"]),
            ("win2", win, t["L2_ffn_w13"].rearrange("e h f -> h e f")),
            ("win2", wout[:, :, :, :], t["L2_ffn_w2"].rearrange("e (c p) h -> p e c h", p=P)),
        ] + [("l3", wC[:, i, :], t[f"L3_xattn_W{n}"]) for i, n in enumerate("qkv")] \
          + [("l3", bqkv[:, i, :], t[f"L3_xattn_b{n}"].partition_broadcast(P)) for i, n in enumerate("qkv")] + [
            ("l3", woC[:, :], t["L3_xattn_Wo"]),
            ("l3", wg3[:, :], t["L3_ffn_gate_W"]),
            ("l3", w31[:, :, :], t["L3_ffn_W1"].rearrange("e d h -> d e h")),
            ("l3", w32[:, :, :], t["L3_ffn_W2"].rearrange("(c two) h d -> (two h) c d", two=2)),
            ("l3", b31[:, :], t["L3_ffn_b1"].rearrange("(c two) h -> (two h) c", two=2)),
            ("l3", b32[:, :], t["L3_ffn_b2"]),
            ("l3", ws1[:, :], t["L3_ffn_Ws1"]),
            ("l3", ws2[:, :], t["L3_ffn_Ws2"]),
            ("l3", bs1[:, :], t["L3_ffn_bs1"].rearrange("(h o) -> h o", o=1)),
            ("l3", rscale[:, :], t["L3_ffn_route_scale"].partition_broadcast(P)),
        ]
        for g, _, _ in loads:
            n_loads[g] = n_loads.get(g, 0) + 16

        def loaded(eng, *groups):
            for g in groups:
                eng.wait_ge(sem("loaded_" + g), n_loads[g])

        @block.sync
        def _(sp):
            with nc.allow_non_contiguous_dma(reason="weights laid out once"):
                for g, dst, src in loads:
                    if g == "win2" and dst is win:
                        sp.wait_ge(sem("win_split"), NE)
                    if g == "win2" and dst is not win:
                        sp.wait_ge(sem("wout_split"), NE)
                    sp.dma_start(dst, src).then_inc(sem("loaded_" + g), 16)
            for b in range(NB):
                sp.wait_ge(sem("x_final"), (b // HALF + 1) * HALF)
                sp.dma_start(t["out"][b], x[:, b, :]).then_inc(done, 16)
            sp.wait_ge(done, 16 * NB)

        @block.gpsimd
        def _(pool):
            ch = Chain(pool, sem("pool_step"))

            def rsqrt(col, eps, ready):
                pool.wait_ge(*ready)
                ch.do(pool.tensor_scalar(vr[:, col:col + 1], mv[:, col, 1:2], eps, None, ALU.add))
                ch.sync()
                ch.do(pool.tensor_tensor(rstd[:, col:col + 1], vr[:, col:col + 1], mhalf[:, 0:1], ALU.pow),
                      sem("rstd_ready"))

            for stage, b in order:
                if stage == "setup":
                    ch.do(pool.memset(ident[:, :], 0.0))
                    ch.do(pool.memset(mhalf[:, :], -0.5))
                    ch.sync()
                    ch.do(pool.affine_select(out=ident[:, :], in_=ident[:, :], compare_op=ALU.not_equal, fill=1.0,
                                             base=0, pattern=[[-1, P]], channel_multiplier=1), sem("ident_ready"))
                    ch.do(pool.memset(tri[:, :], 1.0))
                    ch.do(pool.memset(maskT[:, :, :], 0.0))
                    ch.do(pool.memset(maskQ[:, :, :], 0.0))
                    ch.sync()
                    ch.do(pool.affine_select(out=tri[:, :], in_=tri[:, :], compare_op=ALU.is_ge, fill=0.0,
                                             base=0, pattern=[[1, P]], channel_multiplier=-1))
                    ch.do(pool.affine_select(out=maskT[:, :, :], in_=maskT[:, :, :], compare_op=ALU.is_ge,
                                             fill=MASKED, base=0, pattern=[[0, 4], [1, P]], channel_multiplier=-1))
                    ch.do(pool.affine_select(out=maskQ[:, :, :], in_=maskQ[:, :, :], compare_op=ALU.is_ge,
                                             fill=MASKED, base=0, pattern=[[0, 4], [-1, P]], channel_multiplier=1),
                          sem("const_ready"))
                    pool.wait_ge(sem("wT_ready"), 3)
                    ch.do(pool.tensor_tensor(wifT[:, 1, :], wifT[:, 1, :], wifT[:, 2, :], ALU.add), sem("w_kv_ready"))
                elif stage == "x0_forget":
                    ch.do(pool.memset(reset[:, :, :], 1.0))
                    ch.sync()
                    ch.do(pool.memset(reset[:, :, 0:1], 0.0))
                    for e in range(NE):
                        ch.do(pool.memset(rank[:, :, e:e + 1], float(NE - e)), sem("route_consts") if e == NE - 1 else None)
                    ch.do(pool.memset(sel[:, :, :], 1.0))
                    ch.sync()
                    ch.do(pool.affine_select(out=sel[:, :, :], in_=sel[:, :, :], compare_op=ALU.is_ge, fill=0.0,
                                             base=0, pattern=[[P, 4], [1, P]], channel_multiplier=-64))
                    ch.sync()
                    ch.do(pool.affine_select(out=sel[:, :, :], in_=sel[:, :, :], compare_op=ALU.is_ge, fill=0.0,
                                             base=63, pattern=[[-P, 4], [-1, P]], channel_multiplier=64), sem("sel_ready"))
                elif stage == "x0_split":
                    if b == 0:
                        loaded(pool, "x")
                        pool.wait_ge(sem("stack_zeros"), 1)
                    cb = c[:, b, :].rearrange("p (h d) -> p h d", h=H0)
                    kk = k0[:, b % 2, :, :]
                    pool.wait_ge(sem("k0_high"), b + 1)
                    ch.do(pool.tensor_tensor(kk[:, :, D0:2 * D0], cb, kk[:, :, 0:D0], ALU.subtract), sem("k0_ready"))
                    ch.do(pool.tensor_tensor(v0[:, b, :, D0 + 1:2 * D0 + 1], cb, kk[:, :, 0:D0], ALU.subtract), sem("v0_ready"))
                elif stage == "x0_cut":
                    pool.wait_ge(sem("ch0_ready"), 2 * b + 1)
                    ch.do(pool.tensor_tensor(groups(cl0[:, b % 2, :, :], 2)[:, 0], dec[:, b % 2, 0, :, :], groups(ch0[:, b % 2, :, :], 2)[:, 0], ALU.subtract),
                          sem("cl0_ready_0"))
                elif stage in ("a_exp", "b_exp", "c_exp"):
                    n = pt_turn[stage[0], b]
                    for j in range(4):
                        pool.wait_ge(sem("ph_ready"), 4 * n + j + 1)
                        ch.do(pool.tensor_tensor(groups(pl[:, n % 2, :, :], 4)[:, j], p32[:, j, :].rearrange("p (h q) -> p h q", h=4),
                                                 groups(ph[:, n % 2, :, :], 4)[:, j], ALU.subtract), sem("pl_ready"))
                elif stage in ("split0", "split2"):
                    f = "f0" if stage == "split0" else "f2"
                    pool.wait_ge(sem("win_high"), (NE if f == "f2" else 0) + b + 1)
                    ch.do(pool.tensor_tensor(winl[f][:, b, :], win[:, b, :], winh[f][:, b, :], ALU.subtract),
                          sem("win_split"))
                    if f == "f0":
                        ch.do(pool.tensor_tensor(wout16[:, 1, b, :, :], wout[:, b, :, :], wout16[:, 0, b, :, :], ALU.subtract),
                              sem("wout_split"))
                elif stage == "split_out":
                    pool.wait_ge(sem("wout_high"), b + 1)
                    ch.do(pool.tensor_tensor(wout16[:, 1, b, :, :], wout[:, b, :, :], wout16[:, 0, b, :, :], ALU.subtract),
                          sem("wout_split"))
                elif stage in ("f0_cut", "f2_cut"):
                    n = up_turn[stage[:2] + "_up", b]
                    for k in range(2):
                        pool.wait_ge(sem("hid_high"), 2 * n + k + 1)
                        ch.do(pool.tensor_tensor(hidl[:, n % 2, k, :], act[:, n % 2, k, :], hidh[:, n % 2, k, :], ALU.subtract), sem("hid_low"))
                elif stage in ("f0_t", "f2_t"):
                    l = {"f0_t": 0, "f2_t": 1}[stage]
                    pool.wait_ge(sem("zTh_ready"), l * NB + b + 1)
                    ch.do(pool.tensor_tensor(zTl[:, b, :], zT[:, b, :], zTh[:, b, :], ALU.subtract), sem("zTl_ready"))
                elif stage == "f1_scale":
                    pool.wait_ge(sem("win_split"), 2 * NE)
                    ch.do(pool.memset(vA[:, :, :, DA:DA + 1], 1.0), sem("vA_ones"))
                elif stage == "f1_gate":
                    pool.wait_ge(sem("scale_gate"), 1)
                    for k in range(3):
                        ch.do(pool.tensor_scalar(up[:, k, :], up[:, k, :], col(q_inv, "up"), MAGIC, ALU.mult, ALU.add))
                        ch.sync()
                        ch.do(pool.tensor_scalar(up[:, k, :], up[:, k, :], -MAGIC, None, ALU.add), sem("up_whole"))
                elif stage == "x0_value":
                    pool.wait_ge(sem("hv_ready"), b + 1)
                    ch.do(pool.tensor_tensor(hr[:, b, :], hv[:, b, :], mhalf[:, :], ALU.pow), sem("hr_ready"))
                if stage in NORMS:
                    rsqrt(b, NORMS[stage], (sem("stats_ready"), norm_turn[stage, b]))

        @block.tensor
        def _(pe):
            mm_ = nc.tensor.matmul
            tr = nc.tensor.transpose

            def one(out, a, b_):
                return mm_(out, a, b_, start=True, stop=True)

            def to_T(key, b):
                pe.wait_ge(sem(key[:2] + "_z"), b + 1)
                u = banks.take(pe, key, b, "u")
                banks.fill(tr(u[:, 0:P], z[:, b, :], ident[:, :]), key, b, "u")

            for stage, b in order:
                if stage == "setup":
                    pe.wait_ge(sem("ident_ready"), 1)
                    loaded(pe, "x")
                    for i in range(2):
                        u = banks.take(pe, "setup", 0, f"ctx{i}")
                        for j in range(4):
                            last = tr(u[:, j * P:(j + 1) * P], c[:, 4 * i + j, :], ident[:, :])
                        banks.fill(last, "setup", 0, f"ctx{i}")
                    loaded(pe, "x0")
                    u = banks.take(pe, "setup", 0, "gate_w")
                    for j in range(3):
                        last = tr(u[:, j * 2 * H0:(j + 1) * 2 * H0], wif[:, j * D:(j + 1) * D], ident[0:2 * H0, 0:2 * H0])
                    banks.fill(last, "setup", 0, "gate_w")
                elif stage == "w1":
                    loaded(pe, "l1")
                    u = banks.take(pe, stage, b, "u")
                    for j in range(2):
                        last = tr(u[:, j * D:(j + 1) * D], w1[:, j * D:(j + 1) * D], ident[:, :])
                    banks.fill(last, stage, b, "u")
                elif stage == "w8":
                    pe.wait_ge(sem("w8_ready"), b + 1)
                    u = banks.take(pe, stage, b, "u")
                    for j in range(3):
                        last = tr(u[:, j * P:(j + 1) * P], wq8[:, b, j, :], ident[:, :])
                    banks.fill(last, stage, b, "u")
                elif stage == "router":
                    loaded(pe, "l1")
                    u = banks.take(pe, stage, b, "u")
                    banks.fill(tr(u[:, 0:NE], router[:, :], ident[0:NE, 0:NE]), stage, b, "u")
                elif stage in T_STAGES:
                    to_T(stage, b)
                elif stage == "x0_gate":
                    if b == 0:
                        u0 = banks.take(pe, "x0_gate", 0, "gates")
                        pe.wait_ge(sem("wT_ready"), 3)
                        pe.wait_ge(sem("w_kv_ready"), 1)
                    o = u0[:, b * 2 * H0:(b + 1) * 2 * H0]
                    mm_(o, cT[:, b, :], wifT[:, 1, :], start=True, stop=False)
                    pe.wait_ge(sem("x0_zT"), b + 1)
                    last = mm_(o, zT[:, b, :], wifT[:, 0, :], start=False, stop=True)
                    if b == NB - 1:
                        banks.fill(last, "x0_gate", 0, "gates")
                elif stage == "x0_forget":
                    pe.wait_ge(sem("const_ready"), 1)
                    pe.wait_ge(sem("log_forget"), 1)
                    u = banks.take(pe, stage, 0, "csum")
                    banks.fill(one(u[:, 0:NB * H0], tri[:, :], gf[:, :, :]), stage, 0, "csum")
                    pe.wait_ge(sem("a_ready"), 1)
                    u = banks.take(pe, stage, 0, "at")
                    banks.fill(tr(u[0:NB * H0, 0:P], ga[:, :, :].rearrange("p b h -> p (b h)"), ident[:, :]), stage, 0, "at")
                    pe.wait_ge(sem("mT_ready"), 1)
                    u = banks.take(pe, stage, 0, "m")
                    banks.fill(tr(u[:, 0:NB * H0], mT[:, :], ident[0:NB * H0, 0:NB * H0]), stage, 0, "m")
                elif stage == "x0_stack":
                    if b == 0:
                        pe.wait_ge(sem("ident16_ready"), 2)
                    pe.wait_ge(sem("q0_ready"), b + 1)
                    pe.wait_ge(sem("k0_ready"), b + 1)
                    u = as16(banks.take(pe, stage, b, "qk"))
                    for i, st in enumerate((q0, k0)):
                        for j in range(4):
                            o = (4 * i + j) * P
                            last = tr(u[:, o:o + P], st[:, b % 2, 2 * j:2 * j + 2, :].rearrange("p h s -> p (h s)"), ident16[:, :])
                    banks.fill(last, stage, b, "qk")
                    u = as16(banks.take(pe, stage, b, "am"))
                    pe.wait_ge(sem("am_ready"), 1)
                    for i, st in enumerate((ast, mst)):
                        for j in range(4):
                            h = b * H0 + 2 * j
                            o = (4 * i + j) * P
                            last = tr(u[:, o:o + P], st[:, h:h + 2, :].rearrange("p h s -> p (h s)"), ident16[:, :])
                    banks.fill(last, stage, b, "am")
                elif stage == "x0_score":
                    if b == 0:
                        pe.wait_ge(sem("ident16_ready"), 2)
                    pe.wait_ge(sem("qk0_T"), b + 1)
                    pe.wait_ge(sem("am_T"), b + 1)
                    us = [banks.take(pe, stage, b, f"e{g}") for g in range(2)]
                    for g in range(2):
                        mm_(us[g], identb[:, :], maskT[:, :, :].rearrange("p h q -> p (h q)"), start=True, stop=False)
                    for j in range(4):
                        for g in range(2):
                            r = 64 * g
                            last = mm_(us[g][:, j * P:(j + 1) * P], am[r:r + 6, b % 2, j, :], am[r:r + 6, b % 2, 4 + j, :],
                                       start=False, stop=(j == 3))
                            if j == 3:
                                banks.fill(last, stage, b, f"e{g}")
                    us = [banks.take(pe, stage, b, f"s{g}") for g in range(2)]
                    for j in range(4):
                        for g in range(2):
                            r = 64 * g
                            last = one(us[g][:, j * P:(j + 1) * P], qk0[r:r + 48, b % 2, 4 + j, :], qk0[r:r + 48, b % 2, j, :])
                            if j == 3:
                                banks.fill(last, stage, b, f"s{g}")
                elif stage == "x0_value":
                    for j in range(2):
                        pe.wait_ge(sem(f"cl0_ready_{j}"), b + 1)
                    pe.wait_ge(sem("v0_ready"), b + 1)
                    u = banks.take(pe, stage, b, "u")
                    n = 2 * D0 + 1
                    for h in range(H0):
                        mm_(u[:, h * n:(h + 1) * n], ch0[:, b % 2, h, :], v0[:, b, h, :], start=True, stop=False)
                        last = mm_(u[:, h * n:h * n + D0 + 1], cl0[:, b % 2, h, :], v0[:, b, h, 0:D0 + 1], start=False, stop=True)
                    banks.fill(last, stage, b, "u")
                elif stage in ("f0_route", "f2_route", "f3_route"):
                    w = {"f0_route": wg0, "f2_route": routerT, "f3_route": wg3}[stage]
                    if stage == "f2_route":
                        pe.wait_ge(sem("router_T"), 1)
                    if stage == "f3_route":
                        loaded(pe, "l3")
                    own = range(NB) if stage == "f0_route" else range(HALF * b, HALF * (b + 1))
                    pe.wait_ge(sem(stage[:2] + "_zT"), own[-1] + 1)
                    u = banks.take(pe, stage, b, "logit")
                    for i, b_ in enumerate(own):
                        last = one(u[:, i * NE:(i + 1) * NE], zT[:, b_, :], w[:, :])
                    banks.fill(last, stage, b, "logit")
                    if stage == "f0_route":
                        pe.wait_ge(sem("oh_ready"), 1)
                        u = banks.take(pe, stage, 0, "cum")
                        banks.fill(one(u[:, 0:2 * NB * NE], tri[:, :], oh[:, :, :, :].rearrange("p k b e -> p (k b e)")), stage, 0, "cum")
                        u = banks.take(pe, stage, 0, "total")
                        banks.fill(one(u[:, 0:2 * NB * NE], ones[:, :], oh[:, :, :, :].rearrange("p k b e -> p (k b e)")), stage, 0, "total")
                elif stage == "f3_gt":
                    pe.wait_ge(sem("gate_ready"), route_turn["f3_route", b] + 1)
                    u = banks.take(pe, stage, b, "gt")
                    for j in range(4):
                        last = tr(u[0:NE, j * P:(j + 1) * P], gate[:, 4 * b + j, :], ident[:, :])
                    banks.fill(last, stage, b, "gt")
                elif stage in ("f0_up", "f2_up"):
                    e, g = b
                    l = {"f0": 0, "f2": 1}[stage[:2]]
                    pe.wait_ge(sem("zTl_ready"), l * NB + 4 * (g + 1))
                    pe.wait_ge(sem("win_split"), l * NE + e + 1)
                    cols = slice(4 * g, 4 * g + 4)
                    xh = zTh[:, cols, :].rearrange("p b q -> p (b q)")
                    xl = zTl[:, cols, :].rearrange("p b q -> p (b q)")
                    for i, name in enumerate(("a0", "g0", "a1", "g1")):
                        u = banks.take(pe, stage, b, name)
                        f = (i // 2) * P + (i % 2) * F
                        mm_(u, winh[stage[:2]][:, e, f:f + P], xh, start=True, stop=False)
                        mm_(u, winh[stage[:2]][:, e, f:f + P], xl, start=False, stop=False)
                        last = mm_(u, winl[stage[:2]][:, e, f:f + P], xh, start=False, stop=True)
                        banks.fill(last, stage, b, name)
                elif stage in ("f0_down", "f2_down"):
                    e, g = b
                    f = stage[:2]
                    n = down_turn[stage, b]
                    if e == 0 and g == 0:
                        pe.wait_ge(sem("wout_split"), (1 if f == "f0" else 2) * NE)
                    pe.wait_ge(sem("hid_low"), 2 * (n + 1))
                    u = banks.take(pe, stage, b, "u")
                    for j in range(4):
                        for k in range(2):
                            for i, (h_, w_) in enumerate(((hidh, 0), (hidh, 1), (hidl, 0))):
                                last = mm_(u[:, j * D:(j + 1) * D], h_[:, n % 2, k, j * P:(j + 1) * P], wout16[:, w_, e, k, :],
                                           start=(k == 0 and i == 0), stop=(k == 1 and i == 2))
                    banks.fill(last, stage, b, "u")
                elif stage == "x1_out":
                    pe.wait_ge(sem("x1_zT"), b + 1)
                    if b == 0:
                        pe.wait_ge(sem("cmean_ready"), 1)
                        pe.wait_ge(sem("w1_T"), 1)
                    u = banks.take(pe, stage, b, "u")
                    mm_(u[:, 0:D], zT[:, b, :], w1T[:, 0, :], start=True, stop=False)
                    banks.fill(mm_(u[:, 0:D], cmeanB[:, b, :], w1T[:, 1, :], start=False, stop=True), stage, b, "u")
                elif stage in ("f1_scale", "f1_gate", "f1_prod", "f1_out"):
                    i = ("f1_scale", "f1_gate", "f1_prod", "f1_out").index(stage) + 1
                    n = 2 if stage == "f1_gate" else 1
                    pe.wait_ge(sem("mx_ready"), i)
                    u = banks.take(pe, stage, 0, "t")
                    banks.fill(tr(u[0:n, 0:P], mx[:, 0:n], ident[:, :]), stage, 0, "t")
                    pe.wait_ge(sem("m1_ready"), i)
                    u = banks.take(pe, stage, 0, "b")
                    banks.fill(one(u[:, 0:n], ones[0:n, :], m1b[0:n, 0:n]), stage, 0, "b")
                elif stage == "f1_up":
                    cch, g = b
                    pe.wait_ge(sem("xq_ready"), g + 1)
                    pe.wait_ge(sem("w8_T"), 3)
                    for i, name in enumerate(("up", "gate")):
                        u = banks.take(pe, stage, b, name)
                        banks.fill(one(u, w8T[:, i, cch * P:(cch + 1) * P], xq[:, g * BANK:(g + 1) * BANK]), stage, b, name)
                elif stage == "f1_down":
                    pe.wait_ge(sem("o_ready"), b // 2 + 1)
                    u = banks.take(pe, stage, b, "u")
                    for k in range(3):
                        last = mm_(u[:, 0:D], sg[:, k, b * P:(b + 1) * P], w8T[:, 2, k * P:(k + 1) * P], start=(k == 0), stop=(k == 2))
                    banks.fill(last, stage, b, "u")
                elif stage in ("a_kv", "b_kv", "c_kv"):
                    m = stage[0]
                    u = banks.take(pe, stage, b, "qkv")
                    if m == "a":
                        if b == 0:
                            loaded(pe, "l2")
                        pe.wait_ge(sem("x2_zT"), b + 1)
                        last = one(u[:, 0:3 * D], zT[:, b, :], wA[:, :, :].rearrange("p i d -> p (i d)"))
                    elif m == "b":
                        last = one(u[:, D:3 * D], cT[:, b, :], wB[:, 1:3, :].rearrange("p i d -> p (i d)"))
                    else:
                        if b == 0:
                            loaded(pe, "l3")
                        pe.wait_ge(sem("x3_zT"), b + 1)
                        one(u[:, 0:D], zT[:, b, :], wC[:, 0, :])
                        last = one(u[:, D:3 * D], cT[:, b, :], wC[:, 1:3, :].rearrange("p i d -> p (i d)"))
                    banks.fill(last, stage, b, "qkv")
                elif stage in ("b_qt", "b_ft"):
                    pe.wait_ge(sem("a_out" if stage == "b_qt" else "b_out"), b + 1)
                    u = banks.take(pe, stage, b, "t")
                    banks.fill(tr(u[:, 0:P], t1[:, b, :], ident[:, :]), stage, b, "t")
                elif stage == "b_q":
                    pe.wait_ge(sem("b_qt_T"), b + 1)
                    u = banks.take(pe, stage, b, "q")
                    banks.fill(one(u[:, 0:D], atT["b_qt"][:, :], wB[:, 0, :]), stage, b, "q")
                elif stage in ("a_stack", "b_stack", "c_stack"):
                    m = stage[0]
                    pe.wait_ge(sem(m + "_stacks"), b + 1)
                    if m == "b":
                        pe.wait_ge(sem("b_qs"), b + 1)
                    u = as16(banks.take(pe, stage, b, "qk"))
                    for i, st in enumerate((qs, ks)):
                        for j in range(4):
                            o = (4 * i + j) * P
                            last = tr(u[:, o:o + P], st[:, b, 4 * j:4 * j + 4, :].rearrange("p h s -> p (h s)"), ident16[:, :])
                    banks.fill(last, stage, b, "qk")
                elif stage in ("a_max", "b_max", "c_max"):
                    m = stage[0]
                    pe.wait_ge(sem(m + "_qkT"), b + 1)
                    for pair in ((0, 1), (2, 3)):
                        us = {i: banks.take(pe, stage, b, f"s{i}") for i in pair}
                        if m == "a":
                            for i in pair:
                                mm_(us[i], identb[:, :], maskQ[:, :, :].rearrange("p h q -> p (h q)"), start=True, stop=False)
                        for j in range(4):
                            for i in pair:
                                r = 32 * i
                                last = mm_(us[i][:, j * P:(j + 1) * P], qkT[r:r + DA, b, j, :], qkT[r:r + DA, b, 4 + j, :],
                                           start=(m != "a"), stop=(j == 3 or m != "a"))
                                if j == 3:
                                    banks.fill(last, stage, b, f"s{i}")
                elif stage in ("a_again", "b_again", "c_again"):
                    m = stage[0]
                    pe.wait_ge(sem(m + "_negmax"), b + 1)
                    u = as16(banks.take(pe, stage, b, "q"))
                    for j in range(4):
                        last = tr(u[:, j * P:(j + 1) * P], qs[:, b, 4 * j:4 * j + 4, :].rearrange("p h s -> p (h s)"), ident16[:, :])
                    banks.fill(last, stage, b, "q")
                elif stage in ("a_exp", "b_exp", "c_exp"):
                    m = stage[0]
                    n = 3 * DA + 2
                    pe.wait_ge(sem(m + "_q2T"), b + 1)
                    for pair in ((0, 1), (2, 3)):
                        us = {i: banks.take(pe, stage, b, f"t{i}") for i in pair}
                        if m == "a":
                            for i in pair:
                                mm_(us[i], identb[:, :], maskT[:, :, :].rearrange("p h q -> p (h q)"), start=True, stop=False)
                        for j in range(4):
                            for i in pair:
                                r = 32 * i
                                last = mm_(us[i][:, j * P:(j + 1) * P], qkT[r:r + n, b, 4 + j, :], q2T[r:r + n, b, j, :],
                                           start=(m != "a"), stop=(j == 3 or m != "a"))
                                if j == 3:
                                    banks.fill(last, stage, b, f"t{i}")
                elif stage in ("a_av", "b_av", "c_av"):
                    m = stage[0]
                    n = pt_turn[m, b]
                    u = banks.take(pe, stage, b, "av")
                    for i in range(HA):
                        h = 4 * (i % 4) + i // 4
                        if i % 4 == 0:
                            pe.wait_ge(sem("pl_ready"), 4 * n + i // 4 + 1)
                        o = h * (2 * DA + 1)
                        mm_(u[:, o:o + 2 * DA + 1], ph[:, n % 2, h, :], vA[:, b, h, :], start=True, stop=False)
                        last = mm_(u[:, o:o + DA + 1], pl[:, n % 2, h, :], vA[:, b, h, 0:DA + 1], start=False, stop=True)
                    banks.fill(last, stage, b, "av")
                elif stage in ("a_wt", "b_wt", "c_wt"):
                    pe.wait_ge(sem(stage[0] + "_at"), b + 1)
                    u = banks.take(pe, stage, b, "t")
                    banks.fill(tr(u[:, 0:P], at[:, b, :], ident[:, :]), stage, b, "t")
                elif stage in ("a_wo", "b_wo", "c_wo"):
                    m = stage[0]
                    pe.wait_ge(sem(m + "_wt_T"), b + 1)
                    u = banks.take(pe, stage, b, "wo")
                    banks.fill(one(u[:, 0:D], atT[m + "_wt"][:, :], {"a": woA, "b": woB, "c": woC}[m][:, :]), stage, b, "wo")
                elif stage == "b_f":
                    pe.wait_ge(sem("b_ft_T"), b + 1)
                    u = banks.take(pe, stage, b, "f")
                    banks.fill(one(u[:, 0:D], atT["b_ft"][:, :], wf[:, :]), stage, b, "f")
                elif stage == "f3_up":
                    loaded(pe, "l3")
                    pe.wait_ge(sem("f3_zT"), HALF * (b + 1))
                    xg = zT[:, 4 * b:4 * b + 4, :].rearrange("p b q -> p (b q)")
                    for k in range(5):
                        u = banks.take(pe, stage, b, f"h{k}")
                        if k < 4:
                            banks.fill(one(u, w31[:, 2 * k:2 * k + 2, :].rearrange("p e h -> p (e h)"), xg), stage, b, f"h{k}")
                        else:
                            banks.fill(one(u[0:64, :], ws1[:, :], xg), stage, b, f"h{k}")
                elif stage == "f3_gate":
                    pe.wait_ge(sem("gT_ready"), b + 1)
                    pe.wait_ge(sem("sel_ready"), 1)
                    for k in range(4):
                        u = banks.take(pe, stage, b, f"gate{k}")
                        banks.fill(one(u, sel[:, k, :], gT[:, 4 * b:4 * b + 4, :].rearrange("p b q -> p (b q)")), stage, b, f"gate{k}")
                elif stage == "f3_down":
                    pe.wait_ge(sem("h3_gated"), 4 * (b + 1))
                    pe.wait_ge(sem("h3_ready"), 5 * (b + 1))
                    u = banks.take(pe, stage, b, "o")
                    for j in range(4):
                        o = u[:, j * D:(j + 1) * D]
                        for k in range(4):
                            mm_(o, h3s[b][:, k, j * P:(j + 1) * P], w32[:, k, :], start=(k == 0), stop=False)
                        mm_(o, h3s[b][0:64, 4, j * P:(j + 1) * P], ws2[:, :], start=False, stop=False)
                        last = mm_(o, gT[:, 4 * b + j, :], b32[:, :], start=False, stop=True)
                    banks.fill(last, stage, b, "o")

        @block.scalar
        def _(act_):
            ch = Chain(act_, sem("act_step"))
            A = nc.scalar.activation

            def copy_free(stage, b, name, out, view, signal):
                u = banks.get(act_, stage, b, name)
                ch.do(A(out, view(u), ACT.Copy), banks.freed(stage, b, name))
                ch.sync()
                act_.sem_inc(signal, 1)

            for stage, b in order:
                if stage == "setup":
                    loaded(act_, "x0")
                    ch.do(A(tg[:, :], tg[:, :], ACT.Tanh), sem("tg_ready"))
                    act_.wait_ge(sem("ident_ready"), 1)
                    ch.do(A(ident16[:, :], ident[:, :], ACT.Copy), sem("ident16_ready"))
                    ch.do(A(identb[:, :], ident[:, :], ACT.Copy), sem("ident16_ready"))
                    for i in range(2):
                        copy_free(stage, b, f"ctx{i}", cT[:, 4 * i:4 * i + 4, :], lambda u: u.rearrange("p (b q) -> p b q", b=4), sem("wT_ready"))
                    copy_free(stage, b, "gate_w", wifT[:, :, :], lambda u: u[:, 0:6 * H0].rearrange("p (i g) -> p i g", i=3), sem("wT_ready"))
                elif stage == "w1":
                    copy_free(stage, b, "u", w1T[:, :, :], lambda u: u[:, 0:2 * D].rearrange("p (i g) -> p i g", i=2), sem("w1_T"))
                elif stage == "w8":
                    copy_free(stage, b, "u", w8T[:, b, :], lambda u: u[:, 0:I1], sem("w8_T"))
                elif stage == "router":
                    copy_free(stage, b, "u", routerT[:, :], lambda u: u[:, 0:NE], sem("router_T"))
                elif stage in T_STAGES:
                    copy_free(stage, b, "u", zT[:, b, :], lambda u: u[:, 0:P], sem(stage[:2] + "_zT"))
                    if stage in ("f0_t", "f2_t"):
                        ch.do(A(zTh[:, b, :], zT[:, b, :], ACT.Copy), sem("zTh_ready"))
                elif stage == "x0_split":
                    if b == 0:
                        act_.wait_ge(sem("stack_zeros"), 1)
                    cb = c[:, b, :].rearrange("p (h d) -> p h d", h=H0)
                    kk = k0[:, b % 2, :, :]
                    ch.do(A(kk[:, :, 0:D0], cb, ACT.Copy))
                    ch.do(A(v0[:, b, :, 0:D0], cb, ACT.Copy))
                    ch.do(A(kk[:, :, 2 * D0:3 * D0], cb, ACT.Copy), sem("k0_high"))
                elif stage in ("split0", "split2"):
                    f = "f0" if stage == "split0" else "f2"
                    if b == 0:
                        loaded(act_, *(("win", "wout") if f == "f0" else ("win2",)))
                        if f == "f2":
                            for j in range(2):
                                act_.wait_ge(sem(f"cl0_ready_{j}"), NB)
                    if f == "f0":
                        ch.do(A(wout16[:, 0, b, :, :], wout[:, b, :, :], ACT.Copy))
                    ch.do(A(winh[f][:, b, :], win[:, b, :], ACT.Copy), sem("win_high"))
                elif stage == "split_out":
                    if b == 0:
                        loaded(act_, "win2")
                        act_.wait_ge(sem("hid_used"), NE * FPS)
                    ch.do(A(wout16[:, 0, b, :, :], wout[:, b, :, :], ACT.Copy), sem("wout_high"))
                elif stage in ("f0_cut", "f2_cut"):
                    n = up_turn[stage[:2] + "_up", b]
                    if n >= 2:
                        act_.wait_ge(sem("hid_used"), n - 1)
                    for k in range(2):
                        act_.wait_ge(sem("hid_ready"), 2 * n + k + 1)
                        ch.do(A(hidh[:, n % 2, k, :], act[:, n % 2, k, :], ACT.Copy), sem("hid_high"))
                elif stage == "x0_forget":
                    act_.wait_ge(sem("abs_f"), 1)
                    ch.do(A(ga[:, :, :], ga[:, :, :], ACT.Exp, scale=-1.0))
                    ch.sync()
                    ch.do(A(gb[:, :, :], ga[:, :, :], ACT.Ln, bias=1.0), sem("softplus"))
                    act_.wait_ge(sem("md_ready"), 1)
                    ch.do(A(floor[:, :, :], gb[:, :, :], ACT.Exp, scale=-1.0), sem("floor_ready"))
                elif stage == "x0_stack":
                    if b >= 2:
                        act_.wait_ge(sem("cc_ready"), 2 * (b - 1))
                    copy_free(stage, b, "qk", qk0[:, b % 2, :, :], lambda u: as16(u).rearrange("p (s q) -> p s q", s=8), sem("qk0_T"))
                    act_.sem_inc(sem("x0_stacked"), 1)
                    copy_free(stage, b, "am", am[:, b % 2, :, :], lambda u: as16(u).rearrange("p (s q) -> p s q", s=8), sem("am_T"))
                elif stage == "x0_score":
                    for j in range(2):
                        if b >= 2:
                            act_.wait_ge(sem(f"cl0_ready_{j}"), b - 1)
                        u = banks.get(act_, stage, b, f"e{j}")
                        ch.do(A(dec[:, b % 2, j, :, :], u.rearrange("p (h q) -> p h q", h=4), ACT.Exp), banks.freed(stage, b, f"e{j}"))
                        ch.sync()
                        act_.sem_inc(sem("dec_ready"), 1)
                elif stage == "x0_cut":
                    if b >= 2:
                        act_.wait_ge(sem("cc_used"), b - 1)
                    for j in range(2):
                        act_.wait_ge(sem("cc_ready"), 2 * b + j + 1)
                        ch.do(A(groups(ch0[:, b % 2, :, :], 2)[:, j], dec[:, b % 2, j, :, :], ACT.Copy), sem("ch0_ready"))
                elif stage in ("f0_route", "f2_route", "f3_route"):
                    n = route_turn[stage, b] + 1
                    bs = slice(0, NB) if stage == "f0_route" else slice(HALF * b, HALF * (b + 1))
                    act_.wait_ge(sem("logit_ready"), n)
                    ch.do(A(pr[:, bs, :], lg[:, bs, :], ACT.Exp, scale=-1.0 if stage == "f3_route" else 1.0), sem("route_exp"))
                elif stage == "f3_gt":
                    copy_free(stage, b, "gt", gT[:, 4 * b:4 * b + 4, :], lambda u: u[0:NE, :].rearrange("p (b q) -> p b q", b=4), sem("gT_ready"))
                elif stage in ("f0_up", "f2_up"):
                    e, g = b
                    n = up_turn[stage, b]
                    for k in range(2):
                        if n >= 2:
                            act_.wait_ge(sem("hid_low"), 2 * (n - 2) + k + 1)
                        u = banks.get(act_, stage, b, f"a{k}")
                        ch.do(A(act[:, n % 2, k, :], u, ACT.Gelu if stage == "f0_up" else ACT.Silu),
                              banks.freed(stage, b, f"a{k}"))
                        ch.sync()
                        act_.sem_inc(sem("act_ready"), 1)
                elif stage == "f1_up":
                    cch, g = b
                    for name, dst in (("up", up), ("gate", gt)):
                        copy_free(stage, b, name, dst[:, cch, g * BANK:(g + 1) * BANK], lambda u: u, sem("ug_ready"))
                elif stage == "f1_gate":
                    ch.do(A(primer[:, :], magic[:, :], ACT.Sigmoid))
                    act_.wait_ge(sem("scale_gate"), 1)
                    for k in range(4):
                        if k < 3:
                            ch.do(A(gt[:, k, :], gt[:, k, :], ACT.Identity, bias=magic[:, :], scale=col(q_inv, "gate")), sem("gate_rounded"))
                        if k > 0:
                            act_.wait_ge(sem("gate_whole"), k)
                            ch.do(A(sg[:, k - 1, :], gt[:, k - 1, :], ACT.Sigmoid, scale=col(q_scale, "gate")))
                            ch.sync()
                            ch.do(A(sg[:, k - 1, :], sg[:, k - 1, :], ACT.Identity, bias=magic[:, :], scale=65536.0), sem("sig_rounded"))
                elif stage == "f1_prod":
                    act_.wait_ge(sem("scale_prod"), 1)
                    for k in range(3):
                        ch.do(A(gt[:, k, :], gt[:, k, :], ACT.Identity, bias=magic[:, :], scale=col(q_inv, "prod")), sem("prod_rounded"))
                elif stage == "f1_out":
                    act_.wait_ge(sem("scale_out"), 1)
                    for g in range(4):
                        o = sg[:, :, g * 2 * P:(g + 1) * 2 * P]
                        ch.do(A(o, o, ACT.Identity, bias=magic[:, :], scale=col(q_inv, "out")), sem("out_rounded"))
                elif stage in ("a_stack", "b_stack", "c_stack"):
                    copy_free(stage, b, "qk", qkT[:, b, :, :], lambda u: as16(u).rearrange("p (s q) -> p s q", s=8), sem(stage[0] + "_qkT"))
                elif stage in ("a_again", "b_again", "c_again"):
                    copy_free(stage, b, "q", q2T[:, b, :, :], lambda u: as16(u)[:, 0:4 * P].rearrange("p (s q) -> p s q", s=4), sem(stage[0] + "_q2T"))
                elif stage in ("a_exp", "b_exp", "c_exp"):
                    m = stage[0]
                    n = pt_turn[m, b]
                    if n == 0:
                        act_.wait_ge(sem("wout_split"), 2 * NE)
                    if n >= 2:
                        act_.wait_ge(sem("pt_used"), n - 1)
                    scale = {"a": P ** -0.5, "b": P ** -0.5, "c": DA ** -0.5}[m]
                    for j in range(5):
                        if j < 4:
                            u = banks.get(act_, stage, b, f"t{j}").rearrange("p (h q) -> p h q", h=4)
                            if n >= 1:
                                act_.wait_ge(sem("pl_ready"), 4 * (n - 1) + j + 1)
                            ch.do(A(p32[:, j, :].rearrange("p (h q) -> p h q", h=4), u, ACT.Exp, scale=scale), banks.freed(stage, b, f"t{j}"))
                        if j > 0:
                            act_.wait_ge(*banks.freed(stage, b, f"t{j - 1}"))
                            ch.do(A(groups(ph[:, n % 2, :, :], 4)[:, j - 1], p32[:, j - 1, :].rearrange("p (h q) -> p h q", h=4), ACT.Copy), sem("ph_ready"))
                elif stage in atT:
                    copy_free(stage, b, "t", atT[stage][:, :], lambda u: u[:, 0:P], sem(stage + "_T"))
                elif stage == "f3_up":
                    for k in range(5):
                        u = banks.get(act_, stage, b, f"h{k}")
                        r = P if k < 4 else 64
                        bias = b31[:, k:k + 1] if k < 4 else bs1[:, :]
                        ch.do(A(h3s[b][0:r, k, :], u[0:r, :], ACT.Gelu, bias=bias), banks.freed(stage, b, f"h{k}"))
                        ch.sync()
                        act_.sem_inc(sem("h3_ready"), 1)

        @block.vector
        def _(dve):
            ch = Chain(dve, sem("dve_step"))
            v = nc.vector
            tt, ts, stt = v.tensor_tensor, v.tensor_scalar, v.scalar_tensor_tensor

            def free_of(*key):
                return banks.freed(*key)

            def get(stage, b, name):
                return banks.get(dve, stage, b, name)

            def norm_stats(src, b):
                ch.do(v.bn_stats(stats[:, b, :], src))
                ch.sync()
                ch.do(v.bn_aggr(mv[:, b, :], stats[:, b, :]), sem("stats_ready"))

            def normalise(stage, out, src, b, signal):
                turn = norm_turn[NORM_OF[stage], b]
                dve.wait_ge(sem("stats_ready"), turn)
                dve.wait_ge(sem("rstd_ready"), turn)
                ch.do(ts(out, src, mv[:, b, 0:1], rstd[:, b:b + 1], ALU.subtract, ALU.mult), signal)

            def twice(out, src, n):
                ch.do(v.tensor_copy(out, bc(src.unsqueeze(2), [P, n, 2, src.shape[-1]])))

            def split_q(m, b, src, i, signal=None):
                st = (qs, ks)[i][:, b, :, :]
                src = src.rearrange("p (h d) -> p h d", h=HA)
                lo = 2 if i == 0 else 1
                hi2 = 1 if i == 0 else 2
                twice(st[:, :, 0:4 * DA].rearrange("p h (s d) -> p h s d", d=DA)[:, :, 0:hi2 + 1:hi2, :], src, HA)
                ch.sync()
                ch.do(tt(st[:, :, lo * DA:(lo + 1) * DA], src, st[:, :, 0:DA], ALU.subtract), signal)

            def split_v(b, src, signal):
                src = src.rearrange("p (h d) -> p h d", h=HA)
                ch.do(v.tensor_copy(vA[:, b, :, 0:DA], src))
                ch.sync()
                ch.do(tt(vA[:, b, :, DA + 1:2 * DA + 1], src, vA[:, b, :, 0:DA], ALU.subtract), signal)

            def pick(i, probs, bs, nb):
                ch.sync()
                ch.do(v.tensor_reduce(top[:, bs, 0], probs, AX.X, ALU.max))
                ch.sync()
                ch.do(tt(eq[:, bs, :], probs, bc(top[:, bs, :], [P, nb, NE]), ALU.is_equal))
                ch.sync()
                ch.do(tt(eq[:, bs, :], eq[:, bs, :], rank[:, bs, :], ALU.mult))
                ch.sync()
                ch.do(v.tensor_reduce(top[:, bs, 0], eq[:, bs, :], AX.X, ALU.max))
                ch.sync()
                ch.do(tt(oh[:, i, bs, :], eq[:, bs, :], bc(top[:, bs, :], [P, nb, NE]), ALU.is_equal),
                      sem("oh_ready") if i and nb == NB else None)

            def top2(bs, nb):
                dve.wait_ge(sem("route_consts"), 1)
                pick(0, pr[:, bs, :], bs, nb)
                ch.sync()
                ch.do(ts(p2[:, bs, :], oh[:, 0, bs, :], -3.0e38, None, ALU.mult))
                ch.sync()
                ch.do(tt(p2[:, bs, :], p2[:, bs, :], pr[:, bs, :], ALU.add))
                pick(1, p2[:, bs, :], bs, nb)

            def global_max(stage, cols):
                u = get(stage, 0, "t")
                ch.do(v.tensor_reduce(m1[0:cols, 0:1], u[0:cols, 0:P], AX.X, ALU.max), free_of(stage, 0, "t"))
                ch.sync()
                if cols == 2:
                    ch.do(ts(m1b[0:2, 0:2], ident[0:2, 0:2], m1[0:2, 0:1], None, ALU.mult), sem("m1_ready"))
                else:
                    ch.do(v.tensor_copy(m1b[0:1, 0:1], m1[0:1, 0:1]), sem("m1_ready"))
                return get(stage, 0, "b")[:, 0:cols]

            def scale_of(name, u, n, stage, signal=None):
                s_, un, iv = (col(t_, name, n) for t_ in (q_scale, q_unit, q_inv))
                ch.do(tt(s_, u, un, ALU.mult), free_of(stage, 0, "b"))
                ch.sync()
                ch.do(ts(s_, s_, 1.0 / QMAX, 1e-12, ALU.mult, ALU.max))
                ch.sync()
                ch.do(v.reciprocal(iv, s_))
                ch.sync()
                ch.do(tt(iv, iv, un, ALU.mult), signal)
                ch.sync()

            for stage, b in order:
                if stage == "setup":
                    for st_ in (ast, mst):
                        ch.do(v.memset(st_.rearrange("p h s -> p (h s)").bitcast(F32), 0.0))
                    ch.do(v.memset(q0[:, :, :, 3 * D0:SLOT0], 0.0))
                    ch.do(v.memset(k0[:, :, :, 3 * D0:SLOT0], 0.0))
                    ch.do(v.memset(v0[:, :, :, D0:D0 + 1], 1.0), sem("stack_zeros"))
                    ch.sync()
                    ch.do(v.memset(ast[:, :, 3:6], 1.0))
                    ch.do(v.memset(mst[:, :, 0:3], 1.0))
                    ch.do(v.memset(magic[:, :], MAGIC))
                    ch.do(v.memset(ones[:, :], 1.0), sem("ones_ready"))
                elif stage == "x0_split":
                    if b == 0:
                        ch.do(v.memset(qs[:, :, :, 3 * DA:4 * DA], 0.0))
                        ch.do(v.memset(ks[:, :, :, 3 * DA + 2:4 * DA], 0.0))
                        ch.do(v.memset(ks[:, :, :, 3 * DA:3 * DA + 2], 1.0))
                    qq = q0[:, b % 2, :, :]
                    zb = z[:, b, :].rearrange("p (h d) -> p h d", h=H0)
                    if b >= 2:
                        dve.wait_ge(sem("x0_stacked"), b - 1)
                    twice(qq[:, :, 0:2 * D0].rearrange("p h (s d) -> p h s d", d=D0), zb, H0)
                    ch.sync()
                    ch.do(tt(qq[:, :, 2 * D0:3 * D0], zb, qq[:, :, 0:D0], ALU.subtract), sem("q0_ready"))
                elif stage == "w1":
                    ch.do(v.tensor_reduce(cmean[:, :], cT[:, :, :], AX.X, ALU.add))
                    ch.sync()
                    ch.do(ts(cmean[:, :], cmean[:, :], 1.0 / P, None, ALU.mult))
                    ch.sync()
                    ch.do(v.tensor_copy(cmeanB[:, :, :], bc(cmean[:, :].unsqueeze(2), [P, NB, P])), sem("cmean_ready"))
                elif stage == "w8":
                    if b == 0:
                        loaded(dve, "l1")
                    w = wq8[:, b, :, :].rearrange("p c (n k) -> p (c n) k", k=32)
                    ch.do(v.tensor_reduce(w8s[:, b, :], w, AX.X, ALU.max, apply_absolute_value=True))
                    ch.sync()
                    ch.do(ts(w8s[:, b, :], w8s[:, b, :], 1.0 / QMAX4, 1e-12, ALU.mult, ALU.max))
                    ch.sync()
                    ch.do(v.reciprocal(w8r[:, b, :], w8s[:, b, :]))
                    ch.sync()
                    ch.do(tt(w, w, bc(w8r[:, b, :].unsqueeze(2), [P, 12, 32]), ALU.mult))
                    ch.sync()
                    ch.do(ts(w, w, MAGIC, -MAGIC, ALU.add, ALU.add))
                    ch.sync()
                    ch.do(tt(w, w, bc(w8s[:, b, :].unsqueeze(2), [P, 12, 32]), ALU.mult), sem("w8_ready"))
                elif stage == "x0_norm":
                    if b == 0:
                        loaded(dve, "x")
                    norm_stats(x[:, b, :], b)
                elif stage in ("x1_norm", "x3_norm"):
                    norm_stats(x[:, b, :], b)
                elif stage in Z_STAGES:
                    normalise(stage, z[:, b, :], x[:, b, :], b, sem(stage))
                    if stage == "f1_z":
                        ch.sync()
                        ch.do(v.tensor_reduce(part[:, 0, b:b + 1], z[:, b, :], AX.X, ALU.max, apply_absolute_value=True))
                elif stage == "x0_forget":
                    u = get("x0_gate", 0, "gates")[:, 0:2 * NB * H0].rearrange("p (b g) -> p b g", b=NB)
                    loaded(dve, "x0")
                    ch.do(tt(gi[:, :, :], u[:, :, 0:H0], bc(ifb[:, 0:H0].unsqueeze(1), [P, NB, H0]), ALU.add))
                    ch.do(tt(gf[:, :, :], u[:, :, H0:2 * H0], bc(ifb[:, H0:2 * H0].unsqueeze(1), [P, NB, H0]), ALU.add),
                          free_of("x0_gate", 0, "gates"))
                    ch.sync()
                    ch.do(stt(ga[:, :, :], gf[:, :, :], -1.0, gf[:, :, :], ALU.mult, ALU.max), sem("abs_f"))
                    dve.wait_ge(sem("softplus"), 1)
                    ch.do(stt(gf[:, :, :], gf[:, :, :], 0.0, gb[:, :, :], ALU.min, ALU.subtract), sem("log_forget"))
                    u = get(stage, 0, "csum")[:, 0:NB * H0].rearrange("p (b h) -> p b h", b=NB)
                    ch.do(v.tensor_copy(cs[:, :, :], u))
                    ch.do(tt(ga[:, :, :], gi[:, :, :], u, ALU.subtract), free_of(stage, 0, "csum"))
                    ch.sync()
                    dve.sem_inc(sem("a_ready"), 1)
                    u = get(stage, 0, "at")
                    ch.do(v.tensor_copy(aT[:, :], u[0:NB * H0, 0:P]), free_of(stage, 0, "at"))
                    ch.sync()
                    ch.do(v.tensor_tensor_scan(mT[:, :], aT[:, :], aT[:, :], -3.0e38, ALU.max, ALU.max), sem("mT_ready"))
                    u = get(stage, 0, "m")[:, 0:NB * H0].rearrange("p (b h) -> p b h", b=NB)
                    ch.do(ts(mm[:, :, :], u, -1.0, None, ALU.mult))
                    ch.do(tt(gb[:, :, :], cs[:, :, :], u, ALU.add), free_of(stage, 0, "m"))
                    ch.sync()
                    dve.sem_inc(sem("md_ready"), 1)
                    for src, st, o in ((ga, ast, 0), (mm, mst, 3)):
                        s2 = src[:, :, :].rearrange("p b h -> p (b h)")
                        ch.do(v.tensor_copy(st[:, :, o], s2))
                        ch.sync()
                        ch.do(tt(s2, s2, st[:, :, o], ALU.subtract))
                        ch.sync()
                        ch.do(v.tensor_copy(st[:, :, o + 1], s2))
                        ch.sync()
                        ch.do(tt(st[:, :, o + 2], s2, st[:, :, o + 1], ALU.subtract), sem("am_ready") if o else None)
                elif stage == "x0_score":
                    for j in range(2):
                        dve.wait_ge(sem("dec_ready"), 2 * b + j + 1)
                        u = get(stage, b, f"s{j}").rearrange("p (h q) -> p h q", h=4)
                        ch.do(stt(dec[:, b % 2, j, :, :], u, D0 ** -0.5, dec[:, b % 2, j, :, :], ALU.mult, ALU.mult),
                              free_of(stage, b, f"s{j}"))
                        ch.sync()
                        dve.sem_inc(sem("cc_ready"), 1)
                elif stage == "x0_cut":
                    dve.wait_ge(sem("ch0_ready"), 2 * b + 2)
                    ch.do(tt(groups(cl0[:, b % 2, :, :], 2)[:, 1], dec[:, b % 2, 1, :, :], groups(ch0[:, b % 2, :, :], 2)[:, 1], ALU.subtract),
                          sem("cl0_ready_1"))
                elif stage == "x0_value":
                    u = get(stage, b, "u")[:, 0:H0 * (2 * D0 + 1)].rearrange("p (h d) -> p h d", h=H0)
                    dve.sem_inc(sem("cc_used"), 1)
                    if b == 0:
                        dve.wait_ge(sem("floor_ready"), 1)
                        ch.do(ts(floor[:, :, :], floor[:, :, :], 1e-6, None, ALU.add))
                        ch.sync()
                    ch.do(v.tensor_reduce(nrm[:, :], u[:, :, D0:D0 + 1], AX.X, ALU.max, apply_absolute_value=True))
                    ch.sync()
                    ch.do(stt(nrm[:, :], nrm[:, :], 1e-6, floor[:, b, :], ALU.add, ALU.max))
                    ch.sync()
                    ch.do(v.reciprocal(nrm[:, :], nrm[:, :]))
                    ch.sync()
                    h3d = hh[:, b, :].rearrange("p (h d) -> p h d", h=H0)
                    ch.do(v.tensor_copy(h3d, u[:, :, D0 + 1:2 * D0 + 1]))
                    ch.sync()
                    ch.do(tt(h3d, u[:, :, 0:D0], h3d, ALU.add), free_of(stage, b, "u"))
                    ch.sync()
                    ch.do(tt(h3d, h3d, bc(nrm[:, :].unsqueeze(2), [P, H0, D0]), ALU.mult))
                    ch.sync()
                    ch.do(v.tensor_reduce(hm[:, :], h3d, AX.X, ALU.add))
                    ch.sync()
                    ch.do(stt(h3d, bc(hm[:, :].unsqueeze(2), [P, H0, D0]), -1.0 / D0, h3d, ALU.mult, ALU.add))
                    ch.sync()
                    ch.do(tt(sq[:, :], hh[:, b, :], hh[:, b, :], ALU.mult))
                    ch.sync()
                    ch.do(v.tensor_reduce(hv[:, b, :], sq[:, :].rearrange("p (h d) -> p h d", h=H0), AX.X, ALU.add))
                    ch.sync()
                    ch.do(ts(hv[:, b, :], hv[:, b, :], 1.0 / D0, 1e-5, ALU.mult, ALU.add), sem("hv_ready"))
                elif stage == "x0_group":
                    if b == 0:
                        loaded(dve, "rows")
                        dve.wait_ge(sem("tg_ready"), 1)
                    dve.wait_ge(sem("hr_ready"), b + 1)
                    h3d = hh[:, b, :].rearrange("p (h d) -> p h d", h=H0)
                    ch.do(tt(h3d, h3d, bc(hr[:, b, :].unsqueeze(2), [P, H0, D0]), ALU.mult))
                    ch.sync()
                    ch.do(tt(hh[:, b, :], hh[:, b, :], vec("L0_xattn_gn_w"), ALU.mult))
                    ch.sync()
                    ch.do(tt(hh[:, b, :], hh[:, b, :], vec("L0_xattn_gn_b"), ALU.add))
                    ch.sync()
                    ch.do(stt(x[:, b, :], hh[:, b, :], tg[:, 0:1], x[:, b, :], ALU.mult, ALU.add))
                    ch.sync()
                    norm_stats(x[:, b, :], b)
                elif stage in ("f0_route", "f2_route", "f3_route"):
                    n = {"f0_route": 1, "f2_route": 2, "f3_route": 3}[stage]
                    nb = NB if n == 1 else HALF
                    bs = slice(nb * b, nb * (b + 1))
                    u = get(stage, b, "logit")[:, 0:nb * NE].rearrange("p (b e) -> p b e", b=nb)
                    if n < 3:
                        ch.do(v.tensor_reduce(top[:, bs, 0], u, AX.X, ALU.max))
                        ch.sync()
                        ch.do(tt(lg[:, bs, :], u, bc(top[:, bs, :], [P, nb, NE]), ALU.subtract), free_of(stage, b, "logit"))
                    else:
                        ch.do(v.tensor_copy(lg[:, bs, :], u), free_of(stage, b, "logit"))
                    ch.sync()
                    dve.sem_inc(sem("logit_ready"), 1)
                    dve.wait_ge(sem("route_exp"), route_turn[stage, b] + 1)
                    if n < 3:
                        ch.do(v.tensor_reduce(gsum[:, bs, 0], pr[:, bs, :], AX.X, ALU.add))
                        ch.sync()
                        ch.do(v.reciprocal(gsum[:, bs, :], gsum[:, bs, :]))
                        ch.sync()
                        ch.do(tt(pr[:, bs, :], pr[:, bs, :], bc(gsum[:, bs, :], [P, nb, NE]), ALU.mult))
                    else:
                        loaded(dve, "l3")
                        ch.do(ts(pr[:, bs, :], pr[:, bs, :], 1.0, None, ALU.add))
                        ch.sync()
                        ch.do(v.reciprocal(pr[:, bs, :], pr[:, bs, :]))
                        ch.sync()
                        ch.do(ts(pr[:, bs, :], pr[:, bs, :], rscale[:, 0:1], None, ALU.mult))
                    top2(bs, nb)
                    if n == 1:
                        u = get(stage, 0, "cum")[:, 0:2 * NB * NE].rearrange("p (k b e) -> p k b e", k=2, b=NB)
                        w = get(stage, 0, "total")[:, 0:2 * NB * NE].rearrange("p (k b e) -> p k b e", k=2, b=NB)
                        for k in range(2):
                            ch.do(v.tensor_copy(tot[:, k * NE:(k + 1) * NE, :], w[:, k, :, :].rearrange("p b e -> p e b")),
                                  free_of(stage, 0, "total") if k else None)
                            ch.do(v.tensor_copy(cum[:, k, :, :], u[:, k, :, :]), free_of(stage, 0, "cum") if k else None)
                        ch.sync()
                        dve.wait_ge(*free_of(stage, 0, "total"))
                        ch.do(v.tensor_tensor_scan(inc[:, :, :].rearrange("p e b -> p (e b)"), reset[:, :, :].rearrange("p e b -> p (e b)"),
                                                   tot[:, :, :].rearrange("p e b -> p (e b)"), 0.0, ALU.mult, ALU.add))
                        ch.sync()
                        ch.do(tt(tot[:, :, :], inc[:, :, :], tot[:, :, :], ALU.subtract))
                        ch.sync()
                        ch.do(tt(tot[:, NE:2 * NE, :], tot[:, NE:2 * NE, :], bc(inc[:, 0:NE, NB - 1:NB], [P, NE, NB]), ALU.add))
                        ch.sync()
                        for k in range(2):
                            ch.do(tt(cum[:, k, :, :], cum[:, k, :, :], tot[:, k * NE:(k + 1) * NE, :].rearrange("p e b -> p b e"), ALU.add))
                        ch.sync()
                        ch.do(stt(oh[:, :, :, :].rearrange("p k b e -> p (k b e)"), cum[:, :, :, :].rearrange("p k b e -> p (k b e)"),
                                  CAP + 0.5, oh[:, :, :, :].rearrange("p k b e -> p (k b e)"), ALU.is_lt, ALU.mult))
                    ch.sync()
                    ch.do(tt(gate[:, bs, :], oh[:, 0, bs, :], oh[:, 1, bs, :], ALU.add))
                    ch.sync()
                    ch.do(tt(gate[:, bs, :], gate[:, bs, :], pr[:, bs, :], ALU.mult))
                    ch.sync()
                    ch.do(v.tensor_reduce(gsum[:, bs, 0], gate[:, bs, :], AX.X, ALU.add))
                    ch.sync()
                    if n == 1:
                        ch.do(ts(gsum[:, bs, :], gsum[:, bs, :], 1e-9, None, ALU.max))
                    elif n == 2:
                        ch.do(ts(gsum[:, bs, :], gsum[:, bs, :], 1e-6, None, ALU.add))
                    ch.sync()
                    ch.do(v.reciprocal(gsum[:, bs, :], gsum[:, bs, :]))
                    ch.sync()
                    ch.do(tt(gate[:, bs, :], gate[:, bs, :], bc(gsum[:, bs, :], [P, nb, NE]), ALU.mult), sem("gate_ready"))
                elif stage in ("f0_up", "f2_up"):
                    e, g = b
                    n = up_turn[stage, b]
                    for k in range(2):
                        dve.wait_ge(sem("act_ready"), 2 * n + k + 1)
                        u = get(stage, b, f"g{k}")
                        ch.do(tt(act[:, n % 2, k, :], act[:, n % 2, k, :], u, ALU.mult), free_of(stage, b, f"g{k}"))
                        ch.sync()
                        dve.sem_inc(sem("hid_ready"), 1)
                elif stage in ("f0_down", "f2_down"):
                    e, g = b
                    u = get(stage, b, "u")
                    dve.sem_inc(sem("hid_used"), 1)
                    for j in range(4):
                        bb = 4 * g + j
                        s = gate[:, bb, e:e + 1]
                        ps = u[:, j * D:(j + 1) * D]
                        fr = free_of(stage, b, "u") if j == 3 else None
                        if e == 0:
                            ch.do(ts(acc[:, bb, :], ps, s, None, ALU.mult), fr)
                        else:
                            ch.do(stt(acc[:, bb, :], ps, s, acc[:, bb, :], ALU.mult, ALU.add), fr)
                    ch.sync()
                    if e == NE - 1:
                        k = 4 if stage == "f0_down" else 6
                        ch.do(stt(x[:, 4 * g:4 * g + 4, :], acc[:, 4 * g:4 * g + 4, :], tg[:, k:k + 1], x[:, 4 * g:4 * g + 4, :], ALU.mult, ALU.add))
                        ch.sync()
                elif stage == "x1_out":
                    u = get(stage, b, "u")
                    ch.do(tt(t1[:, b, :], u[:, 0:D], vec("L1_xattn_b"), ALU.add), free_of(stage, b, "u"))
                    ch.sync()
                    ch.do(stt(x[:, b, :], t1[:, b, :], tg[:, 1:2], x[:, b, :], ALU.mult, ALU.add))
                    ch.sync()
                    norm_stats(x[:, b, :], b)
                elif stage == "f1_scale":
                    ch.sync()
                    ch.do(v.tensor_reduce(mx[:, 0:1], part[:, 0, :], AX.X, ALU.max), sem("mx_ready"))
                    ch.do(v.memset(col(q_unit, "x"), 1.0))
                    u = global_max(stage, 1)
                    ch.sync()
                    scale_of("x", u, 1, stage)
                    for g in range(FPS):
                        dve.wait_ge(sem("f1_zT"), 4 * (g + 1))
                        o = xq[:, g * BANK:(g + 1) * BANK]
                        ch.do(ts(o, zT[:, 4 * g:4 * g + 4, :].rearrange("p b q -> p (b q)"), col(q_inv, "x"), MAGIC, ALU.mult, ALU.add))
                        ch.sync()
                        ch.do(ts(o, o, -MAGIC, None, ALU.add), sem("xq_ready"))
                    ch.do(v.tensor_copy(col(q_unit, "up"), col(q_scale, "x")))
                    ch.do(v.tensor_copy(col(q_unit, "gate"), col(q_scale, "x")))
                elif stage == "f1_up":
                    cch, g = b
                    n = 2 * cch + g
                    for i, src in enumerate((up, gt)):
                        dve.wait_ge(sem("ug_ready"), 2 * n + i + 1)
                        ch.do(v.tensor_reduce(part[:, i, n:n + 1], src[:, cch, g * BANK:(g + 1) * BANK], AX.X, ALU.max,
                                              apply_absolute_value=True))
                elif stage == "f1_gate":
                    ch.sync()
                    ch.do(v.tensor_reduce(mx[:, 0:2], part[:, :, 0:6], AX.X, ALU.max), sem("mx_ready"))
                    u = global_max(stage, 2)
                    scale_of("up", u, 2, stage, sem("scale_gate"))
                    ch.do(ts(col(q_unit, "prod"), col(q_scale, "gate"), 1.0 / 65536.0, None, ALU.mult))
                    for k in range(4):
                        if k < 3:
                            dve.wait_ge(sem("gate_rounded"), k + 1)
                            ch.do(ts(gt[:, k, :], gt[:, k, :], -MAGIC, None, ALU.add), sem("gate_whole"))
                        if k > 0:
                            i = k - 1
                            dve.wait_ge(sem("sig_rounded"), k)
                            ch.do(ts(sg[:, i, :], sg[:, i, :], MAGIC + 65535.0, -MAGIC, ALU.min, ALU.add))
                            ch.sync()
                            dve.wait_ge(sem("gate_whole"), k)
                            ch.do(tt(gt[:, i, :], gt[:, i, :], sg[:, i, :], ALU.mult))
                            ch.sync()
                            ch.do(v.tensor_reduce(part[:, 0, i:i + 1], gt[:, i, :], AX.X, ALU.max, apply_absolute_value=True))
                elif stage == "f1_prod":
                    ch.sync()
                    ch.do(v.tensor_reduce(mx[:, 0:1], part[:, 0, 0:3], AX.X, ALU.max), sem("mx_ready"))
                    u = global_max(stage, 1)
                    scale_of("prod", u, 1, stage, sem("scale_prod"))
                    ch.do(tt(col(q_unit, "out"), col(q_scale, "prod"), col(q_scale, "up"), ALU.mult))
                    for k in range(3):
                        dve.wait_ge(sem("up_whole"), k + 1)
                        dve.wait_ge(sem("prod_rounded"), k + 1)
                        ch.do(stt(sg[:, k, :], gt[:, k, :], -MAGIC, up[:, k, :], ALU.add, ALU.mult))
                        ch.sync()
                        ch.do(v.tensor_reduce(part[:, 0, k:k + 1], sg[:, k, :], AX.X, ALU.max, apply_absolute_value=True))
                elif stage == "f1_out":
                    ch.sync()
                    ch.do(v.tensor_reduce(mx[:, 0:1], part[:, 0, 0:3], AX.X, ALU.max), sem("mx_ready"))
                    u = global_max(stage, 1)
                    scale_of("out", u, 1, stage, sem("scale_out"))
                    ch.do(tt(q_last[:, :], col(q_scale, "out"), tg[:, 5:6], ALU.mult))
                    for g in range(4):
                        dve.wait_ge(sem("out_rounded"), g + 1)
                        o = sg[:, :, g * 2 * P:(g + 1) * 2 * P]
                        ch.do(ts(o, o, -MAGIC, None, ALU.add), sem("o_ready"))
                    ch.sync()
                elif stage == "f1_down":
                    u = get(stage, b, "u")
                    ch.do(stt(x[:, b, :], u[:, 0:D], q_last[:, :], x[:, b, :], ALU.mult, ALU.add), free_of(stage, b, "u"))
                    ch.sync()
                    norm_stats(x[:, b, :], b)
                elif stage in ("a_kv", "b_kv", "c_kv"):
                    m = stage[0]
                    if m == "a" and b == 0:
                        dve.wait_ge(sem("vA_ones"), 1)
                    u = get(stage, b, "qkv")
                    f = free_of(stage, b, "qkv")
                    if m == "c":
                        w = q32[:, b % 2, :, :]
                        ch.do(tt(w, u[:, 0:3 * D].rearrange("p (i d) -> p i d", i=3), bqkv[:, :, :], ALU.add), f)
                        ch.sync()
                        q_, k_, v_ = (w[:, i, :] for i in range(3))
                        split_q(m, b, q_, 0)
                        split_q(m, b, k_, 1)
                        split_v(b, v_, sem("c_stacks"))
                    else:
                        q_, k_, v_ = (u[:, i * D:(i + 1) * D] for i in range(3))
                        if m == "a":
                            split_q(m, b, q_, 0)
                        split_q(m, b, k_, 1)
                        split_v(b, v_, f)
                        ch.sync()
                        dve.sem_inc(sem(m + "_stacks"), 1)
                elif stage == "b_q":
                    u = get(stage, b, "q")
                    split_q("b", b, u[:, 0:D], 0, free_of(stage, b, "q"))
                    ch.sync()
                    dve.sem_inc(sem("b_qs"), 1)
                elif stage in ("a_max", "b_max", "c_max"):
                    m = stage[0]
                    for j in range(4):
                        u = get(stage, b, f"s{j}").rearrange("p (h k) -> p h k", h=4)
                        ch.do(v.tensor_reduce(nmax[:, b, :].rearrange("p (i g) -> p g i", g=4)[:, j], u, AX.X, ALU.max, negate=True), free_of(stage, b, f"s{j}"))
                    ch.sync()
                    for j in range(3):
                        dve.wait_ge(*free_of(stage, b, f"s{j}"))
                    ch.do(v.tensor_copy(qs[:, b, :, 3 * DA], nmax[:, b, :]))
                    ch.sync()
                    ch.do(tt(qs[:, b, :, 3 * DA + 1], nmax[:, b, :], qs[:, b, :, 3 * DA], ALU.subtract), sem(m + "_negmax"))
                elif stage in ("a_av", "b_av", "c_av"):
                    m = stage[0]
                    u = get(stage, b, "av")[:, 0:HA * (2 * DA + 1)].rearrange("p (h d) -> p h d", h=HA)
                    dve.sem_inc(sem("pt_used"), 1)
                    o = at[:, b, :].rearrange("p (h d) -> p h d", h=HA)
                    ch.do(v.reciprocal(rden[:, :], u[:, :, DA]))
                    ch.do(v.tensor_copy(o, u[:, :, DA + 1:2 * DA + 1]))
                    ch.sync()
                    ch.do(tt(o, u[:, :, 0:DA], o, ALU.add), free_of(stage, b, "av"))
                    ch.sync()
                    ch.do(tt(o, o, bc(rden[:, :].unsqueeze(2), [P, HA, DA]), ALU.mult))
                    ch.sync()
                    dve.sem_inc(sem(m + "_at"), 1)
                elif stage in ("a_wo", "b_wo"):
                    m = stage[0]
                    u = get(stage, b, "wo")
                    ch.do(tt(t2[:, b, :], u[:, 0:D], vec("L2_xattn_bo1" if m == "a" else "L2_xattn_bo2"), ALU.add), free_of(stage, b, "wo"))
                    ch.sync()
                    if m == "a":
                        ch.do(stt(t2[:, b, :], t2[:, b, :], 0.0, z[:, b, :], ALU.max, ALU.add))
                    else:
                        ch.do(ts(t2[:, b, :], t2[:, b, :], 0.0, 2.0, ALU.max, ALU.mult))
                    ch.sync()
                    norm_stats(t2[:, b, :], b)
                elif stage in ("a_norm", "b_norm"):
                    m = stage[0]
                    normalise(stage, t1[:, b, :], t2[:, b, :], b, None)
                    ch.sync()
                    g_, b_ = ("L2_xattn_g1", "L2_xattn_b1") if m == "a" else ("L2_xattn_g2", "L2_xattn_b2")
                    ch.do(tt(t1[:, b, :], t1[:, b, :], vec(g_), ALU.mult))
                    ch.sync()
                    ch.do(tt(t1[:, b, :], t1[:, b, :], vec(b_), ALU.add), sem(m + "_out"))
                elif stage == "b_f":
                    u = get(stage, b, "f")
                    ch.do(tt(t2[:, b, :], u[:, 0:D], vec("L2_xattn_bf"), ALU.add), free_of(stage, b, "f"))
                    ch.sync()
                    ch.do(stt(t2[:, b, :], t2[:, b, :], 0.0, t1[:, b, :], ALU.max, ALU.add))
                    ch.sync()
                    norm_stats(t2[:, b, :], b)
                elif stage == "b_last":
                    normalise(stage, t1[:, b, :], t2[:, b, :], b, None)
                    ch.sync()
                    ch.do(tt(t1[:, b, :], t1[:, b, :], vec("L2_xattn_g3"), ALU.mult))
                    ch.sync()
                    ch.do(tt(t1[:, b, :], t1[:, b, :], vec("L2_xattn_b3"), ALU.add))
                    ch.sync()
                    ch.do(stt(x[:, b, :], t1[:, b, :], tg[:, 2:3], x[:, b, :], ALU.mult, ALU.add))
                    ch.sync()
                    norm_stats(x[:, b, :], b)
                elif stage == "c_wo":
                    u = get(stage, b, "wo")
                    ch.do(tt(t2[:, b, :], u[:, 0:D], vec("L3_xattn_bo"), ALU.add), free_of(stage, b, "wo"))
                    ch.sync()
                    ch.do(stt(x[:, b, :], t2[:, b, :], tg[:, 3:4], x[:, b, :], ALU.mult, ALU.add))
                    ch.sync()
                    norm_stats(x[:, b, :], b)
                elif stage == "f3_gate":
                    for k in range(4):
                        dve.wait_ge(sem("h3_ready"), 5 * b + k + 1)
                        u = get(stage, b, f"gate{k}")
                        ch.do(tt(h3s[b][:, k, :], h3s[b][:, k, :], u, ALU.mult), free_of(stage, b, f"gate{k}"))
                        ch.sync()
                        dve.sem_inc(sem("h3_gated"), 1)
                elif stage == "f3_down":
                    u = get(stage, b, "o").rearrange("p (j d) -> p j d", j=4)
                    ch.do(tt(t2[:, 4 * b:4 * b + 4, :], u, bc(vec("L3_ffn_bs2").unsqueeze(1), [P, 4, D]), ALU.add), free_of(stage, b, "o"))
                    ch.sync()
                    for j in range(4):
                        bb = 4 * b + j
                        ch.do(stt(x[:, bb, :], t2[:, bb, :], tg[:, 7:8], x[:, bb, :], ALU.mult, ALU.add), sem("x_final"))


_INS = ["x", "ctx_1024", "g_xattn", "g_ffn", "L0_xattn_Wi_w", "L0_xattn_Wi_b", "L0_xattn_Wf_w", "L0_xattn_Wf_b",
        "L0_xattn_gn_w", "L0_xattn_gn_b", "L0_ffn_Wg", "L0_ffn_W_in", "L0_ffn_W_out", "L1_xattn_W", "L1_xattn_b",
        "L1_ffn_w_gate", "L1_ffn_w_up", "L1_ffn_w_down", "L2_xattn_Wk1", "L2_xattn_Wv1", "L2_xattn_Wq1",
        "L2_xattn_Wo1", "L2_xattn_bo1", "L2_xattn_Wk2", "L2_xattn_Wv2", "L2_xattn_Wq2", "L2_xattn_Wo2",
        "L2_xattn_bo2", "L2_xattn_Wf", "L2_xattn_bf", "L2_xattn_g1", "L2_xattn_b1", "L2_xattn_g2", "L2_xattn_b2",
        "L2_xattn_g3", "L2_xattn_b3", "L2_ffn_router_w", "L2_ffn_w13", "L2_ffn_w2", "L3_xattn_Wq", "L3_xattn_bq",
        "L3_xattn_Wk", "L3_xattn_bk", "L3_xattn_Wv", "L3_xattn_bv", "L3_xattn_Wo", "L3_xattn_bo", "L3_ffn_gate_W",
        "L3_ffn_W1", "L3_ffn_b1", "L3_ffn_W2", "L3_ffn_b2", "L3_ffn_Ws1", "L3_ffn_bs1", "L3_ffn_Ws2",
        "L3_ffn_bs2", "L3_ffn_route_scale"]


def kernel(**inputs):
    import numpy as _np
    import concourse.bacc as _bacc
    from concourse import mybir as _mybir
    from concourse.bass_utils import run_bass_kernel_spmd as _run

    nc = _bacc.Bacc("TRN2", target_bir_lowering=False, num_devices=1)
    arrays, tensors = {}, {}
    for name in _INS:
        a = _np.ascontiguousarray(inputs[name])
        if a.ndim == 0:
            a = a.reshape(1)
        arrays[f"in_{name}"] = a
        tensors[name] = nc.dram_tensor(f"in_{name}", a.shape, _mybir.dt.from_np(a.dtype), kind="ExternalInput").ap()
    tensors["out"] = nc.dram_tensor("out", (8, 128, 128), _mybir.dt.float32, kind="ExternalOutput").ap()
    gated_stack(nc, tensors)
    r = _run(nc, [arrays], core_ids=[0])
    return r.results[0]["out"]
```
